# Optimizing a Trainium2 kernel written in Bass

```python
import numpy as np
import jax
import jax.numpy as jnp

def _softmax(x, axis=-1):
    return jax.nn.softmax(x, axis=axis)

def _gelu(x):
    return jax.nn.gelu(x, approximate=True)

def _silu(x):
    return jax.nn.silu(x)

def _sigmoid(x):
    return jax.nn.sigmoid(x)

def _layernorm(x, axis=-1, eps=1e-05):
    m = jnp.mean(x, axis=axis, keepdims=True)
    v = jnp.var(x, axis=axis, keepdims=True)
    return (x - m) / jnp.sqrt(v + eps)

def _scatter_add(tgt, idx, src, axis=0):
    return tgt.at[idx].add(src)

def _segment_sum(src, seg, n):
    return jax.ops.segment_sum(src, seg, n)
kernel_name = 'mk_seq_preln_d2_jaxref_r8_48b223'

def setup_inputs(seed: int=0):
    np.random.seed(seed)
    _w = jnp.asarray

    def _L0_attn_setup():
        import jax, jax.numpy as jnp
        import numpy as np
        VEC_DIM = 128
        NUM_HEADS = 16
        key = jax.random.key(seed)
        k_x, k_q, k_k, k_v, k_u = jax.random.split(key, 5)
        s = 1.0 / np.sqrt(VEC_DIM)
        return {'x': jax.random.normal(k_x, (4, 256, VEC_DIM), dtype=jnp.float32), 'Wq': jax.random.normal(k_q, (VEC_DIM, VEC_DIM), dtype=jnp.float32) * s, 'Wk': jax.random.normal(k_k, (VEC_DIM, VEC_DIM), dtype=jnp.float32) * s, 'Wv': jax.random.normal(k_v, (VEC_DIM, VEC_DIM), dtype=jnp.float32) * s, 'Wu': jax.random.normal(k_u, (VEC_DIM, VEC_DIM), dtype=jnp.float32) * s}
    _L0_attn_in = _L0_attn_setup()

    def _L0_ffn_setup():
        import jax, jax.numpy as jnp
        import numpy as np
        B, S, D = (4, 256, 128)
        N_EXPERTS, EXPERT_SIZE = (16, 32)
        WIDTH = N_EXPERTS * EXPERT_SIZE
        key = jax.random.key(seed)
        k_x, k_w1, k_w2, k_g = jax.random.split(key, 4)
        x = jax.random.normal(k_x, (B, S, D), dtype=jnp.float32)
        w1 = jax.random.normal(k_w1, (D, WIDTH), dtype=jnp.float32) / np.sqrt(D).astype(np.float32)
        b1 = jnp.zeros((WIDTH,), dtype=jnp.float32)
        w2 = jax.random.normal(k_w2, (WIDTH, D), dtype=jnp.float32) / np.sqrt(WIDTH).astype(np.float32)
        b2 = jnp.zeros((D,), dtype=jnp.float32)
        return {'x': x, 'w1': w1, 'b1': b1, 'w2': w2, 'b2': b2}
    _L0_ffn_in = _L0_ffn_setup()

    def _L1_attn_setup():
        import jax, jax.numpy as jnp
        import numpy as np
        import math
        D_MODEL = 128
        NUM_HEADS = 16
        THETA = 10000.0

        def _rope(x, theta):
            n, d_k = (x.shape[-2], x.shape[-1])
            powers = jnp.arange(0, d_k, 2, dtype=jnp.float32) / d_k
            freqs = 1.0 / theta ** powers
            t = jnp.arange(n, dtype=jnp.float32)
            angles = jnp.outer(t, freqs)
            cos = jnp.cos(angles).astype(x.dtype)
            sin = jnp.sin(angles).astype(x.dtype)
            x_even = x[..., 0::2]
            x_odd = x[..., 1::2]
            rot_even = x_even * cos - x_odd * sin
            rot_odd = x_even * sin + x_odd * cos
            return jnp.stack([rot_even, rot_odd], axis=-1).reshape(x.shape)
        key = jax.random.key(seed)
        ks = jax.random.split(key, 5)
        B, N, D = (2, 256, D_MODEL)
        std = math.sqrt(2.0 / (D + D))
        x = jax.random.normal(ks[0], (B, N, D), dtype=jnp.float32)
        wq = jax.random.normal(ks[1], (D, D), dtype=jnp.float32) * std
        wk = jax.random.normal(ks[2], (D, D), dtype=jnp.float32) * std
        wv = jax.random.normal(ks[3], (D, D), dtype=jnp.float32) * std
        wo = jax.random.normal(ks[4], (D, D), dtype=jnp.float32) * std
        return {'x': x, 'wq': wq, 'wk': wk, 'wv': wv, 'wo': wo}
    _L1_attn_in = _L1_attn_setup()

    def _L1_ffn_setup():
        import jax, jax.numpy as jnp
        import numpy as np
        DIM = 128
        DEPTH = 2
        HEADS = 8
        DIM_HEAD = 64
        WINDOW = 64
        INNER = HEADS * DIM_HEAD
        HID = int(DIM * 4 * 2 / 3)
        B, N = (2, 1024)
        QK_SCALE = 8.0

        def shift_token(t):
            t1, t2 = jnp.split(t, 2, axis=-1)
            t2 = jnp.pad(t2, ((0, 0), (1, 0), (0, 0)))[:, :-1]
            return jnp.concatenate([t1, t2], axis=-1)

        def l2norm(t):
            return t / jnp.clip(jnp.linalg.norm(t, axis=-1, keepdims=True), 1e-12)

        def rotate_half(x):
            x1, x2 = jnp.split(x, 2, axis=-1)
            return jnp.concatenate([-x2, x1], axis=-1)

        def rotary_xpos(q, k):
            n = q.shape[-2]
            half_idx = jnp.arange(0, DIM_HEAD, 2, dtype=jnp.float32)
            inv_freq = 1.0 / 10000.0 ** (half_idx / DIM_HEAD)
            t = jnp.arange(n, dtype=jnp.float32)
            freqs = t[:, None] * inv_freq[None, :]
            freqs = jnp.concatenate([freqs, freqs], axis=-1)
            base = (half_idx + 0.4 * DIM_HEAD) / (1.4 * DIM_HEAD)
            power = (t - n // 2) / float(WINDOW // 2)
            scale = base[None, :] ** power[:, None]
            scale = jnp.concatenate([scale, scale], axis=-1)
            cos, sin = (jnp.cos(freqs), jnp.sin(freqs))
            q = q * cos * scale + rotate_half(q) * sin * scale
            k = k * cos / scale + rotate_half(k) * sin / scale
            return (q, k)

        def local_attention(q, k, v):
            b, h, n, d = q.shape
            w = n // WINDOW
            bq = q.reshape(b, h, w, WINDOW, d) * QK_SCALE
            bk = k.reshape(b, h, w, WINDOW, d)
            bv = v.reshape(b, h, w, WINDOW, d)

            def look_around(t):
                p = jnp.pad(t, ((0, 0), (0, 0), (1, 0), (0, 0), (0, 0)))
                return jnp.concatenate([p[:, :, :w], p[:, :, 1:]], axis=3)
            bk, bv = (look_around(bk), look_around(bv))
            bt = jnp.arange(n).reshape(w, WINDOW)
            btp = jnp.pad(bt, ((1, 0), (0, 0)), constant_values=-1)
            btk = jnp.concatenate([btp[:w], btp[1:]], axis=1)
            sim = jnp.einsum('bhwid,bhwjd->bhwij', bq, bk)
            i = bt[:, :, None]
            j = btk[:, None, :]
            mask = (i < j) | (i > j + WINDOW) | (j == -1)
            sim = jnp.where(mask, -jnp.finfo(sim.dtype).max, sim)
            attn = jax.nn.softmax(sim, axis=-1)
            out = jnp.einsum('bhwij,bhwjd->bhwid', attn, bv)
            return out.reshape(b, h, n, d)

        def _layer(x, wqkv, qs, ksc, wo, lg, lb, w1, b1, w2, b2):
            b, n, _ = x.shape
            h = shift_token(x)
            qkv = h @ wqkv
            q, k, v = jnp.split(qkv, 3, axis=-1)
            to_heads = lambda t: t.reshape(b, n, HEADS, DIM_HEAD).transpose(0, 2, 1, 3)
            q, k, v = (to_heads(q), to_heads(k), to_heads(v))
            q = l2norm(q) * qs
            k = l2norm(k) * ksc
            q, k = rotary_xpos(q, k)
            o = local_attention(q, k, v)
            o = o.transpose(0, 2, 1, 3).reshape(b, n, INNER)
            x = x + o @ wo
            h = shift_token(x)
            mu = h.mean(-1, keepdims=True)
            var = h.var(-1, keepdims=True)
            h = (h - mu) / jnp.sqrt(var + 1e-05) * lg + lb
            h = h @ w1 + b1
            a, g = jnp.split(h, 2, axis=-1)
            h = a * jax.nn.gelu(g, approximate=False)
            x = x + h @ w2 + b2
            return x
        key = jax.random.key(seed)
        ks = jax.random.split(key, 6)
        return {'x': jax.random.normal(ks[0], (B, N, DIM), jnp.float32), 'wqkv': jax.random.normal(ks[1], (DEPTH, DIM, 3 * INNER), jnp.float32) * 0.02, 'q_scale': jnp.ones((DEPTH, DIM_HEAD), jnp.float32), 'k_scale': jnp.ones((DEPTH, DIM_HEAD), jnp.float32), 'wo': jax.random.normal(ks[2], (DEPTH, INNER, DIM), jnp.float32) * 0.02, 'ln_g': jnp.ones((DEPTH, DIM), jnp.float32), 'ln_b': jnp.zeros((DEPTH, DIM), jnp.float32), 'w1': jax.random.normal(ks[3], (DEPTH, DIM, 2 * HID), jnp.float32) * 0.02, 'b1': jnp.zeros((DEPTH, 2 * HID), jnp.float32), 'w2': jax.random.normal(ks[4], (DEPTH, HID, DIM), jnp.float32) * 0.02, 'b2': jnp.zeros((DEPTH, DIM), jnp.float32)}
    _L1_ffn_in = _L1_ffn_setup()
    _d = {'L0_attn_x': _L0_attn_in['x'], 'L0_attn_Wq': _L0_attn_in['Wq'], 'L0_attn_Wk': _L0_attn_in['Wk'], 'L0_attn_Wv': _L0_attn_in['Wv'], 'L0_attn_Wu': _L0_attn_in['Wu'], 'L0_ffn_w1': _L0_ffn_in['w1'], 'L0_ffn_b1': _L0_ffn_in['b1'], 'L0_ffn_w2': _L0_ffn_in['w2'], 'L0_ffn_b2': _L0_ffn_in['b2'], 'L1_attn_wq': _L1_attn_in['wq'], 'L1_attn_wk': _L1_attn_in['wk'], 'L1_attn_wv': _L1_attn_in['wv'], 'L1_attn_wo': _L1_attn_in['wo'], 'L1_ffn_wqkv': _L1_ffn_in['wqkv'], 'L1_ffn_q_scale': _L1_ffn_in['q_scale'], 'L1_ffn_k_scale': _L1_ffn_in['k_scale'], 'L1_ffn_wo': _L1_ffn_in['wo'], 'L1_ffn_ln_g': _L1_ffn_in['ln_g'], 'L1_ffn_ln_b': _L1_ffn_in['ln_b'], 'L1_ffn_w1': _L1_ffn_in['w1'], 'L1_ffn_b1': _L1_ffn_in['b1'], 'L1_ffn_w2': _L1_ffn_in['w2'], 'L1_ffn_b2': _L1_ffn_in['b2']}
    _x0 = _d['L0_attn_x']
    _d['L0_attn_x'] = jax.random.normal(jax.random.fold_in(jax.random.key(seed), 1), (32, 256, 128), dtype=_x0.dtype)
    del _x0
    return _d

def reference(L0_attn_x, L0_attn_Wq, L0_attn_Wk, L0_attn_Wv, L0_attn_Wu, L0_ffn_w1, L0_ffn_b1, L0_ffn_w2, L0_ffn_b2, L1_attn_wq, L1_attn_wk, L1_attn_wv, L1_attn_wo, L1_ffn_wqkv, L1_ffn_q_scale, L1_ffn_k_scale, L1_ffn_wo, L1_ffn_ln_g, L1_ffn_ln_b, L1_ffn_w1, L1_ffn_b1, L1_ffn_w2, L1_ffn_b2):

    def _L0_attn_ref(x, Wq, Wk, Wv, Wu):
        import jax, jax.numpy as jnp
        import numpy as np
        VEC_DIM = 128
        NUM_HEADS = 16
        B, S, D = x.shape
        H = NUM_HEADS
        hd = D // H
        q = (x @ Wq.T).reshape(B, S, H, hd).transpose(0, 2, 1, 3)
        k = (x @ Wk.T).reshape(B, S, H, hd).transpose(0, 2, 1, 3)
        v = (x @ Wv.T).reshape(B, S, H, hd).transpose(0, 2, 1, 3)
        scores = jnp.einsum('bhqd,bhkd->bhqk', q, k) / jnp.sqrt(jnp.float32(D))
        attn = jax.nn.softmax(scores, axis=-1)
        out = jnp.einsum('bhqk,bhkd->bhqd', attn, v)
        out = out.transpose(0, 2, 1, 3).reshape(B, S, D)
        return out

    def _L0_ffn_ref(x, w1, b1, w2, b2):
        import jax, jax.numpy as jnp
        import numpy as np
        B, S, D = (4, 256, 128)
        N_EXPERTS, EXPERT_SIZE = (16, 32)
        WIDTH = N_EXPERTS * EXPERT_SIZE
        h = jax.nn.relu(jnp.einsum('bsd,dw->bsw', x, w1) + b1)
        return jnp.einsum('bsw,wd->bsd', h, w2) + b2

    def _L1_attn_ref(x, wq, wk, wv, wo):
        import jax, jax.numpy as jnp
        import numpy as np
        import math
        D_MODEL = 128
        NUM_HEADS = 16
        THETA = 10000.0

        def _rope(x, theta):
            n, d_k = (x.shape[-2], x.shape[-1])
            powers = jnp.arange(0, d_k, 2, dtype=jnp.float32) / d_k
            freqs = 1.0 / theta ** powers
            t = jnp.arange(n, dtype=jnp.float32)
            angles = jnp.outer(t, freqs)
            cos = jnp.cos(angles).astype(x.dtype)
            sin = jnp.sin(angles).astype(x.dtype)
            x_even = x[..., 0::2]
            x_odd = x[..., 1::2]
            rot_even = x_even * cos - x_odd * sin
            rot_odd = x_even * sin + x_odd * cos
            return jnp.stack([rot_even, rot_odd], axis=-1).reshape(x.shape)
        B, N, D = x.shape
        H = NUM_HEADS
        d_k = D // H

        def split_heads(t):
            return t.reshape(B, N, H, d_k).transpose(0, 2, 1, 3)
        Q = split_heads(x @ wq.T)
        K = split_heads(x @ wk.T)
        V = split_heads(x @ wv.T)
        Q = _rope(Q, THETA)
        K = _rope(K, THETA)
        scale = 1.0 / math.sqrt(d_k)
        scores = jnp.einsum('bhqd,bhkd->bhqk', Q, K) * scale
        causal_mask = jnp.triu(jnp.ones((N, N), dtype=bool), k=1)
        scores = jnp.where(causal_mask, -jnp.inf, scores)
        attn = jax.nn.softmax(scores, axis=-1)
        out = jnp.einsum('bhqk,bhkd->bhqd', attn, V)
        out = out.transpose(0, 2, 1, 3).reshape(B, N, D)
        return out @ wo.T

    def _L1_ffn_ref(x, wqkv, q_scale, k_scale, wo, ln_g, ln_b, w1, b1, w2, b2):
        import jax, jax.numpy as jnp
        import numpy as np
        DIM = 128
        DEPTH = 2
        HEADS = 8
        DIM_HEAD = 64
        WINDOW = 64
        INNER = HEADS * DIM_HEAD
        HID = int(DIM * 4 * 2 / 3)
        B, N = (2, 1024)
        QK_SCALE = 8.0

        def shift_token(t):
            t1, t2 = jnp.split(t, 2, axis=-1)
            t2 = jnp.pad(t2, ((0, 0), (1, 0), (0, 0)))[:, :-1]
            return jnp.concatenate([t1, t2], axis=-1)

        def l2norm(t):
            return t / jnp.clip(jnp.linalg.norm(t, axis=-1, keepdims=True), 1e-12)

        def rotate_half(x):
            x1, x2 = jnp.split(x, 2, axis=-1)
            return jnp.concatenate([-x2, x1], axis=-1)

        def rotary_xpos(q, k):
            n = q.shape[-2]
            half_idx = jnp.arange(0, DIM_HEAD, 2, dtype=jnp.float32)
            inv_freq = 1.0 / 10000.0 ** (half_idx / DIM_HEAD)
            t = jnp.arange(n, dtype=jnp.float32)
            freqs = t[:, None] * inv_freq[None, :]
            freqs = jnp.concatenate([freqs, freqs], axis=-1)
            base = (half_idx + 0.4 * DIM_HEAD) / (1.4 * DIM_HEAD)
            power = (t - n // 2) / float(WINDOW // 2)
            scale = base[None, :] ** power[:, None]
            scale = jnp.concatenate([scale, scale], axis=-1)
            cos, sin = (jnp.cos(freqs), jnp.sin(freqs))
            q = q * cos * scale + rotate_half(q) * sin * scale
            k = k * cos / scale + rotate_half(k) * sin / scale
            return (q, k)

        def local_attention(q, k, v):
            b, h, n, d = q.shape
            w = n // WINDOW
            bq = q.reshape(b, h, w, WINDOW, d) * QK_SCALE
            bk = k.reshape(b, h, w, WINDOW, d)
            bv = v.reshape(b, h, w, WINDOW, d)

            def look_around(t):
                p = jnp.pad(t, ((0, 0), (0, 0), (1, 0), (0, 0), (0, 0)))
                return jnp.concatenate([p[:, :, :w], p[:, :, 1:]], axis=3)
            bk, bv = (look_around(bk), look_around(bv))
            bt = jnp.arange(n).reshape(w, WINDOW)
            btp = jnp.pad(bt, ((1, 0), (0, 0)), constant_values=-1)
            btk = jnp.concatenate([btp[:w], btp[1:]], axis=1)
            sim = jnp.einsum('bhwid,bhwjd->bhwij', bq, bk)
            i = bt[:, :, None]
            j = btk[:, None, :]
            mask = (i < j) | (i > j + WINDOW) | (j == -1)
            sim = jnp.where(mask, -jnp.finfo(sim.dtype).max, sim)
            attn = jax.nn.softmax(sim, axis=-1)
            out = jnp.einsum('bhwij,bhwjd->bhwid', attn, bv)
            return out.reshape(b, h, n, d)

        def _layer(x, wqkv, qs, ksc, wo, lg, lb, w1, b1, w2, b2):
            b, n, _ = x.shape
            h = shift_token(x)
            qkv = h @ wqkv
            q, k, v = jnp.split(qkv, 3, axis=-1)
            to_heads = lambda t: t.reshape(b, n, HEADS, DIM_HEAD).transpose(0, 2, 1, 3)
            q, k, v = (to_heads(q), to_heads(k), to_heads(v))
            q = l2norm(q) * qs
            k = l2norm(k) * ksc
            q, k = rotary_xpos(q, k)
            o = local_attention(q, k, v)
            o = o.transpose(0, 2, 1, 3).reshape(b, n, INNER)
            x = x + o @ wo
            h = shift_token(x)
            mu = h.mean(-1, keepdims=True)
            var = h.var(-1, keepdims=True)
            h = (h - mu) / jnp.sqrt(var + 1e-05) * lg + lb
            h = h @ w1 + b1
            a, g = jnp.split(h, 2, axis=-1)
            h = a * jax.nn.gelu(g, approximate=False)
            x = x + h @ w2 + b2
            return x
        for l in range(DEPTH):
            x = _layer(x, wqkv[l], q_scale[l], k_scale[l], wo[l], ln_g[l], ln_b[l], w1[l], b1[l], w2[l], b2[l])
        return x
    x = L0_attn_x
    x = x + _L0_attn_ref(_layernorm(x, axis=-1), L0_attn_Wq, L0_attn_Wk, L0_attn_Wv, L0_attn_Wu)
    x = x + _L0_ffn_ref(_layernorm(x, axis=-1), L0_ffn_w1, L0_ffn_b1, L0_ffn_w2, L0_ffn_b2)
    x = x + _L1_attn_ref(_layernorm(x, axis=-1), L1_attn_wq, L1_attn_wk, L1_attn_wv, L1_attn_wo)
    x = x + _L1_ffn_ref(_layernorm(x, axis=-1), L1_ffn_wqkv, L1_ffn_q_scale, L1_ffn_k_scale, L1_ffn_wo, L1_ffn_ln_g, L1_ffn_ln_b, L1_ffn_w1, L1_ffn_b1, L1_ffn_w2, L1_ffn_b2)
    return x

_drawn_inputs = setup_inputs


def setup_inputs(seed=0):
    import zlib

    import numpy as np

    out = dict(_drawn_inputs(seed))
    spreads = {'L0_ffn_b1': (0.0, 0.1),
     'L0_ffn_b2': (0.0, 0.1),
     'L1_ffn_q_scale': (1.0, 0.6),
     'L1_ffn_k_scale': (1.0, 0.6),
     'L1_ffn_ln_g': (1.0, 0.6),
     'L1_ffn_ln_b': (0.0, 0.8),
     'L1_ffn_b1': (0.0, 0.8),
     'L1_ffn_b2': (0.0, 0.8)}
    factors = {'L1_ffn_w1': 7.524, 'L1_ffn_w2': 7.313}
    for name, (base, spread) in spreads.items():
        noise = np.random.default_rng([zlib.crc32(name.encode()), seed]).standard_normal(out[name].shape)
        drawn = base * np.exp(spread * noise) if base else spread * noise
        out[name] = jnp.asarray(drawn.astype(out[name].dtype))
    for name, factor in factors.items():
        out[name] = (out[name] * factor).astype(out[name].dtype)
    return out
```

```python
import numpy as np
from contextlib import ExitStack

import concourse.bass as bass
from concourse import mybir

BATCH, SEQ, DIM = 32, 256, 128
SLOTS = 2
PASSES = BATCH // SLOTS
P = 128
TT = SEQ // P
H16, HD8 = 16, 8
GROUPS = H16 // 4
FF0 = 512
HEADS, HD, INNER = 8, 64, 512
PAIRS = HEADS // 2
WINDOW = 64
LAYERS = 2
HID = int(DIM * 4 * 2 / 3)
HTILES = [(0, 128), (128, 128), (256, HID - 256)]
EPS = 1e-5
NEG = -1e30
SCALE0 = 1.0 / float(np.sqrt(DIM))
SCALE1 = 1.0 / float(np.sqrt(HD8))


def shape_constants():
    f = np.float32
    tri = np.where(np.arange(P)[None, :] > np.arange(P)[:, None], f(NEG), f(0)).astype(f)
    i1 = P + np.arange(P)[:, None]
    j1 = WINDOW + np.arange(SEQ - WINDOW)[None, :]
    i0, j0 = np.arange(P)[:, None], np.arange(P)[None, :]

    def band(i, j):
        return np.where((i < j) | (i > j + WINDOW), f(NEG), f(0)).astype(f)

    masks = np.concatenate([tri, np.zeros((P, P), f), tri, band(i0, j0), band(i1, j1)], axis=1)
    t = np.arange(SEQ, dtype=f)
    freq1 = (f(1) / f(10000.0) ** (np.arange(0, HD8, 2, dtype=f) / f(HD8))).astype(f)
    ang1 = np.outer(t, freq1).astype(f)
    cos1 = np.repeat(np.cos(ang1), 2, axis=1)
    sin1 = np.stack([-np.sin(ang1), np.sin(ang1)], axis=-1).reshape(SEQ, HD8)
    rope1 = np.concatenate([cos1, sin1], axis=1).astype(f)
    half = np.arange(0, HD, 2, dtype=f)
    freq2 = (f(1) / f(10000.0) ** (half / f(HD))).astype(f)
    ang2 = (t[:, None] * freq2[None, :]).astype(f)
    base = (half + f(0.4 * HD)) / f(1.4 * HD)
    power = (t - SEQ // 2) / f(WINDOW // 2)
    scale = (base[None, :] ** power[:, None]).astype(f)
    cos2, sin2 = np.cos(ang2).astype(f), np.sin(ang2).astype(f)
    qk_scale = f(8.0)

    def table(c, s):
        return np.concatenate([c, c, -s, s], axis=1)

    rope2 = np.concatenate([table(cos2 * scale * qk_scale, sin2 * scale * qk_scale),
                            table(cos2 / scale, sin2 / scale)], axis=1).astype(f)
    return {"c_ident": np.eye(P, dtype=f), "c_masks": masks, "c_rope1": rope1, "c_rope2": rope2}


class Signal:

    def __init__(self, sem):
        self.sem, self.per_pass, self.latest = sem, 0, {}


class Step:

    def __init__(self, kind, where, slot, layer=0, source=None):
        self.kind, self.where, self.slot, self.layer, self.source = kind, where, slot, layer, source
        self.base, self.before = {}, {}


def raises(st):
    k, w = st.kind, st.where
    dense = w in ("attn0", "attn1")
    return {
        "stats": dict(bn_done=2, moments=2, var_eps=1, rstd=1),
        "apply": dict(normed=1, resid=1 if st.source == "z" else 0),
        "turn": dict(G=1, turned=1),
        "qkv": dict(G=2, v_ready=2, hi_ready=2, lo_ready=2, m_clear=1,
                    **(dict(rot_cos=2, rot_sin=2, rot_done=2) if w == "attn1" else {})),
        "turn_q": dict(G=2, q_ready=2),
        "turn_k": dict(G=2, k_ready=2),
        "maxes": dict(S=8 if w == "attn0" else 6, max_done=1, m_hi=1, m_ready=1),
        "softmax": dict(S=8, O=2, PT=8, exp_done=8 if w == "attn1" else 0, o_ready=2),
        "attn_out": dict(G=2, rec_done=2, att_done=2, resid=1 if w == "attn0" else 0, xin_used=1 if w == "attn0" else 0),
        "project1": dict(G=1, resid=1),
        "up0": dict(G=2, up_ready=2),
        "down0": dict(G=1, plus_bias=1, resid=1),
        "shift": dict(G=1, turned=1),
        "qkv2": dict(G=6, raw_ready=4, sq_ready=4, sums=4, v_ready=2, sq_free=4),
        "rope2": dict(ss_ready=1, rn_ready=1, cos_part=4, sin_part=4, rot_sum=4, rope_ready=4),
        "turn_q2": dict(G=2, q_ready=2),
        "turn_k2": dict(G=2, k_ready=2),
        "scores2": dict(S=3, max_done=3, exps=3, rec_done=2, p_ready=2),
        "mix2": dict(S=4, PT=4, O=2, o_ready=2),
        "project2": dict(G=1, resid=1),
        "back": dict(G=1, bn_done=2, moments=2, var_eps=1, rstd=1, normed=1),
        "up2": dict(G=3, gelu_done=3, up_ready=3),
        "down2": dict(G=1, plus_bias=1, resid=1),
        "finish": dict(out_ready=1),
    }[k]


RINGS = {"G": 2, "S": 2, "O": 2, "PT": 2}


def plan():
    steps = []

    def both(kind, where, **kw):
        for s in range(SLOTS):
            steps.append(Step(kind, where, s, **kw))

    def norm(where, source):
        both("stats", where, source=source)
        both("apply", where, source=source)

    def attention(where):
        both("turn", where, source="h")
        for kind in ("qkv", "turn_q", "turn_k", "maxes", "turn_q", "softmax", "attn_out"):
            both(kind, where)

    norm("attn0", "xin")
    attention("attn0")
    norm("ffn0", "x")
    both("turn", "ffn0", source="h")
    both("up0", "ffn0")
    both("down0", "ffn0")
    norm("attn1", "x")
    attention("attn1")
    both("turn", "attn1", source="att")
    both("project1", "attn1")
    norm("local", "z")
    for layer in range(LAYERS):
        both("shift", "local", layer=layer)
        for kind in ("qkv2", "rope2", "turn_q2", "turn_k2", "scores2", "mix2", "project2", "shift", "back"):
            both(kind, "local", layer=layer)
        both("turn", "local", source="gained", layer=layer)
        both("up2", "local", layer=layer)
        both("down2", "local", layer=layer)
    both("finish", "local")
    return steps


def fused_block(nc, x, wqkv0, w1_0, b1_0, w2_0, b2_0, wqkv1, wo1, wqkv2, q_scale, k_scale, wo2,
                ln_g, ln_b, w1_2, b1_2, w2_2, b2_2, c_ident, c_masks, c_rope1, c_rope2, out):
    f32, f32r = mybir.dt.float32, mybir.dt.float32r
    ALU, ACT, AX = mybir.AluOpType, mybir.ActivationFunctionType, mybir.AxisListType

    x_pass = x.rearrange("(n s) (t p) d -> n p s t d", s=SLOTS, p=P)
    out_pass = out.rearrange("(n s) (t p) d -> n p s t d", s=SLOTS, p=P)

    with ExitStack() as ctx:
        def sb(name, shape, dt=f32):
            return ctx.enter_context(nc.sbuf_tensor(name, shape, dt))

        def pb(name, shape):
            return ctx.enter_context(nc.psum_tensor(name, shape, f32))

        def sem(name):
            return ctx.enter_context(nc.semaphore(name))

        ident = sb("ident", [P, P])
        ident_r = sb("ident_r", [P, P], f32r)
        masks = sb("masks", [P, 3 * P + P + SEQ - WINDOW], f32r)
        causal0 = masks[:, 0:P]
        causal1 = masks[:, P:3 * P]
        band0 = masks[:, 3 * P:4 * P]
        band1 = masks[:, 4 * P:4 * P + SEQ - WINDOW]
        wqkv0_sb = sb("wqkv0_sb", [P, 3 * DIM])
        wqkv1_sb = sb("wqkv1_sb", [P, 3 * DIM])
        wo1_sb = sb("wo1_sb", [P, DIM])
        w1_0_sb = sb("w1_0_sb", [P, FF0])
        b1_0_sb = sb("b1_0_sb", [P, FF0 // P])
        w2_0_sb = sb("w2_0_sb", [P, FF0 // P, DIM])
        b2_0_sb = sb("b2_0_sb", [P, DIM])
        wqkv2_sb = sb("wqkv2_sb", [P, LAYERS, 3 * INNER])
        wo2_sb = sb("wo2_sb", [P, LAYERS, INNER // P, DIM])
        w1_2_sb = sb("w1_2_sb", [P, LAYERS, 2 * HID])
        b1_2_sb = sb("b1_2_sb", [P, LAYERS, 2, 3])
        w2_2_sb = sb("w2_2_sb", [P, LAYERS, 3, DIM])
        b2_2_sb = sb("b2_2_sb", [P, LAYERS, DIM])
        lng_sb = sb("lng_sb", [P, LAYERS])
        lnb_sb = sb("lnb_sb", [P, LAYERS])
        rope1_sb = sb("rope1_sb", [P, TT, 2, HD8])
        rope2_sb = sb("rope2_sb", [P, LAYERS, TT, 2, 2, HD])
        minus_half = sb("minus_half", [P, 4 * HEADS])
        eps_tile = sb("eps_tile", [P, TT])

        xin = sb("xin", [P, SLOTS, TT, DIM])
        X = sb("X", [P, SLOTS, TT, DIM])
        Y = sb("Y", [P, SLOTS, TT, DIM])
        h = sb("h", [P, SLOTS, TT, DIM])
        att = h
        biased = h
        hT = sb("hT", [P, SLOTS, SEQ])
        hS = sb("hS", [P, SLOTS, SEQ + 1])
        QB = sb("QB", [P, SLOTS, TT, H16, 32])
        KB = sb("KB", [P, SLOTS, TT, H16, 32])
        qT = sb("qT", [P, SLOTS, GROUPS, SEQ], f32r)
        kT = sb("kT", [P, SLOTS, H16, SEQ], f32r)
        V = sb("V", [P, SLOTS, TT, H16, 16])
        V2 = sb("V2", [P, SLOTS, TT, INNER])
        rawA = sb("rawA", [P, SLOTS, 1024])
        rawB = sb("rawB", [P, SLOTS, 1024])
        qT2 = sb("qT2", [P, SLOTS, PAIRS, SEQ])
        kT2 = sb("kT2", [P, SLOTS, PAIRS, 2, SEQ])
        P0 = sb("P0", [P, SLOTS, HEADS, P])
        P1 = sb("P1", [P, SLOTS, HEADS, SEQ])
        PT = sb("PT", [P, RINGS["PT"], 1024])
        squares = sb("squares", [P, 2, INNER])
        cosine = sb("cosine", [P, 2, INNER])
        sine = sb("sine", [P, 2, INNER])
        gate = sine[:, :, 0:SEQ]
        bn = sb("bn", [P, SLOTS, TT, 6])
        moments = sb("moments", [P, SLOTS, TT, 2])
        veps = sb("veps", [P, SLOTS, TT])
        rstd = sb("rstd", [P, SLOTS, TT])
        negmax = sb("negmax", [P, SLOTS, TT, H16])
        recip = sb("recip", [P, SLOTS, TT, H16])
        expsum = sb("expsum", [P, SLOTS, TT, HEADS])
        ss = sb("ss", [P, SLOTS, TT, 2, HEADS])
        rn = sb("rn", [P, SLOTS, TT, 2, HEADS])
        oT = rawA[:, :, :].rearrange("p s (g q) -> p s g q", g=GROUPS)
        q2 = rawA[:, :, :].rearrange("p s (t n) -> p s t n", t=TT)
        k2 = rawB[:, :, :].rearrange("p s (t n) -> p s t n", t=TT)
        up0T = rawB[:, :, :].rearrange("p s (c q) -> p s c q", c=FF0 // P)
        o2T = rawB[:, :, :].rearrange("p s (c q) -> p s c q", c=PAIRS)
        up2T = rawA[:, :, 0:3 * SEQ].rearrange("p s (c q) -> p s c q", c=3)
        masks_in = rawA[:, 0, 0:4 * P + SEQ - WINDOW]
        scales_in = rawB[:, 0, 0:2 * LAYERS * HD].rearrange("p (m l d) -> p m l d", m=2, l=LAYERS)
        rope2_in = rawB[:, 1, 0:TT * 4 * HD].rearrange("p (t m c d) -> p t m c d", t=TT, m=2, c=2)

        S = [pb(f"score{b}", [P, 1024]) for b in range(2)]
        O = [pb(f"mixed{b}", [P, 512]) for b in range(2)]
        G = [pb(f"dense{b}", [P, 512]) for b in range(2)]

        steps = plan()
        signals = {}
        for st in steps:
            for name, n in raises(st).items():
                if n and name not in RINGS and name not in signals:
                    signals[name] = Signal(sem(name))
        uses = {r: 0 for r in RINGS}
        for st in steps:
            st.before = {n: s.latest.get(st.slot, 0) for n, s in signals.items()}
            for name, n in raises(st).items():
                if name in RINGS:
                    st.base[name] = uses[name]
                    uses[name] += n
                elif n:
                    st.base[name] = signals[name].per_pass
                    signals[name].per_pass += n
                    signals[name].latest[st.slot] = signals[name].per_pass
        full = {r: [sem(f"{r}{b}_full") for b in range(n)] for r, n in RINGS.items()}
        free = {r: [sem(f"{r}{b}_free") for b in range(n)] for r, n in RINGS.items()}
        for r, n in RINGS.items():
            assert uses[r] % n == 0, r
        loaded = sem("loaded")
        N_LOADS = [0]
        x_loaded, stored = sem("x_loaded"), sem("stored")
        setup_pool, setup_act, setup_dve = sem("setup_pool"), sem("setup_act"), sem("setup_dve")
        paced = sem("paced")
        staged = sem("staged")

        def sig(name):
            return signals[name].sem

        def buf(ring, st, k):
            return (st.base[ring] + k) % RINGS[ring]

        def count_in_ring(ring, st, k, i):
            n = RINGS[ring]
            return i * (uses[ring] // n) + (st.base[ring] + k) // n + 1

        def await_free(eng, ring, st, k, i):
            eng.wait_ge(free[ring][buf(ring, st, k)], count_in_ring(ring, st, k, i))

        def await_full(eng, ring, st, k, i):
            eng.wait_ge(full[ring][buf(ring, st, k)], count_in_ring(ring, st, k, i))

        def await_own(eng, name, st, k, i):
            assert st.base[name] + k > 0
            eng.wait_ge(sig(name), i * signals[name].per_pass + st.base[name] + k)

        def await_before(eng, name, st, i):
            if st.before[name]:
                eng.wait_ge(sig(name), i * signals[name].per_pass + st.before[name])

        block = ctx.enter_context(nc.Block())

        @block.sync
        def _(sp):
            def load(dst, src):
                sp.dma_start(dst, src).then_inc(loaded, 16)
                N_LOADS[0] += 1

            sp.sem_inc(stored, 16)
            sp.dma_start(xin[:], x_pass[0]).then_inc(x_loaded, 16)
            load(ident[:], c_ident)
            load(masks_in, c_masks)
            load(wqkv0_sb[:], wqkv0)
            load(w1_0_sb[:], w1_0)
            load(b1_0_sb[:], b1_0)
            load(w2_0_sb[:], w2_0.rearrange("(c p) d -> p c d", p=P))
            load(b2_0_sb[:], b2_0.partition_broadcast(P))
            load(wqkv1_sb[:], wqkv1)
            load(wo1_sb[:], wo1)
            load(rope1_sb[:], c_rope1.rearrange("(t p) (c d) -> p t c d", p=P, c=2))
            load(rope2_in, c_rope2.rearrange("(t p) (m c d) -> p t m c d", p=P, m=2, c=2))
            load(wqkv2_sb[:], wqkv2.rearrange("l k n -> k l n"))
            load(lng_sb[:], ln_g)
            load(lnb_sb[:], ln_b)
            load(b1_2_sb[:], b1_2)
            load(w1_2_sb[:], w1_2.rearrange("l k n -> k l n"))
            for l in range(LAYERS):
                load(scales_in[:, 0, l, :], q_scale[l].partition_broadcast(P))
                load(scales_in[:, 1, l, :], k_scale[l].partition_broadcast(P))
                load(b2_2_sb[:, l, :], b2_2[l].partition_broadcast(P))
                load(wo2_sb[:, l], wo2[l].rearrange("(c p) d -> p c d", p=P))
                for c, (at, n) in enumerate(HTILES):
                    load(w2_2_sb[0:n, l, c, :], w2_2[l, at:at + n, :])
            used = signals["xin_used"].per_pass
            ready = signals["out_ready"].per_pass
            with sp.Fori(0, PASSES - 1) as i:
                sp.wait_ge(sig("xin_used"), i * used + used)
                sp.dma_start(xin[:], x_pass[i + 1]).then_inc(x_loaded, 16)
                sp.wait_ge(sig("out_ready"), i * ready + ready)
                sp.dma_start(out_pass[i], Y[:]).then_inc(stored, 16)
            sp.wait_ge(sig("out_ready"), PASSES * ready)
            sp.dma_start(out_pass[PASSES - 1], Y[:]).then_inc(stored, 16)
            sp.wait_ge(stored, 16 * PASSES + 16)

        ALL_LOADED = 16 * N_LOADS[0]

        @block.gpsimd
        def _(pool):
            nc.gpsimd.memset(minus_half[:], -0.5).then_inc(setup_pool, 1)
            nc.gpsimd.memset(kT[:].bitcast(f32), 0.0).then_inc(setup_pool, 1)
            nc.gpsimd.memset(kT2[:], 0.0).then_inc(setup_pool, 1)
            nc.gpsimd.memset(V[:], 0.0).then_inc(setup_pool, 1)
            nc.gpsimd.memset(QB[:], 0.0).then_inc(setup_pool, 1)
            nc.gpsimd.memset(KB[:], 0.0).then_inc(setup_pool, 1)
            nc.gpsimd.memset(P1[:], 0.0).then_inc(setup_pool, 1)
            nc.gpsimd.memset(hS[:], 0.0).then_inc(setup_pool, 1)
            nc.gpsimd.memset(eps_tile[:], EPS).then_inc(setup_pool, 1)
            pool.wait_ge(setup_pool, 9)
            nc.gpsimd.memset(V[:, :, :, :, HD8:HD8 + 1], 1.0).then_inc(setup_pool, 1)
            nc.gpsimd.memset(KB[:, :, :, :, 24:26], 1.0).then_inc(setup_pool, 1)
            for r, n in RINGS.items():
                for b in range(n):
                    pool.sem_inc(free[r][b], 1)
            pool.sem_inc(sig("sq_free"), 2)
            pool.wait_ge(loaded, ALL_LOADED)

            def roots(st, i):
                pool.wait_ge(setup_pool, 11)
                s = st.slot
                await_own(pool, "moments", st, 2, i)
                nc.gpsimd.tensor_tensor(veps[:, s, :], moments[:, s, :, 1], eps_tile[:], ALU.add)\
                    .then_inc(sig("var_eps"), 1)
                await_own(pool, "var_eps", st, 1, i)
                nc.gpsimd.tensor_tensor(rstd[:, s, :], veps[:, s, :], minus_half[:, 0:TT], ALU.pow)\
                    .then_inc(sig("rstd"), 1)

            with pool.Fori(0, PASSES) as i:
                for st in steps:
                    s, l = st.slot, st.layer
                    if st.kind in ("stats", "back"):
                        roots(st, i)
                    elif st.kind == "qkv" and st.where == "attn1":
                        for t in range(TT):
                            await_own(pool, "rot_cos", st, t + 1, i)
                            await_own(pool, "rot_sin", st, t + 1, i)
                            nc.gpsimd.tensor_tensor(cosine[:, t, 0:2 * DIM], cosine[:, t, 0:2 * DIM],
                                                    sine[:, t, 0:2 * DIM], ALU.add).then_inc(sig("rot_done"), 1)
                    elif st.kind == "softmax" and st.where == "attn1":
                        for u in range(2 * GROUPS):
                            await_own(pool, "exp_done", st, u + 1, i)
                            pool.sem_inc(paced, 1)
                            b = buf("PT", st, u)
                            w = SEQ if u % 2 == 0 else P
                            part = PT[:, b, 0:4 * w].rearrange("p (j q) -> p j q", j=4)[:, :, 0:P]
                            nc.gpsimd.affine_select(out=part, in_=part, compare_op=ALU.is_ge, fill=0.0, base=0,
                                                    pattern=[[0, 4], [1, P]], channel_multiplier=-1)\
                                .then_inc(full["PT"][b], 1)
                    elif st.kind == "down0":
                        await_before(pool, "resid", st, i)
                        await_before(pool, "turned", st, i)
                        nc.gpsimd.tensor_tensor(biased[:, s], X[:, s],
                                                b2_0_sb[:].unsqueeze(1).broadcast_to([P, TT, DIM]), ALU.add)\
                            .then_inc(sig("plus_bias"), 1)
                    elif st.kind == "down2":
                        await_before(pool, "resid", st, i)
                        await_before(pool, "turned", st, i)
                        nc.gpsimd.tensor_tensor(biased[:, s], Y[:, s],
                                                b2_2_sb[:, l].unsqueeze(1).broadcast_to([P, TT, DIM]), ALU.add)\
                            .then_inc(sig("plus_bias"), 1)
                    elif st.kind == "rope2":
                        for u in range(4):
                            t, m = u // 2, u % 2
                            raw = (q2, k2)[m][:, s, t, :].rearrange("p (h d) -> p h d", h=HEADS)
                            tab = rope2_sb[:, l, t, m, 0, :].unsqueeze(1).broadcast_to([P, HEADS, HD])
                            if u == 0:
                                await_before(pool, "raw_ready", st, i)
                            if u >= 2 or st.base["rot_sum"]:
                                await_own(pool, "rot_sum", st, u - 1, i)
                            nc.gpsimd.tensor_tensor(cosine[:, u % 2, :].rearrange("p (h d) -> p h d", h=HEADS),
                                                    raw, tab, ALU.mult).then_inc(sig("cos_part"), 1)
                            if u == 0:
                                await_own(pool, "ss_ready", st, 1, i)
                                nc.gpsimd.tensor_tensor(rn[:, s].rearrange("p t m h -> p (t m h)"),
                                                        ss[:, s].rearrange("p t m h -> p (t m h)"),
                                                        minus_half[:], ALU.pow).then_inc(sig("rn_ready"), 1)
                    elif st.kind == "finish":
                        await_before(pool, "resid", st, i)
                        nc.gpsimd.tensor_tensor(Y[:, s], X[:, s], Y[:, s], ALU.add).then_inc(sig("out_ready"), 1)

        @block.scalar
        def _(act):
            act.wait_ge(loaded, ALL_LOADED)
            nc.scalar.activation(ident_r[:], ident[:], ACT.Copy).then_inc(setup_act, 1)
            nc.scalar.activation(masks[:], masks_in, ACT.Copy).then_inc(setup_act, 1)
            act.wait_ge(setup_pool, 11)

            with act.Fori(0, PASSES) as i:
                for st in steps:
                    s, l = st.slot, st.layer
                    if st.kind == "turn":
                        b = buf("G", st, 0)
                        await_full(act, "G", st, 0, i)
                        if st.source == "gained":
                            nc.scalar.activation(hT[:, s], G[b][:, 0:SEQ], ACT.Identity,
                                                 bias=lnb_sb[:, l:l + 1], scale=lng_sb[:, l:l + 1])\
                                .then_inc(sig("turned"), 1)
                        else:
                            nc.scalar.activation(hT[:, s], G[b][:, 0:SEQ], ACT.Copy).then_inc(sig("turned"), 1)
                        await_own(act, "turned", st, 1, i)
                        act.sem_inc(free["G"][b], 1)
                    elif st.kind == "shift":
                        b = buf("G", st, 0)
                        await_full(act, "G", st, 0, i)
                        nc.scalar.activation(hS[0:64, s, 0:SEQ], G[b][0:64, 0:SEQ], ACT.Copy)
                        nc.scalar.activation(hS[64:128, s, 1:SEQ + 1], G[b][64:128, 0:SEQ], ACT.Copy)\
                            .then_inc(sig("turned"), 1)
                        await_own(act, "turned", st, 1, i)
                        act.sem_inc(free["G"][b], 1)
                    elif st.kind == "qkv":
                        for t in range(TT):
                            b = buf("G", st, t)
                            qb, kb = QB[:, s, t], KB[:, s, t]
                            await_full(act, "G", st, t, i)
                            nc.scalar.activation(V[:, s, t, :, 0:HD8],
                                                 G[b][:, 2 * DIM:3 * DIM].rearrange("p (h d) -> p h d", h=H16),
                                                 ACT.Copy).then_inc(sig("v_ready"), 1)
                            if st.where == "attn0":
                                qk = G[b][:, 0:2 * DIM]
                            else:
                                await_own(act, "rot_done", st, t + 1, i)
                                qk = cosine[:, t, 0:2 * DIM]
                            q = qk[:, 0:DIM].rearrange("p (h d) -> p h d", h=H16)
                            k = qk[:, DIM:2 * DIM].rearrange("p (h d) -> p h d", h=H16)
                            for src, dst, at in ((q, qb, 0), (q, qb, 8), (k, kb, 0), (k, kb, 16)):
                                last = nc.scalar.activation(dst[:, :, at:at + HD8].bitcast(f32r), src, ACT.Copy)
                            last.then_inc(sig("hi_ready"), 1)
                    elif st.kind == "turn_q":
                        for u in range(2):
                            b = buf("G", st, u)
                            await_full(act, "G", st, u, i)
                            nc.scalar.activation(qT[:, s, 2 * u:2 * u + 2, :].rearrange("p g q -> p (g q)"), G[b][:],
                                                 ACT.Copy).then_inc(sig("q_ready"), 1)
                            await_own(act, "q_ready", st, u + 1, i)
                            act.sem_inc(free["G"][b], 1)
                    elif st.kind == "softmax":
                        scale = SCALE0 if st.where == "attn0" else SCALE1
                        for u in range(2 * GROUPS):
                            w = P if st.where == "attn1" and u % 2 else SEQ
                            b, pt = buf("S", st, u), buf("PT", st, u)
                            await_full(act, "S", st, u, i)
                            await_free(act, "PT", st, u, i)
                            done = full["PT"][pt] if st.where == "attn0" else sig("exp_done")
                            nc.scalar.activation(PT[:, pt, 0:4 * w], S[b][:, 0:4 * w], ACT.Exp, scale=scale)\
                                .then_inc(done, 1)
                            if st.where == "attn0":
                                await_full(act, "PT", st, u, i)
                            else:
                                await_own(act, "exp_done", st, u + 1, i)
                            act.sem_inc(free["S"][b], 1)
                    elif st.kind == "up0":
                        for u in range(2):
                            b = buf("G", st, u)
                            await_full(act, "G", st, u, i)
                            for e in range(2):
                                c = 2 * u + e
                                last = nc.scalar.activation(up0T[:, s, c, :], G[b][:, e * SEQ:(e + 1) * SEQ], ACT.Relu,
                                                            bias=b1_0_sb[:, c:c + 1])
                            last.then_inc(sig("up_ready"), 1)
                            await_own(act, "up_ready", st, u + 1, i)
                            act.sem_inc(free["G"][b], 1)
                    elif st.kind == "qkv2":
                        n_sq = n_raw = n_v = 0
                        for t in range(TT):
                            for part in range(3):
                                u = 3 * t + part
                                b = buf("G", st, u)
                                await_full(act, "G", st, u, i)
                                if part < 2:
                                    act.wait_ge(sig("sq_free"), i * signals["sq_free"].per_pass + st.base["sq_free"] + n_sq + 1)
                                    nc.scalar.activation(squares[:, n_sq % 2, :], G[b][:], ACT.Square)\
                                        .then_inc(sig("sq_ready"), 1)
                                    n_sq += 1
                                    nc.scalar.activation((q2, k2)[part][:, s, t, :], G[b][:], ACT.Copy)\
                                        .then_inc(sig("raw_ready"), 1)
                                    n_raw += 1
                                    await_own(act, "raw_ready", st, n_raw, i)
                                else:
                                    nc.scalar.activation(V2[:, s, t, :], G[b][:], ACT.Copy).then_inc(sig("v_ready"), 1)
                                    n_v += 1
                                    await_own(act, "v_ready", st, n_v, i)
                                act.sem_inc(free["G"][b], 1)
                    elif st.kind == "turn_q2":
                        for u in range(2):
                            b = buf("G", st, u)
                            await_full(act, "G", st, u, i)
                            nc.scalar.activation(qT2[:, s, 2 * u:2 * u + 2, :].rearrange("p g q -> p (g q)"), G[b][:],
                                                 ACT.Copy).then_inc(sig("q_ready"), 1)
                            await_own(act, "q_ready", st, u + 1, i)
                            act.sem_inc(free["G"][b], 1)
                    elif st.kind == "scores2":
                        for u in range(3):
                            b = buf("S", st, u)
                            await_own(act, "max_done", st, u + 1, i)
                            for e in range(8 if u == 0 else 4):
                                hd = e if u == 0 else 4 * (u - 1) + e
                                if u == 0:
                                    dst, src = P0[:, s, hd, :], S[b][:, e * P:(e + 1) * P]
                                else:
                                    dst, src = P1[:, s, hd, WINDOW:SEQ], S[b][:, e * SEQ:e * SEQ + SEQ - WINDOW]
                                t = 0 if u == 0 else 1
                                last = nc.scalar.activation(dst, src, ACT.Exp, bias=negmax[:, s, t, hd:hd + 1],
                                                            accum_out=expsum[:, s, t, hd:hd + 1])
                            last.then_inc(sig("exps"), 1)
                            await_own(act, "exps", st, u + 1, i)
                            act.sem_inc(free["S"][b], 1)
                    elif st.kind == "mix2":
                        for u in range(PAIRS):
                            b, pt = buf("S", st, u), buf("PT", st, u)
                            await_full(act, "S", st, u, i)
                            await_free(act, "PT", st, u, i)
                            nc.scalar.activation(PT[:, pt, :].rearrange("p (e n) -> p e n", e=2)[:, :, 0:320],
                                                 S[b][:, :].rearrange("p (e n) -> p e n", e=2)[:, :, 0:320], ACT.Copy)\
                                .then_inc(full["PT"][pt], 1)
                            await_full(act, "PT", st, u, i)
                            act.sem_inc(free["S"][b], 1)
                    elif st.kind == "up2":
                        for c, (at, n) in enumerate(HTILES):
                            b = buf("G", st, c)
                            await_full(act, "G", st, c, i)
                            await_own(act, "up_ready", st, max(c - 1, 0), i)
                            nc.scalar.activation(gate[0:n, c % 2, :], G[b][0:n, SEQ:2 * SEQ], ACT.Gelu,
                                                 bias=b1_2_sb[0:n, l, 1, c:c + 1]).then_inc(sig("gelu_done"), 1)

        @block.vector
        def _(dve):
            dve.wait_ge(loaded, ALL_LOADED)
            dve.wait_ge(setup_pool, 11)
            for b in range(RINGS["O"]):
                nc.vector.memset(O[b][:], 0.0).then_inc(setup_dve, 1)
            for l in range(LAYERS):
                for t in range(TT):
                    for m in range(2):
                        sc = scales_in[:, m, l, :]
                        nc.vector.tensor_tensor(rope2_sb[:, l, t, m, 0, :], rope2_in[:, t, m, 0, :], sc, ALU.mult)
                        nc.vector.tensor_tensor(rope2_sb[:, l, t, m, 1, 0:32], rope2_in[:, t, m, 1, 0:32], sc[:, 32:64], ALU.mult)
                        nc.vector.tensor_tensor(rope2_sb[:, l, t, m, 1, 32:64], rope2_in[:, t, m, 1, 32:64], sc[:, 0:32], ALU.mult)\
                            .then_inc(staged, 1)
            dve.wait_ge(staged, 4 * LAYERS)
            dve.wait_ge(setup_act, 2)

            def stats(st, i, src):
                s = st.slot
                for t in range(TT):
                    nc.vector.bn_stats(bn[:, s, t, :], src(t)).then_inc(sig("bn_done"), 1)
                for t in range(TT):
                    await_own(dve, "bn_done", st, t + 1, i)
                    dve.sem_inc(paced, 1)
                    nc.vector.bn_aggr(moments[:, s, t, :], bn[:, s, t, :]).then_inc(sig("moments"), 1)

            def apply(st, i, src, dst, raised):
                s = st.slot
                for t in range(TT):
                    last = nc.vector.tensor_scalar(dst(t), src(t), moments[:, s, t, 0:1], rstd[:, s, t:t + 1],
                                                   ALU.subtract, ALU.mult)
                last.then_inc(sig(raised), 1)

            with dve.Fori(0, PASSES) as i:
                for st in steps:
                    s, l = st.slot, st.layer
                    rows = xin if st.source == "xin" else X
                    if st.kind == "stats":
                        if st.source == "xin":
                            dve.wait_ge(x_loaded, i * 16 + 16)
                        else:
                            await_before(dve, "resid", st, i)
                        stats(st, i, lambda t: rows[:, s, t, :])
                    elif st.kind == "apply":
                        await_before(dve, "rstd", st, i)
                        if st.source == "z":
                            if s == 0:
                                dve.wait_ge(stored, i * 16 + 16)
                            apply(st, i, lambda t: rows[:, s, t, :], lambda t: Y[:, s, t, :], "resid")
                            nc.vector.memset(bn[:, s, 0, 0:1], 0.0).then_inc(sig("normed"), 1)
                        else:
                            apply(st, i, lambda t: rows[:, s, t, :], lambda t: h[:, s, t, :], "normed")
                    elif st.kind == "qkv":
                        await_full(dve, "G", st, 0, i)
                        nc.vector.memset(QB[:, s, :, :, 24:26], 0.0).then_inc(sig("m_clear"), 1)
                        for t in range(TT):
                            b = buf("G", st, t)
                            if st.where == "attn1":
                                await_full(dve, "G", st, t, i)
                                await_own(dve, "v_ready", st, t + 1, i)
                                if t == 0:
                                    await_own(dve, "lo_ready", st, 0, i)
                                qk = G[b][:, 0:2 * DIM].rearrange("p (h d) -> p h d", d=HD8)
                                cos = rope1_sb[:, t, 0, :].unsqueeze(1).broadcast_to([P, 2 * H16, HD8])
                                nc.vector.tensor_tensor(cosine[:, t, 0:2 * DIM].rearrange("p (h d) -> p h d", d=HD8),
                                                        qk, cos, ALU.mult).then_inc(sig("rot_cos"), 1)
                                sn = sine[:, t, 0:2 * DIM].rearrange("p (h d e) -> p h d e", d=HD8 // 2, e=2)
                                sw = G[b][:, 0:2 * DIM].rearrange("p (h d e) -> p h d e", d=HD8 // 2, e=2)
                                tab = rope1_sb[:, t, 1, :].rearrange("p (d e) -> p d e", e=2)
                                for e in range(2):
                                    last = nc.vector.tensor_tensor(
                                        sn[:, :, :, e], sw[:, :, :, 1 - e],
                                        tab[:, :, e].unsqueeze(1).broadcast_to([P, 2 * H16, HD8 // 2]), ALU.mult)
                                last.then_inc(sig("rot_sin"), 1)
                                await_own(dve, "rot_sin", st, t + 1, i)
                                dve.sem_inc(free["G"][b], 1)
                        for t in range(TT):
                            b = buf("G", st, t)
                            await_own(dve, "hi_ready", st, t + 1, i)
                            qk = G[b][:, 0:2 * DIM] if st.where == "attn0" else cosine[:, t, 0:2 * DIM]
                            q = qk[:, 0:DIM].rearrange("p (h d) -> p h d", h=H16)
                            k = qk[:, DIM:2 * DIM].rearrange("p (h d) -> p h d", h=H16)
                            nc.vector.tensor_tensor(QB[:, s, t, :, 16:24].bitcast(f32r), q, QB[:, s, t, :, 0:8], ALU.subtract)
                            nc.vector.tensor_tensor(KB[:, s, t, :, 8:16].bitcast(f32r), k, KB[:, s, t, :, 0:8], ALU.subtract)\
                                .then_inc(sig("lo_ready"), 1)
                            if st.where == "attn0":
                                await_own(dve, "lo_ready", st, t + 1, i)
                                dve.sem_inc(free["G"][b], 1)
                    elif st.kind == "turn_k":
                        for u in range(2):
                            b = buf("G", st, u)
                            await_full(dve, "G", st, u, i)
                            heads = kT[:, s, 8 * u:8 * u + 8, :].rearrange("p (g j) q -> p j g q", j=4)
                            for j in range(4):
                                r = slice(32 * j, 32 * j + 32)
                                last = nc.vector.tensor_copy(heads[r, j], G[b][r, :].rearrange("p (g q) -> p g q", g=2))
                            last.then_inc(sig("k_ready"), 1)
                            await_own(dve, "k_ready", st, u + 1, i)
                            dve.sem_inc(free["G"][b], 1)
                    elif st.kind == "maxes":
                        tiles = raises(st)["S"]
                        for u in range(tiles):
                            b = buf("S", st, u)
                            await_full(dve, "S", st, u, i)
                            if st.where == "attn0":
                                t, h0, n = u // 4, 4 * (u % 4), 4
                            elif u < 2:
                                t, h0, n = 0, 8 * u, 8
                            else:
                                t, h0, n = 1, 4 * (u - 2), 4
                            nc.vector.reduce_max(negmax[:, s, t, h0:h0 + n], S[b][:, :].rearrange("p (h k) -> p h k", h=n),
                                                 AX.X, negate=True).then_inc(free["S"][b], 1)
                        for u in (tiles - 2, tiles - 1):
                            b = buf("S", st, u)
                            dve.wait_ge(free["S"][b], count_in_ring("S", st, u, i) + 1)
                        neg = negmax[:, s].rearrange("p t h -> p (t h)")
                        slot3 = QB[:, s].rearrange("p t h c -> p (t h) c")
                        nc.vector.tensor_copy(slot3[:, :, 24].bitcast(f32r), neg).then_inc(sig("m_hi"), 1)
                        await_own(dve, "m_hi", st, 1, i)
                        nc.vector.tensor_tensor(slot3[:, :, 25].bitcast(f32r), neg, slot3[:, :, 24], ALU.subtract)\
                            .then_inc(sig("m_ready"), 1)
                        nc.vector.memset(bn[:, s, 0, 0:1], 0.0).then_inc(sig("max_done"), 1)
                    elif st.kind in ("softmax", "mix2"):
                        dst = oT if st.kind == "softmax" else o2T
                        for u in range(2):
                            b = buf("O", st, u)
                            await_full(dve, "O", st, u, i)
                            nc.vector.tensor_copy(dst[:, s, 2 * u:2 * u + 2, :].rearrange("p g q -> p (g q)"), O[b][:])\
                                .then_inc(sig("o_ready"), 1)
                            await_own(dve, "o_ready", st, u + 1, i)
                            dve.sem_inc(free["O"][b], 1)
                    elif st.kind == "attn_out":
                        for t in range(TT):
                            b = buf("G", st, t)
                            await_full(dve, "G", st, t, i)
                            heads = G[b][:, :].rearrange("p (h c) -> p h c", c=32)
                            nc.vector.reciprocal(recip[:, s, t, :], heads[:, :, HD8]).then_inc(sig("rec_done"), 1)
                            await_own(dve, "rec_done", st, t + 1, i)
                            nc.vector.tensor_tensor(att[:, s, t, :].rearrange("p (h d) -> p h d", h=H16), heads[:, :, 0:HD8],
                                                    recip[:, s, t, :].unsqueeze(2).broadcast_to([P, H16, HD8]), ALU.mult)\
                                .then_inc(sig("att_done"), 1)
                            await_own(dve, "att_done", st, t + 1, i)
                            dve.sem_inc(free["G"][b], 1)
                        if st.where == "attn0":
                            nc.vector.tensor_tensor(X[:, s], xin[:, s], att[:, s], ALU.add).then_inc(sig("resid"), 1)
                            await_own(dve, "resid", st, 1, i)
                            dve.sem_inc(sig("xin_used"), 1)
                    elif st.kind in ("project1", "project2", "down0", "down2"):
                        b = buf("G", st, 0)
                        dst = X if st.kind in ("project1", "down0") else Y
                        old = dst
                        if st.kind in ("down0", "down2"):
                            await_own(dve, "plus_bias", st, 1, i)
                            old = biased
                        await_full(dve, "G", st, 0, i)
                        nc.vector.tensor_tensor(dst[:, s], G[b][:, 0:SEQ].rearrange("p (t d) -> p t d", t=TT),
                                                old[:, s], ALU.add).then_inc(sig("resid"), 1)
                        await_own(dve, "resid", st, 1, i)
                        dve.sem_inc(free["G"][b], 1)
                    elif st.kind == "qkv2":
                        for n in range(4):
                            t, m = n // 2, n % 2
                            await_own(dve, "sq_ready", st, n + 1, i)
                            nc.vector.reduce_sum(ss[:, s, t, m, :], squares[:, n % 2, :].rearrange("p (h d) -> p h d", h=HEADS),
                                                 AX.X).then_inc(sig("sums"), 1)
                            await_own(dve, "sums", st, n + 1, i)
                            dve.sem_inc(sig("sq_free"), 1)
                    elif st.kind == "rope2":
                        flat = ss[:, s].rearrange("p t m h -> p (t m h)")
                        nc.vector.tensor_scalar(flat, flat, 1e-24, None, ALU.max).then_inc(sig("ss_ready"), 1)
                        await_before(dve, "raw_ready", st, i)
                        for u in range(4):
                            t, m = u // 2, u % 2
                            raw = (q2, k2)[m][:, s, t, :].rearrange("p (h d) -> p h d", h=HEADS)
                            tab = rope2_sb[:, l, t, m, 1, :]
                            sn = sine[:, u % 2, :].rearrange("p (h d) -> p h d", h=HEADS)
                            nc.vector.tensor_tensor(sn[:, :, 0:32], raw[:, :, 32:64],
                                                    tab[:, 0:32].unsqueeze(1).broadcast_to([P, HEADS, 32]), ALU.mult)
                            nc.vector.tensor_tensor(sn[:, :, 32:64], raw[:, :, 0:32],
                                                    tab[:, 32:64].unsqueeze(1).broadcast_to([P, HEADS, 32]), ALU.mult)\
                                .then_inc(sig("sin_part"), 1)
                            await_own(dve, "sin_part", st, u + 1, i)
                            await_own(dve, "cos_part", st, u + 1, i)
                            nc.vector.tensor_tensor(sine[:, u % 2, :], sine[:, u % 2, :], cosine[:, u % 2, :], ALU.add)\
                                .then_inc(sig("rot_sum"), 1)
                            await_own(dve, "rot_sum", st, u + 1, i)
                            if u == 0:
                                await_own(dve, "rn_ready", st, 1, i)
                            nc.vector.tensor_tensor(raw, sn, rn[:, s, t, m, :].unsqueeze(2).broadcast_to([P, HEADS, HD]),
                                                    ALU.mult).then_inc(sig("rope_ready"), 1)
                    elif st.kind == "turn_k2":
                        for u in range(2):
                            b = buf("G", st, u)
                            await_full(dve, "G", st, u, i)
                            for e in range(2):
                                r = slice(64 * e, 64 * e + 64)
                                last = nc.vector.tensor_copy(kT2[r, s, 2 * u:2 * u + 2, e, :],
                                                             G[b][r, :].rearrange("p (g q) -> p g q", g=2))
                            last.then_inc(sig("k_ready"), 1)
                            await_own(dve, "k_ready", st, u + 1, i)
                            dve.sem_inc(free["G"][b], 1)
                    elif st.kind == "scores2":
                        for u in range(3):
                            b = buf("S", st, u)
                            await_full(dve, "S", st, u, i)
                            if u == 0:
                                dst, src = negmax[:, s, 0, 0:8], S[b][:, :].rearrange("p (h k) -> p h k", h=8)
                            else:
                                dst = negmax[:, s, 1, 4 * (u - 1):4 * u]
                                src = S[b][:, :].rearrange("p (h k) -> p h k", h=4)[:, :, 0:SEQ - WINDOW]
                            nc.vector.reduce_max(dst, src, AX.X, negate=True).then_inc(sig("max_done"), 1)
                        for t in range(TT):
                            await_own(dve, "exps", st, 1 if t == 0 else 3, i)
                            nc.vector.reciprocal(recip[:, s, t, 0:HEADS], expsum[:, s, t, :]).then_inc(sig("rec_done"), 1)
                            await_own(dve, "rec_done", st, t + 1, i)
                            part = P0[:, s] if t == 0 else P1[:, s, :, WINDOW:SEQ]
                            n = P if t == 0 else SEQ - WINDOW
                            nc.vector.tensor_tensor(part, part, recip[:, s, t, 0:HEADS].unsqueeze(2).broadcast_to([P, HEADS, n]),
                                                    ALU.mult).then_inc(sig("p_ready"), 1)
                    elif st.kind == "back":
                        b = buf("G", st, 0)
                        await_full(dve, "G", st, 0, i)
                        stats(st, i, lambda t: G[b][:, t * P:(t + 1) * P])
                        await_own(dve, "rstd", st, 1, i)
                        apply(st, i, lambda t: G[b][:, t * P:(t + 1) * P], lambda t: h[:, s, t, :], "normed")
                        await_own(dve, "normed", st, 1, i)
                        dve.sem_inc(free["G"][b], 1)
                    elif st.kind == "up2":
                        for c, (at, n) in enumerate(HTILES):
                            b = buf("G", st, c)
                            await_own(dve, "gelu_done", st, c + 1, i)
                            nc.vector.scalar_tensor_tensor(up2T[0:n, s, c, :], G[b][0:n, 0:SEQ], b1_2_sb[0:n, l, 0, c:c + 1],
                                                           gate[0:n, c % 2, :], ALU.add, ALU.mult).then_inc(sig("up_ready"), 1)
                            await_own(dve, "up_ready", st, c + 1, i)
                            dve.sem_inc(free["G"][b], 1)

        @block.tensor
        def _(pe):
            pe.wait_ge(loaded, ALL_LOADED)
            pe.wait_ge(setup_pool, 11)
            pe.wait_ge(setup_act, 2)
            pe.wait_ge(setup_dve, RINGS["O"])
            mm = nc.tensor.matmul

            def turn_rows(st, i, k, src):
                b = buf("G", st, k)
                await_free(pe, "G", st, k, i)
                for t in range(TT):
                    last = nc.tensor.transpose(G[b][:, t * P:(t + 1) * P], src(t), ident[:])
                last.then_inc(full["G"][b], 1)

            with pe.Fori(0, PASSES) as i:
                for st in steps:
                    s, l = st.slot, st.layer
                    if st.kind == "turn":
                        if st.source == "att":
                            await_before(pe, "att_done", st, i)
                            turn_rows(st, i, 0, lambda t: att[:, s, t, :])
                        else:
                            await_before(pe, "normed", st, i)
                            turn_rows(st, i, 0, lambda t: h[:, s, t, :])
                    elif st.kind == "shift":
                        await_before(pe, "resid", st, i)
                        turn_rows(st, i, 0, lambda t: Y[:, s, t, :])
                    elif st.kind == "back":
                        await_before(pe, "turned", st, i)
                        turn_rows(st, i, 0, lambda t: hS[:, s, t * P:(t + 1) * P])
                    elif st.kind == "qkv":
                        w = wqkv0_sb if st.where == "attn0" else wqkv1_sb
                        await_before(pe, "turned", st, i)
                        for t in range(TT):
                            b = buf("G", st, t)
                            await_free(pe, "G", st, t, i)
                            mm(G[b][:, 0:3 * DIM], hT[:, s, t * P:(t + 1) * P], w[:], start=True, stop=True)\
                                .then_inc(full["G"][b], 1)
                    elif st.kind in ("turn_q", "turn_k"):
                        src = QB if st.kind == "turn_q" else KB
                        await_before(pe, "lo_ready", st, i)
                        if st.kind == "turn_q":
                            await_before(pe, "m_clear", st, i)
                            await_before(pe, "m_ready", st, i)
                        for u in range(2):
                            b = buf("G", st, u)
                            await_free(pe, "G", st, u, i)
                            for e in range(2):
                                g = 2 * u + e
                                for t in range(TT):
                                    last = nc.tensor.transpose(G[b][:, e * SEQ + t * P:e * SEQ + (t + 1) * P],
                                                               src[:, s, t, 4 * g:4 * g + 4, :].rearrange("p h c -> p (h c)"),
                                                               ident[:])
                            last.then_inc(full["G"][b], 1)
                    elif st.kind == "maxes":
                        await_before(pe, "q_ready", st, i)
                        await_before(pe, "k_ready", st, i)
                        for u in range(raises(st)["S"]):
                            b = buf("S", st, u)
                            await_free(pe, "S", st, u, i)
                            for e in range(2):
                                bank = S[b][:, e * 512:(e + 1) * 512]
                                if st.where == "attn0":
                                    t, g = u // 4, u % 4
                                    last = mm(bank, qT[:, s, g, t * P:(t + 1) * P], kT[:, s, 4 * g + 2 * e:4 * g + 2 * e + 2, :],
                                              start=True, stop=True)
                                elif u < 2:
                                    g = 2 * u + e
                                    mm(bank, ident_r[:], causal0.unsqueeze(1).broadcast_to([P, 4, P]), start=True, stop=False)
                                    last = mm(bank, qT[:, s, g, 0:P], kT[:, s, 4 * g:4 * g + 4, 0:P], start=False, stop=True)
                                else:
                                    g = u - 2
                                    mm(bank, ident_r[:], causal1.unsqueeze(1).broadcast_to([P, 2, SEQ]), start=True, stop=False)
                                    last = mm(bank, qT[:, s, g, P:SEQ], kT[:, s, 4 * g + 2 * e:4 * g + 2 * e + 2, :],
                                              start=False, stop=True)
                            last.then_inc(full["S"][b], 1)
                    elif st.kind == "softmax":
                        await_before(pe, "q_ready", st, i)
                        await_before(pe, "v_ready", st, i)
                        tiles = 2 * GROUPS
                        for u in range(tiles + 2):
                            if u < tiles:
                                g, t = u // 2, u % 2
                                q0 = P if st.where == "attn1" and t == 1 else 0
                                w = SEQ - q0
                                b = buf("S", st, u)
                                await_free(pe, "S", st, u, i)
                                for j in range(4):
                                    last = mm(S[b][:, j * w:(j + 1) * w], kT[:, s, 4 * g + j, t * P:(t + 1) * P],
                                              qT[:, s, g, q0:SEQ], start=True, stop=True)
                                last.then_inc(full["S"][b], 1)
                            if u >= 2:
                                v = u - 2
                                g, t = v // 2, v % 2
                                q0 = P if st.where == "attn1" and t == 1 else 0
                                w = SEQ - q0
                                pt, o = buf("PT", st, v), buf("O", st, g // 2)
                                if v % 4 == 0:
                                    await_free(pe, "O", st, g // 2, i)
                                await_full(pe, "PT", st, v, i)
                                for j in range(4):
                                    at = (g % 2) * SEQ
                                    last = mm(O[o][32 * j:32 * j + 16, at + q0:at + SEQ], V[:, s, t, 4 * g + j, :],
                                              PT[:, pt, j * w:(j + 1) * w], start=t == 0, stop=t == 1)
                                last.then_inc(free["PT"][pt], 1)
                                if v % 4 == 3:
                                    await_free_next = count_in_ring("PT", st, v, i) + 1
                                    pe.wait_ge(free["PT"][pt], await_free_next)
                                    pe.sem_inc(full["O"][o], 1)
                    elif st.kind == "attn_out":
                        for t in range(TT):
                            b = buf("G", st, t)
                            await_before(pe, "o_ready", st, i)
                            await_free(pe, "G", st, t, i)
                            for g in range(GROUPS):
                                last = nc.tensor.transpose(G[b][:, g * P:(g + 1) * P], oT[:, s, g, t * P:(t + 1) * P], ident[:])
                            last.then_inc(full["G"][b], 1)
                    elif st.kind == "project1":
                        b = buf("G", st, 0)
                        await_before(pe, "turned", st, i)
                        await_free(pe, "G", st, 0, i)
                        for t in range(TT):
                            last = mm(G[b][:, t * P:(t + 1) * P], hT[:, s, t * P:(t + 1) * P], wo1_sb[:], start=True, stop=True)
                        last.then_inc(full["G"][b], 1)
                    elif st.kind == "up0":
                        await_before(pe, "turned", st, i)
                        for u in range(2):
                            b = buf("G", st, u)
                            await_free(pe, "G", st, u, i)
                            for e in range(2):
                                c = 2 * u + e
                                last = mm(G[b][:, e * SEQ:(e + 1) * SEQ], w1_0_sb[:, c * P:(c + 1) * P], hT[:, s, :],
                                          start=True, stop=True)
                            last.then_inc(full["G"][b], 1)
                    elif st.kind == "down0":
                        b = buf("G", st, 0)
                        await_before(pe, "up_ready", st, i)
                        await_free(pe, "G", st, 0, i)
                        for t in range(TT):
                            for c in range(FF0 // P):
                                last = mm(G[b][:, t * P:(t + 1) * P], up0T[:, s, c, t * P:(t + 1) * P], w2_0_sb[:, c, :],
                                          start=c == 0, stop=c == FF0 // P - 1)
                        last.then_inc(full["G"][b], 1)
                    elif st.kind == "qkv2":
                        await_before(pe, "turned", st, i)
                        for t in range(TT):
                            for part in range(3):
                                u = 3 * t + part
                                b = buf("G", st, u)
                                await_free(pe, "G", st, u, i)
                                mm(G[b][:], hS[:, s, t * P:(t + 1) * P], wqkv2_sb[:, l, part * INNER:(part + 1) * INNER],
                                   start=True, stop=True).then_inc(full["G"][b], 1)
                    elif st.kind in ("turn_q2", "turn_k2"):
                        src = q2 if st.kind == "turn_q2" else k2
                        await_before(pe, "rope_ready", st, i)
                        for u in range(2):
                            b = buf("G", st, u)
                            await_free(pe, "G", st, u, i)
                            for e in range(2):
                                pr = 2 * u + e
                                for t in range(TT):
                                    last = nc.tensor.transpose(G[b][:, e * SEQ + t * P:e * SEQ + (t + 1) * P],
                                                               src[:, s, t, pr * P:(pr + 1) * P], ident[:])
                            last.then_inc(full["G"][b], 1)
                    elif st.kind == "scores2":
                        await_before(pe, "q_ready", st, i)
                        await_before(pe, "k_ready", st, i)
                        for u in range(3):
                            b = buf("S", st, u)
                            await_free(pe, "S", st, u, i)
                            for e in range(2):
                                bank = S[b][:, e * 512:(e + 1) * 512]
                                if u == 0:
                                    mm(bank, ident_r[:], band0.unsqueeze(1).broadcast_to([P, 4, P]), start=True, stop=False)
                                    for pr in (2 * e, 2 * e + 1):
                                        last = mm(bank[:, (pr - 2 * e) * SEQ:(pr - 2 * e + 1) * SEQ], qT2[:, s, pr, 0:P],
                                                  kT2[:, s, pr, :, 0:P], start=False, stop=pr == 2 * e + 1)
                                else:
                                    pr = 2 * (u - 1) + e
                                    two = bank.rearrange("p (a k) -> p a k", a=2)[:, :, 0:SEQ - WINDOW]
                                    mm(two, ident_r[:], band1.unsqueeze(1).broadcast_to([P, 2, SEQ - WINDOW]),
                                       start=True, stop=False)
                                    last = mm(two, qT2[:, s, pr, P:SEQ], kT2[:, s, pr, :, WINDOW:SEQ], start=False, stop=True)
                            last.then_inc(full["S"][b], 1)
                    elif st.kind == "mix2":
                        await_before(pe, "p_ready", st, i)
                        await_before(pe, "v_ready", st, i)
                        for u in range(PAIRS + 1):
                            if u < PAIRS:
                                b = buf("S", st, u)
                                await_free(pe, "S", st, u, i)
                                for e in range(2):
                                    hd, at = 2 * u + e, 512 * e
                                    nc.tensor.transpose(S[b][:, at:at + P], P0[:, s, hd, :], ident[:])
                                    nc.tensor.transpose(S[b][:, at + P:at + P + WINDOW], P1[0:WINDOW, s, hd, 0:P],
                                                        ident[0:WINDOW, 0:WINDOW])
                                    last = nc.tensor.transpose(S[b][:, at + P + WINDOW:at + 2 * P + WINDOW],
                                                               P1[:, s, hd, P:SEQ], ident[:])
                                last.then_inc(full["S"][b], 1)
                            if u >= 1:
                                v = u - 1
                                pt, o = buf("PT", st, v), buf("O", st, v // 2)
                                if v % 2 == 0:
                                    await_free(pe, "O", st, v // 2, i)
                                await_full(pe, "PT", st, v, i)
                                at = (v % 2) * SEQ
                                for q0, n, t, c0, first, last_one in ((0, P + WINDOW, 0, 0, True, False),
                                                                      (P, WINDOW, 1, P + WINDOW, False, True),
                                                                      (P + WINDOW, WINDOW, 1, P + 2 * WINDOW, True, True)):
                                    for e in range(2):
                                        hd = 2 * v + e
                                        last = mm(O[o][64 * e:64 * e + 64, at + q0:at + q0 + n],
                                                  V2[:, s, t, hd * HD:(hd + 1) * HD],
                                                  PT[:, pt, 512 * e + c0:512 * e + c0 + n], start=first, stop=last_one)
                                last.then_inc(free["PT"][pt], 1)
                                if v % 2 == 1:
                                    pe.wait_ge(free["PT"][pt], count_in_ring("PT", st, v, i) + 1)
                                    pe.sem_inc(full["O"][o], 1)
                    elif st.kind == "project2":
                        b = buf("G", st, 0)
                        await_before(pe, "o_ready", st, i)
                        await_free(pe, "G", st, 0, i)
                        for t in range(TT):
                            for c in range(PAIRS):
                                last = mm(G[b][:, t * P:(t + 1) * P], o2T[:, s, c, t * P:(t + 1) * P], wo2_sb[:, l, c, :],
                                          start=c == 0, stop=c == PAIRS - 1)
                        last.then_inc(full["G"][b], 1)
                    elif st.kind == "up2":
                        await_before(pe, "turned", st, i)
                        for c, (at, n) in enumerate(HTILES):
                            b = buf("G", st, c)
                            await_free(pe, "G", st, c, i)
                            for half in range(2):
                                last = mm(G[b][0:n, half * SEQ:(half + 1) * SEQ],
                                          w1_2_sb[:, l, half * HID + at:half * HID + at + n], hT[:, s, :], start=True, stop=True)
                            last.then_inc(full["G"][b], 1)
                    elif st.kind == "down2":
                        b = buf("G", st, 0)
                        await_before(pe, "up_ready", st, i)
                        await_free(pe, "G", st, 0, i)
                        for t in range(TT):
                            for c, (at, n) in enumerate(HTILES):
                                last = mm(G[b][:, t * P:(t + 1) * P], up2T[0:n, s, c, t * P:(t + 1) * P], w2_2_sb[0:n, l, c, :],
                                          start=c == 0, stop=c == 2)
                        last.then_inc(full["G"][b], 1)


def tiles_on_columns(b):
    out = np.zeros((P, LAYERS, 2, len(HTILES)), b.dtype)
    for c, (at, n) in enumerate(HTILES):
        out[0:n, :, :, c] = b.reshape(LAYERS, 2, HID)[:, :, at:at + n].transpose(2, 0, 1)
    return out


def kernel(**inputs):
    import concourse.bacc as bacc
    from concourse.bass_utils import run_bass_kernel_spmd

    a = {k: np.asarray(v) for k, v in inputs.items()}
    arrays = {
        "x": a["L0_attn_x"],
        "wqkv0": np.concatenate([a["L0_attn_Wq"].T, a["L0_attn_Wk"].T, a["L0_attn_Wv"].T], axis=1),
        "w1_0": a["L0_ffn_w1"], "b1_0": a["L0_ffn_b1"].reshape(FF0 // P, P).T, "w2_0": a["L0_ffn_w2"], "b2_0": a["L0_ffn_b2"],
        "wqkv1": np.concatenate([a["L1_attn_wq"].T, a["L1_attn_wk"].T, a["L1_attn_wv"].T], axis=1),
        "wo1": a["L1_attn_wo"].T,
        "wqkv2": a["L1_ffn_wqkv"], "q_scale": a["L1_ffn_q_scale"], "k_scale": a["L1_ffn_k_scale"], "wo2": a["L1_ffn_wo"],
        "ln_g": a["L1_ffn_ln_g"].T, "ln_b": a["L1_ffn_ln_b"].T, "w1_2": a["L1_ffn_w1"], "b1_2": tiles_on_columns(a["L1_ffn_b1"]),
        "w2_2": a["L1_ffn_w2"], "b2_2": a["L1_ffn_b2"],
    }
    arrays.update(shape_constants())
    arrays = {k: np.ascontiguousarray(v) for k, v in arrays.items()}
    nc = bacc.Bacc("TRN2", target_bir_lowering=False, num_devices=1)
    args = [nc.dram_tensor(k, v.shape, mybir.dt.from_np(v.dtype), kind="ExternalInput").ap() for k, v in arrays.items()]
    args.append(nc.dram_tensor("out", (BATCH, SEQ, DIM), mybir.dt.float32, kind="ExternalOutput").ap())
    fused_block(nc, *args)
    r = run_bass_kernel_spmd(nc, [arrays], core_ids=[0])
    return r.results[0]["out"]
```

```python
import numpy as np
from contextlib import ExitStack

import concourse.bass as bass
from concourse import mybir

BATCH, SEQ, DIM = 32, 256, 128
STREAMS = 4
P = 128
TT = SEQ // P
H16, HD8 = 16, 8
GROUPS = H16 // 4
FF0 = 512
HEADS, HD, INNER = 8, 64, 512
PAIRS = HEADS // 2
WINDOW = 64
LAYERS = 2
HID = int(DIM * 4 * 2 / 3)
HTILES = [(0, 128), (128, 128), (256, HID - 256)]
EPS = 1e-5
NEG = -1e30
SCALE0 = 1.0 / float(np.sqrt(DIM))
SCALE1 = 1.0 / float(np.sqrt(HD8))


def shape_constants():
    f = np.float32
    tri = np.where(np.arange(P)[None, :] > np.arange(P)[:, None], f(NEG), f(0)).astype(f)
    i1 = P + np.arange(P)[:, None]
    j1 = WINDOW + np.arange(SEQ - WINDOW)[None, :]
    band = np.where((i1 < j1) | (i1 > j1 + WINDOW), f(NEG), f(0)).astype(f)
    masks = np.concatenate([tri, band], axis=1)
    t = np.arange(SEQ, dtype=f)
    freq1 = (f(1) / f(10000.0) ** (np.arange(0, HD8, 2, dtype=f) / f(HD8))).astype(f)
    ang1 = np.outer(t, freq1).astype(f)
    cos1 = np.repeat(np.cos(ang1), 2, axis=1)
    sin1 = np.stack([-np.sin(ang1), np.sin(ang1)], axis=-1).reshape(SEQ, HD8)
    rope1 = np.concatenate([cos1, sin1], axis=1).astype(f)
    half = np.arange(0, HD, 2, dtype=f)
    freq2 = (f(1) / f(10000.0) ** (half / f(HD))).astype(f)
    ang2 = (t[:, None] * freq2[None, :]).astype(f)
    base = (half + f(0.4 * HD)) / f(1.4 * HD)
    power = (t - SEQ // 2) / f(WINDOW // 2)
    scale = (base[None, :] ** power[:, None]).astype(f)
    cos2, sin2 = np.cos(ang2).astype(f), np.sin(ang2).astype(f)
    qk_scale = f(8.0)

    def table(c, s):
        return np.concatenate([c, c, -s, s], axis=1)

    rope2 = np.concatenate([table(cos2 * scale * qk_scale, sin2 * scale * qk_scale),
                            table(cos2 / scale, sin2 / scale)], axis=1).astype(f)
    return {"c_ident": np.eye(P, dtype=f), "c_masks": masks, "c_rope1": rope1, "c_rope2": rope2}


ATTN0, ATTN1, LOCAL0, LOCAL1 = range(STREAMS)
TAKES_UP = (0, 1, 2, 4)
BEGINS = (0, 17, 20, 40)
TURNS = (
    "02333110022313001213333333221202222000222333130000"
    "33112210013123331200232211111030013313201221001222"
    "22113003331333002322213032000203222303101023112311"
    "1020"
)
RINGS = {"dense": 4, "score": 2}


class Unit:

    def __init__(self, kind, part=0, source=None, **counts):
        self.kind, self.part, self.source = kind, part, source
        self.uses = {r: counts.pop(r) for r in RINGS if r in counts}
        self.raises = counts
        self.at, self.buffers = {}, {}


def norm_units(source):
    return [Unit("stats", source=source, bn_done=2, moments=2, var_eps=1, rstd=1),
            Unit("apply", source=source, normed=1)]


def attention_units(rotary):
    units = [Unit("turn", source="h", dense=1)]
    extra = dict(rot_cos=1, rot_done=1, lo_ready=1) if rotary else {}
    units += [Unit("qkv", t, dense=1, v_ready=1, hi_ready=1, **extra) for t in range(TT)]
    units += [Unit("turn_q", u, dense=1) for u in range(2)]
    units += [Unit("turn_k", u, dense=1) for u in range(2)]
    units += [Unit("maxes", u, score=1) for u in range(6 if rotary else 8)]
    units += [Unit("negmax", m_hi=1, m_ready=1)]
    units += [Unit("turn_q", u, source="with maxima", dense=1) for u in range(2)]
    for g in range(GROUPS):
        units += [Unit("scores", g, score=2, **(dict(masked=2) if rotary else {})),
                  Unit("mix", g, dense=1)]
    units += [Unit("attn_out", t, dense=1, rec_done=1, att_done=1 if t == 1 else 0) for t in range(TT)]
    return units


def local_units(last):
    units = [Unit("shift", part=0, dense=1)]
    units += [Unit("qkv2", n, dense=1, **(dict(sq_ready=1, sums=1) if n % 3 < 2 else {})) for n in range(6)]

    def rope(u):
        return Unit("rope2", u, cos_part=1, sin_part=1, rot_sum=1, **(dict(ss_ready=1, rn_ready=1) if u == 0 else {}))

    def scale(u):
        return Unit("scale2", u, rope_ready=1)

    units += [rope(0), rope(1), scale(0), rope(2), scale(1), rope(3), scale(2), scale(3)]
    units += [Unit("turn_q2", u, dense=1) for u in range(2)]
    units += [Unit("turn_k2", u, dense=1) for u in range(2)]
    units += [Unit("scores2", u, score=1, max_done=1) for u in range(3)]
    units += [Unit("norm2", t, rec_done=1, p_ready=1) for t in range(TT)]

    def turn_p(u):
        return Unit("turn_p", u, score=1)

    def mix2(u):
        return Unit("mix2", u, dense=1)

    units += [turn_p(0), turn_p(1), mix2(0), turn_p(2), mix2(1), turn_p(3), mix2(2), mix2(3)]
    units += [Unit("project2", dense=1, resid=1)]
    units += [Unit("shift", part=1, dense=1), Unit("back", dense=1)]
    units += norm_units("h")
    units += [Unit("turn", source="gained", dense=1)]
    units += [Unit("up2", dense=3, gelu_done=3)]
    units += [Unit("down2", dense=1, plus_bias=1, resid=1)]
    units += [Unit("finish", out_ready=1) if last else Unit("carry", carried=1)]
    return units


def stream_units(k):
    if k == ATTN0:
        units = norm_units("x") + attention_units(rotary=False)
        units += [Unit("residual", resid=1)] + norm_units("x")
        units += [Unit("turn", source="h", dense=1)] + [Unit("up0", u, dense=1) for u in range(2)]
        units += [Unit("down0", dense=1, plus_bias=1, handed=1)]
    elif k == ATTN1:
        units = [Unit("accept", accepted=1)] + norm_units("x") + attention_units(rotary=True)
        units += [Unit("turn", source="att", dense=1), Unit("project1", dense=1, resid=1)]
        units += norm_units("z") + [Unit("carry", carried=1)]
    else:
        units = ([Unit("accept", accepted=1)] if k == LOCAL1 else []) + local_units(last=k == LOCAL1)
    for n, u in enumerate(units):
        u.stream, u.number = k, n
        u.stage = TAKES_UP[k] + (1 if n >= BEGINS[k] > 0 else 0)
    return units


def merged_units():
    queues = []
    for k in range(STREAMS):
        units = stream_units(k)
        queues.append(iter(units[BEGINS[k]:] + units[:BEGINS[k]]))
    return [next(queues[int(k)]) for k in TURNS]


class Pass:

    def __init__(self, first, times):
        self.first, self.times = first, times
        self.units = merged_units()
        position = {r: 0 for r in RINGS}
        for u in self.units:
            for r, n in u.uses.items():
                u.buffers[r] = [(position[r] + i) % RINGS[r] for i in range(n)]
                position[r] += n
        self.units = [u for u in self.units if 0 <= first - u.stage < BATCH]
        self.per, self.before = {}, None


def plan():
    last = max(u.stage for k in range(STREAMS) for u in stream_units(k))
    passes = [Pass(p, 1) for p in range(last + 1)]
    passes += [Pass(last + 1, BATCH - last - 1)]
    passes += [Pass(BATCH + p, 1) for p in range(last)]
    count, before = {}, None
    for pas in passes:
        start = dict(count)
        pas.before, before = before, pas
        for u in pas.units:
            u.at = dict(count)
            for r, buffers in u.buffers.items():
                for i, b in enumerate(buffers):
                    count[r, b] = count.get((r, b), 0) + 1
                    buffers[i] = (b, count[r, b])
            for name, n in u.raises.items():
                count[name, u.stream] = count.get((name, u.stream), 0) + n
        pas.per = {c: n - start.get(c, 0) for c, n in count.items()}
        for c in count:
            count[c] += (pas.times - 1) * pas.per[c]
    return passes


def earlier(pas, u, kind, part=None):
    v = [v for v in stream_units(u.stream) if v.number < u.number and v.kind == kind and (part is None or v.part == part)][-1]
    ago = u.stage - v.stage
    assert ago in (0, 1)
    home = pas if ago == 0 or pas.times > 1 else pas.before
    found = [w for w in home.units if (w.stream, w.number) == (v.stream, v.number)][0]
    if ago == 0:
        return found
    rounds = -1 if home is pas else home.times - 1
    seen = Unit(kind, found.part)
    seen.stream, seen.number, seen.stage = found.stream, found.number, found.stage
    seen.at = {c: n + rounds * home.per.get(c, 0) for c, n in found.at.items()}
    seen.buffers = {r: [(b, n + rounds * home.per[r, b]) for b, n in found.buffers[r]] for r in found.buffers}
    return seen


def fused_block(nc, x, wqkv0, w1_0, b1_0, w2_0, b2_0, wqkv1, wo1, wqkv2, q_scale, k_scale, wo2,
                ln_g, ln_b, w1_2, b1_2, w2_2, b2_2, c_ident, c_masks, c_rope1, c_rope2, out):
    f32, f32r = mybir.dt.float32, mybir.dt.float32r
    ALU, ACT, AX = mybir.AluOpType, mybir.ActivationFunctionType, mybir.AxisListType

    x_rows = x.rearrange("b (t p) d -> b p t d", p=P)
    out_rows = out.rearrange("b (t p) d -> b p t d", p=P)

    with ExitStack() as ctx:
        def sb(name, shape, dt=f32):
            return ctx.enter_context(nc.sbuf_tensor(name, shape, dt))

        def pb(name, shape):
            return ctx.enter_context(nc.psum_tensor(name, shape, f32))

        def sem(name):
            return ctx.enter_context(nc.semaphore(name))

        ident_r = sb("ident_r", [P, P], f32r)
        ident = ident_r[:].bitcast(f32)
        masks = sb("masks", [P, P + SEQ - WINDOW], f32r)
        causal = masks[:, 0:P]
        band1 = masks[:, P:P + SEQ - WINDOW]
        band0 = masks[:, P + WINDOW:2 * P + WINDOW]
        wqkv_sb = sb("wqkv_sb", [P, 2, 3 * DIM])
        wo1_sb = sb("wo1_sb", [P, DIM])
        w1_0_sb = sb("w1_0_sb", [P, FF0])
        b1_0_sb = sb("b1_0_sb", [P, FF0 // P])
        w2_0_sb = sb("w2_0_sb", [P, FF0 // P, DIM])
        b2_0_sb = sb("b2_0_sb", [P, DIM])
        wqkv2_sb = sb("wqkv2_sb", [P, LAYERS, 3 * INNER])
        wo2_sb = sb("wo2_sb", [P, LAYERS, INNER // P, DIM])
        w1_2_sb = sb("w1_2_sb", [P, LAYERS, 2 * HID])
        b1_2_sb = sb("b1_2_sb", [P, LAYERS, 2, 3])
        w2_2_sb = sb("w2_2_sb", [P, LAYERS, 3, DIM])
        b2_2_sb = sb("b2_2_sb", [P, LAYERS, DIM])
        lng_sb = sb("lng_sb", [P, LAYERS])
        lnb_sb = sb("lnb_sb", [P, LAYERS])
        rope1_sb = sb("rope1_sb", [P, TT, 2, HD8])
        rope2_sb = sb("rope2_sb", [P, LAYERS, TT, 2, 2, HD])
        minus_half = sb("minus_half", [P, 4 * HEADS])
        eps_tile = sb("eps_tile", [P, TT])

        xin = sb("xin", [P, TT, DIM])
        xout = sb("xout", [P, TT, DIM])
        X1 = sb("X1", [P, TT, DIM])
        X2 = sb("X2", [P, TT, DIM])
        Y2 = sb("Y2", [P, TT, DIM])
        XY3 = sb("XY3", [P, 2, TT, DIM])
        hand01 = sb("hand01", [P, TT, DIM])
        hand23 = sb("hand23", [P, 2, TT, DIM])
        bn = sb("bn", [P, STREAMS, TT, 6])
        moments = sb("moments", [P, STREAMS, TT, 2])
        veps = sb("veps", [P, STREAMS, TT])
        rstd = sb("rstd", [P, STREAMS, TT])
        negmax = sb("negmax", [P, STREAMS, TT, H16])
        recip = sb("recip", [P, STREAMS, TT, H16])
        QB = sb("QB", [P, 2, TT, H16, 32])
        KB = sb("KB", [P, 2, TT, H16, 32])
        qT = sb("qT", [P, 2, GROUPS, SEQ], f32r)
        kT = sb("kT", [P, 2, H16, SEQ], f32r)
        V = sb("V", [P, 2, TT, H16, 16])
        rawC = sb("rawC", [P, 2, 1024])
        probs_in = sb("probs", [P, 3 * 1024 + 512])
        probs = [[probs_in[:, 0:1024], probs_in[:, 1024:2048]], [probs_in[:, 2048:3072], probs_in[:, 3072:3584]]]
        oT = rawC[:, :, :].rearrange("p a (g q) -> p a g q", g=GROUPS)
        up0T = rawC[:, ATTN0, :].rearrange("p (c q) -> p c q", c=FF0 // P)
        cosine1 = rawC[:, ATTN1, 0:512].rearrange("p (t n) -> p t n", t=TT)
        sine1 = rawC[:, ATTN1, 512:1024].rearrange("p (t n) -> p t n", t=TT)
        hS = sb("hS", [P, 2, SEQ + 1])
        rawA = sb("rawA", [P, 2, 1024])
        rawB = sb("rawB", [P, 2, 1024])
        V2 = sb("V2", [P, 2, TT, INNER])
        rawQ = sb("rawQ", [P, 2, PAIRS * SEQ])
        qT2 = rawQ[:, :, :].rearrange("p l (c q) -> p l c q", c=PAIRS)
        kT2 = sb("kT2", [P, 2, PAIRS, 2, SEQ])
        rawP = sb("rawP", [P, 2, HEADS * P])
        P0 = rawP[:, :, :].rearrange("p l (h k) -> p l h k", h=HEADS)
        P1 = sb("P1", [P, 2, HEADS, SEQ])
        expsum = sb("expsum", [P, 2, TT, HEADS])
        ss = sb("ss", [P, 2, TT, 2, HEADS])
        rn = sb("rn", [P, 2, TT, 2, HEADS])
        q2 = rawA[:, :, 0:1024].rearrange("p l (t n) -> p l t n", t=TT)
        k2 = rawB[:, :, :].rearrange("p l (t n) -> p l t n", t=TT)
        probs2 = [[raw[:, l, 0:640].rearrange("p (e n) -> p e n", e=2) for raw in (rawA, rawQ)] for l in range(LAYERS)]
        o2T = rawB[:, :, :].rearrange("p l (c q) -> p l c q", c=PAIRS)
        up2T = rawA[:, :, 0:3 * SEQ].rearrange("p l (c q) -> p l c q", c=3)
        two_in_P0 = rawP[:, :, :].rearrange("p l (u n) -> p l u n", u=2)
        gates = rawP[:, :, :].rearrange("p l (c q) -> p l c q", c=4)
        cosine2 = rawQ[:, :, :].rearrange("p l (u n) -> p l u n", u=2)
        h = [probs[k][1][:, 0:TT * DIM].rearrange("p (t d) -> p t d", t=TT) for k in range(2)]\
            + [V2[:, l, 0, 0:TT * DIM].rearrange("p (t d) -> p t d", t=TT) for l in range(LAYERS)]
        hT = [probs[k][0][:, 0:SEQ] for k in range(2)] + [rawQ[:, l, 0:SEQ] for l in range(LAYERS)]
        X = [probs[ATTN0][0][:, 2 * SEQ:2 * SEQ + TT * DIM].rearrange("p (t d) -> p t d", t=TT), X1[:], X2[:], XY3[:, 0]]
        Y = [Y2[:], XY3[:, 1]]
        att = h
        biased = h
        ident_in = rawC[:, 0, 0:P]
        masks_in = rawA[:, 0, 0:P + SEQ - WINDOW]
        scales_in = rawB[:, 0, 0:2 * LAYERS * HD].rearrange("p (m l d) -> p m l d", m=2, l=LAYERS)
        rope2_in = rawB[:, 1, 0:TT * 4 * HD].rearrange("p (t m c d) -> p t m c d", t=TT, m=2, c=2)

        psum = {"dense": [pb(f"dense{b}", [P, 512]) for b in range(RINGS["dense"])],
                "score": [pb(f"score{b}", [P, 1024]) for b in range(RINGS["score"])]}

        passes = plan()
        raised = {}
        for pas in passes:
            for u in pas.units:
                for name, n in u.raises.items():
                    if n and (name, u.stream) not in raised:
                        raised[name, u.stream] = sem(f"{name}_{u.stream}")
        full = {r: [sem(f"{r}{b}_full") for b in range(n)] for r, n in RINGS.items()}
        emptied = {r: [sem(f"{r}{b}_emptied") for b in range(n)] for r, n in RINGS.items()}
        loaded = sem("loaded")
        N_LOADS = [0]
        x_loaded, stored = sem("x_loaded"), sem("stored")
        setup_pool, setup_act, setup_dve = sem("setup_pool"), sem("setup_act"), sem("setup_dve")
        paced = sem("paced")
        staged = sem("staged")

        def sig(name, u):
            return raised[name, u.stream]

        def total(pas, j, c, count):
            return count + (j * pas.per.get(c, 0) if pas.times > 1 else 0)

        def so_far(name, k, u, pas, j):
            return total(pas, j, (name, k), u.at.get((name, k), 0))

        def ever(name, k, u):
            return u.at.get((name, k), 0) > 0

        def free(ring, u, n=0):
            b, count = u.buffers[ring][n]
            return (ring, b), count

        def taken(ring, u, n=0):
            b, count = u.buffers[ring][n]
            return (ring, b), count + 1

        def newest(pas, j, *counts):
            return [(emptied[c[0]][c[1]], total(pas, j, c, max(n for b, n in counts if b == c))) for c in dict(counts)]

        def uses(ring, u, pas, j, n=0):
            b, count = u.buffers[ring][n]
            return total(pas, j, (ring, b), count)

        def tile(ring, u, n=0):
            return psum[ring][u.buffers[ring][n][0]]

        def has_emptied(ring, u, n=0):
            return emptied[ring][u.buffers[ring][n][0]]

        def has_filled(ring, u, n=0):
            return full[ring][u.buffers[ring][n][0]]

        def run(eng, unit):
            for pas in passes:
                if pas.times > 1:
                    with eng.Fori(0, pas.times) as j:
                        for u in pas.units:
                            unit(u, pas, j)
                else:
                    for u in pas.units:
                        unit(u, pas, 0)

        block = ctx.enter_context(nc.Block())

        @block.sync
        def _(sp):
            def load(dst, src):
                sp.dma_start(dst, src).then_inc(loaded, 16)
                N_LOADS[0] += 1

            sp.sem_inc(stored, 16)
            sp.dma_start(xin[:], x_rows[0]).then_inc(x_loaded, 16)
            load(ident_in, c_ident)
            load(masks_in, c_masks)
            load(wqkv_sb[:, 0], wqkv0)
            load(w1_0_sb[:], w1_0)
            load(b1_0_sb[:], b1_0)
            load(w2_0_sb[:], w2_0.rearrange("(c p) d -> p c d", p=P))
            load(b2_0_sb[:], b2_0.partition_broadcast(P))
            load(wqkv_sb[:, 1], wqkv1)
            load(wo1_sb[:], wo1)
            load(rope1_sb[:], c_rope1.rearrange("(t p) (c d) -> p t c d", p=P, c=2))
            load(rope2_in, c_rope2.rearrange("(t p) (m c d) -> p t m c d", p=P, m=2, c=2))
            load(wqkv2_sb[:], wqkv2.rearrange("l k n -> k l n"))
            load(lng_sb[:], ln_g)
            load(lnb_sb[:], ln_b)
            load(b1_2_sb[:], b1_2)
            load(w1_2_sb[:], w1_2.rearrange("l k n -> k l n"))
            for l in range(LAYERS):
                load(scales_in[:, 0, l, :], q_scale[l].partition_broadcast(P))
                load(scales_in[:, 1, l, :], k_scale[l].partition_broadcast(P))
                load(b2_2_sb[:, l, :], b2_2[l].partition_broadcast(P))
                load(wo2_sb[:, l], wo2[l].rearrange("(c p) d -> p c d", p=P))
                for c, (at, n) in enumerate(HTILES):
                    load(w2_2_sb[0:n, l, c, :], w2_2[l, at:at + n, :])

            def next_in(n):
                sp.wait_ge(raised["resid", ATTN0], n)
                sp.dma_start(xin[:], x_rows[n]).then_inc(x_loaded, 16)

            def next_out(n):
                sp.wait_ge(raised["out_ready", LOCAL1], n + 1)
                sp.dma_start(out_rows[n], xout[:]).then_inc(stored, 16)

            LAG = 4
            for p in range(LAG):
                next_in(p + 1)
            with sp.Fori(0, BATCH - 1 - LAG) as j:
                next_in(j + LAG + 1)
                next_out(j)
            for n in range(BATCH - 1 - LAG, BATCH):
                next_out(n)
            sp.wait_ge(stored, 16 * BATCH + 16)

        ALL_LOADED = 16 * N_LOADS[0]
        PRESETS = 11

        @block.gpsimd
        def _(pool):
            nc.gpsimd.memset(minus_half[:], -0.5).then_inc(setup_pool, 1)
            nc.gpsimd.memset(eps_tile[:], EPS).then_inc(setup_pool, 1)
            nc.gpsimd.memset(V[:], 0.0).then_inc(setup_pool, 1)
            nc.gpsimd.memset(QB[:], 0.0).then_inc(setup_pool, 1)
            nc.gpsimd.memset(KB[:], 0.0).then_inc(setup_pool, 1)
            nc.gpsimd.memset(kT[:].bitcast(f32), 0.0).then_inc(setup_pool, 1)
            nc.gpsimd.memset(kT2[:], 0.0).then_inc(setup_pool, 1)
            nc.gpsimd.memset(P1[:], 0.0).then_inc(setup_pool, 1)
            nc.gpsimd.memset(hS[:], 0.0).then_inc(setup_pool, 1)
            pool.wait_ge(setup_pool, PRESETS - 2)
            nc.gpsimd.memset(V[:, :, :, :, HD8:HD8 + 1], 1.0).then_inc(setup_pool, 1)
            nc.gpsimd.memset(KB[:, :, :, :, 24:26], 1.0).then_inc(setup_pool, 1)
            for r, n in RINGS.items():
                for b in range(n):
                    pool.sem_inc(emptied[r][b], 1)
            pool.wait_ge(loaded, ALL_LOADED)
            pool.wait_ge(setup_pool, PRESETS)

            def unit(u, pas, j):
                k, l = u.stream, u.stream - LOCAL0
                if u.kind == "stats":
                    pool.wait_ge(sig("moments", u), so_far("moments", k, u, pas, j) + 2)
                    nc.gpsimd.tensor_tensor(veps[:, k, :], moments[:, k, :, 1], eps_tile[:], ALU.add)\
                        .then_inc(sig("var_eps", u), 1)
                    pool.wait_ge(sig("var_eps", u), so_far("var_eps", k, u, pas, j) + 1)
                    nc.gpsimd.tensor_tensor(rstd[:, k, :], veps[:, k, :], minus_half[:, 0:TT], ALU.pow)\
                        .then_inc(sig("rstd", u), 1)
                elif u.kind == "qkv" and k == ATTN1:
                    t = u.part
                    for sem, count in newest(pas, j, taken("dense", u, 0)):
                        pool.wait_ge(sem, count)
                    nc.gpsimd.tensor_tensor(cosine1[:, t], cosine1[:, t], sine1[:, t], ALU.add)\
                        .then_inc(sig("rot_done", u), 1)
                elif u.kind == "scores" and k == ATTN1:
                    for t in range(TT):
                        for sem, count in newest(pas, j, taken("score", u, t)):
                            pool.wait_ge(sem, count)
                        pool.sem_inc(paced, 1)
                        w = SEQ if t == 0 else P
                        part = probs[k][t][:, 0:4 * w].rearrange("p (j q) -> p j q", j=4)[:, :, 0:P]
                        nc.gpsimd.affine_select(out=part, in_=part, compare_op=ALU.is_ge, fill=0.0, base=0,
                                                pattern=[[0, 4], [1, P]], channel_multiplier=-1)\
                            .then_inc(sig("masked", u), 1)
                elif u.kind in ("down0", "down2"):
                    pool.wait_ge(sig("resid", u), so_far("resid", k, u, pas, j))
                    for sem, count in newest(pas, j, taken("dense", earlier(pas, u, "turn"), 0)):
                        pool.wait_ge(sem, count)
                    old, bias = (X[k], b2_0_sb[:]) if u.kind == "down0" else (Y[l], b2_2_sb[:, l])
                    nc.gpsimd.tensor_tensor(biased[k], old, bias.unsqueeze(1).broadcast_to([P, TT, DIM]), ALU.add)\
                        .then_inc(sig("plus_bias", u), 1)
                elif u.kind == "rope2":
                    t, m, n = u.part // 2, u.part % 2, u.part % 2
                    raw = (q2, k2)[m][:, l, t, :].rearrange("p (h d) -> p h d", h=HEADS)
                    tab = rope2_sb[:, l, t, m, 0, :].unsqueeze(1).broadcast_to([P, HEADS, HD])
                    cos = cosine2[:, l, n, :].rearrange("p (h d) -> p h d", h=HEADS)
                    for sem, count in newest(pas, j, taken("dense", earlier(pas, u, "qkv2", 3 * t + m), 0)):
                        pool.wait_ge(sem, count)
                    if u.part >= 2:
                        pool.wait_ge(sig("rope_ready", u), so_far("rope_ready", k, u, pas, j))
                    nc.gpsimd.tensor_tensor(cos, raw, tab, ALU.mult).then_inc(sig("cos_part", u), 1)
                    pool.wait_ge(sig("cos_part", u), so_far("cos_part", k, u, pas, j) + 1)
                    pool.wait_ge(sig("sin_part", u), so_far("sin_part", k, u, pas, j) + 1)
                    nc.gpsimd.tensor_tensor(cosine2[:, l, n, :], cosine2[:, l, n, :], two_in_P0[:, l, n, :], ALU.add)\
                        .then_inc(sig("rot_sum", u), 1)
                    if u.part == 0:
                        pool.wait_ge(sig("ss_ready", u), so_far("ss_ready", k, u, pas, j) + 1)
                        nc.gpsimd.tensor_tensor(rn[:, l].rearrange("p t m h -> p (t m h)"),
                                                ss[:, l].rearrange("p t m h -> p (t m h)"),
                                                minus_half[:], ALU.pow).then_inc(sig("rn_ready", u), 1)
                elif u.kind == "finish":
                    pool.wait_ge(sig("resid", u), so_far("resid", k, u, pas, j))
                    pool.wait_ge(stored, total(pas, j, ("out_ready", k), 16 * (u.at.get(("out_ready", k), 0) + 1))
                                 if pas.times == 1 else j * 16 + 16 * (u.at.get(("out_ready", k), 0) + 1))
                    nc.gpsimd.tensor_tensor(xout[:], X[k], Y[l], ALU.add).then_inc(sig("out_ready", u), 1)

            run(pool, unit)

        @block.scalar
        def _(act):
            act.wait_ge(loaded, ALL_LOADED)
            nc.scalar.activation(ident_r[:], ident_in, ACT.Copy).then_inc(setup_act, 1)
            nc.scalar.activation(masks[:], masks_in, ACT.Copy).then_inc(setup_act, 1)
            act.wait_ge(setup_pool, PRESETS)

            def unit(u, pas, j):
                k, l = u.stream, u.stream - LOCAL0
                if u.kind == "turn":
                    act.wait_ge(has_filled("dense", u), uses("dense", u, pas, j))
                    src = tile("dense", u)[:, 0:SEQ]
                    if u.source == "gained":
                        nc.scalar.activation(hT[k], src, ACT.Identity, bias=lnb_sb[:, l:l + 1], scale=lng_sb[:, l:l + 1])\
                            .then_inc(has_emptied("dense", u), 1)
                    else:
                        nc.scalar.activation(hT[k], src, ACT.Copy).then_inc(has_emptied("dense", u), 1)
                elif u.kind == "back":
                    act.wait_ge(has_filled("dense", u), uses("dense", u, pas, j))
                    nc.scalar.activation(h[k].rearrange("p t d -> p (t d)"), tile("dense", u)[:, 0:SEQ], ACT.Copy)\
                        .then_inc(has_emptied("dense", u), 1)
                elif u.kind == "shift":
                    act.wait_ge(has_filled("dense", u), uses("dense", u, pas, j))
                    src = tile("dense", u)
                    nc.scalar.activation(hS[0:64, l, 0:SEQ], src[0:64, 0:SEQ], ACT.Copy)
                    nc.scalar.activation(hS[64:128, l, 1:SEQ + 1], src[64:128, 0:SEQ], ACT.Copy)\
                        .then_inc(has_emptied("dense", u), 1)
                elif u.kind == "qkv":
                    t = u.part
                    src = tile("dense", u)
                    act.wait_ge(has_filled("dense", u), uses("dense", u, pas, j))
                    nc.scalar.activation(V[:, k, t, :, 0:HD8], src[:, 2 * DIM:3 * DIM].rearrange("p (h d) -> p h d", h=H16),
                                         ACT.Copy).then_inc(sig("v_ready", u), 1)
                    qk = src[:, 0:2 * DIM]
                    if k == ATTN1:
                        act.wait_ge(sig("rot_done", u), so_far("rot_done", k, u, pas, j) + 1)
                        qk = cosine1[:, t]
                    q, kk = (qk[:, m * DIM:(m + 1) * DIM].rearrange("p (h d) -> p h d", h=H16) for m in range(2))
                    for dst, src, places in ((QB, q, (0, 8)), (KB, kk, (0, 16))):
                        for at in places:
                            last = nc.scalar.activation(dst[:, k, t, :, at:at + HD8].bitcast(f32r), src, ACT.Copy)
                    last.then_inc(sig("hi_ready", u), 1)
                elif u.kind in ("turn_q", "turn_q2"):
                    act.wait_ge(has_filled("dense", u), uses("dense", u, pas, j))
                    dst = qT[:, k] if u.kind == "turn_q" else qT2[:, l]
                    nc.scalar.activation(dst[:, 2 * u.part:2 * u.part + 2, :].rearrange("p g q -> p (g q)"), tile("dense", u)[:],
                                         ACT.Copy).then_inc(has_emptied("dense", u), 1)
                elif u.kind == "turn_k":
                    act.wait_ge(has_filled("dense", u), uses("dense", u, pas, j))
                    heads = kT[:, k, 8 * u.part:8 * u.part + 8, :].rearrange("p (g j) q -> p j g q", j=4)
                    for n in range(4):
                        r = slice(32 * n, 32 * n + 32)
                        last = nc.scalar.activation(heads[r, n], tile("dense", u)[r, :].rearrange("p (g q) -> p g q", g=2), ACT.Copy)
                    last.then_inc(has_emptied("dense", u), 1)
                elif u.kind == "scores":
                    for t in range(TT):
                        act.wait_ge(has_filled("score", u, t), uses("score", u, pas, j, t))
                        s = tile("score", u, t)
                        if k == ATTN0:
                            nc.scalar.activation(probs[k][t], s[:], ACT.Exp, scale=SCALE0)\
                                .then_inc(has_emptied("score", u, t), 1)
                        elif t == 0:
                            nc.scalar.activation(probs[k][t], s[:], ACT.Exp, scale=SCALE1)\
                                .then_inc(has_emptied("score", u, t), 1)
                        else:
                            nc.scalar.activation(probs[k][t].rearrange("p (j q) -> p j q", j=4),
                                                 s[:, :].rearrange("p (j q) -> p j q", j=4)[:, :, P:SEQ], ACT.Exp, scale=SCALE1)\
                                .then_inc(has_emptied("score", u, t), 1)
                elif u.kind == "up0":
                    act.wait_ge(has_filled("dense", u), uses("dense", u, pas, j))
                    for e in range(2):
                        c = 2 * u.part + e
                        last = nc.scalar.activation(up0T[:, c, :], tile("dense", u)[:, e * SEQ:(e + 1) * SEQ], ACT.Relu,
                                                    bias=b1_0_sb[:, c:c + 1])
                    last.then_inc(has_emptied("dense", u), 1)
                elif u.kind == "qkv2":
                    t, m = u.part // 3, u.part % 3
                    act.wait_ge(has_filled("dense", u), uses("dense", u, pas, j))
                    if m < 2:
                        if t == 1:
                            act.wait_ge(sig("sums", u), so_far("sums", k, u, pas, j) - 1)
                        nc.scalar.activation(two_in_P0[:, l, m, :], tile("dense", u)[:], ACT.Square).then_inc(sig("sq_ready", u), 1)
                    dst = (q2, k2, V2)[m]
                    nc.scalar.activation(dst[:, l, t, :], tile("dense", u)[:], ACT.Copy).then_inc(has_emptied("dense", u), 1)
                elif u.kind == "scores2":
                    n = u.part
                    act.wait_ge(sig("max_done", u), so_far("max_done", k, u, pas, j) + 1)
                    s = tile("score", u)
                    t = 0 if n == 0 else 1
                    for e in range(8 if n == 0 else 4):
                        hd = e if n == 0 else 4 * (n - 1) + e
                        if n == 0:
                            dst, src = P0[:, l, hd, :], s[:, e * P:(e + 1) * P]
                        else:
                            dst, src = P1[:, l, hd, WINDOW:SEQ], s[:, e * SEQ:e * SEQ + SEQ - WINDOW]
                        last = nc.scalar.activation(dst, src, ACT.Exp, bias=negmax[:, k, t, hd:hd + 1],
                                                    accum_out=expsum[:, l, t, hd:hd + 1])
                    last.then_inc(has_emptied("score", u), 1)
                elif u.kind == "turn_p":
                    act.wait_ge(has_filled("score", u), uses("score", u, pas, j))
                    nc.scalar.activation(probs2[l][u.part % 2],
                                         tile("score", u)[:, :].rearrange("p (e n) -> p e n", e=2)[:, :, 0:320], ACT.Copy)\
                        .then_inc(has_emptied("score", u), 1)
                elif u.kind == "up2":
                    for c, (at, n) in enumerate(HTILES):
                        act.wait_ge(has_filled("dense", u, c), uses("dense", u, pas, j, c))
                        nc.scalar.activation(gates[0:n, l, c, :], tile("dense", u, c)[0:n, SEQ:2 * SEQ], ACT.Gelu,
                                             bias=b1_2_sb[0:n, l, 1, c:c + 1]).then_inc(sig("gelu_done", u), 1)
                elif u.kind == "carry":
                    if k == LOCAL0:
                        if ever("accepted", LOCAL1, u):
                            act.wait_ge(raised["accepted", LOCAL1], so_far("accepted", LOCAL1, u, pas, j))
                    else:
                        if ever("carried", LOCAL0, u):
                            act.wait_ge(raised["carried", LOCAL0], so_far("carried", LOCAL0, u, pas, j))
                        act.wait_ge(sig("resid", u), so_far("resid", k, u, pas, j))
                    nc.scalar.activation(X[LOCAL0] if k == ATTN1 else hand23[:, 0], X[k], ACT.Copy).then_inc(sig("carried", u), 1)
                elif u.kind == "accept":
                    if k == ATTN1:
                        act.wait_ge(raised["handed", ATTN0], so_far("handed", ATTN0, u, pas, j))
                        if ever("normed", k, u):
                            act.wait_ge(sig("normed", u), so_far("normed", k, u, pas, j))
                            act.wait_ge(sig("carried", u), so_far("carried", k, u, pas, j))
                        nc.scalar.activation(X1[:], hand01[:], ACT.Copy).then_inc(sig("accepted", u), 1)
                    else:
                        act.wait_ge(raised["resid", LOCAL0], so_far("resid", LOCAL0, u, pas, j))
                        act.wait_ge(raised["carried", LOCAL0], so_far("carried", LOCAL0, u, pas, j))
                        if ever("out_ready", k, u):
                            act.wait_ge(sig("out_ready", u), so_far("out_ready", k, u, pas, j))
                        nc.scalar.activation(XY3[:], hand23[:], ACT.Copy).then_inc(sig("accepted", u), 1)

            run(act, unit)

        @block.vector
        def _(dve):
            dve.wait_ge(loaded, ALL_LOADED)
            dve.wait_ge(setup_pool, PRESETS)
            for t in psum["dense"]:
                nc.vector.memset(t[:], 0.0).then_inc(setup_dve, 1)
            for l in range(LAYERS):
                for t in range(TT):
                    for m in range(2):
                        sc = scales_in[:, m, l, :]
                        nc.vector.tensor_tensor(rope2_sb[:, l, t, m, 0, :], rope2_in[:, t, m, 0, :], sc, ALU.mult)
                        nc.vector.tensor_tensor(rope2_sb[:, l, t, m, 1, 0:32], rope2_in[:, t, m, 1, 0:32], sc[:, 32:64], ALU.mult)
                        nc.vector.tensor_tensor(rope2_sb[:, l, t, m, 1, 32:64], rope2_in[:, t, m, 1, 32:64], sc[:, 0:32], ALU.mult)\
                            .then_inc(staged, 1)
            dve.wait_ge(staged, 4 * LAYERS)
            dve.wait_ge(setup_act, 2)

            def unit(u, pas, j):
                k, l = u.stream, u.stream - LOCAL0
                first = u.number < 3
                if u.kind in ("stats", "apply"):
                    rows = xin[:] if k == ATTN0 and first else h[k] if u.source == "h" else X[k]
                if u.kind == "stats":
                    if k == ATTN0 and first:
                        n = 16 * (pas.first + 1)
                        dve.wait_ge(x_loaded, n + j * 16 if pas.times > 1 else n)
                    elif k == ATTN1 and first:
                        dve.wait_ge(sig("accepted", u), so_far("accepted", k, u, pas, j))
                    elif u.source == "h":
                        for sem, count in newest(pas, j, taken("dense", earlier(pas, u, "back"), 0)):
                            dve.wait_ge(sem, count)
                    else:
                        dve.wait_ge(sig("resid", u), so_far("resid", k, u, pas, j))
                    for t in range(TT):
                        nc.vector.bn_stats(bn[:, k, t, :], rows[:, t, :]).then_inc(sig("bn_done", u), 1)
                    for t in range(TT):
                        dve.wait_ge(sig("bn_done", u), so_far("bn_done", k, u, pas, j) + t + 1)
                        dve.sem_inc(paced, 1)
                        nc.vector.bn_aggr(moments[:, k, t, :], bn[:, k, t, :]).then_inc(sig("moments", u), 1)
                elif u.kind == "apply":
                    dve.wait_ge(sig("rstd", u), so_far("rstd", k, u, pas, j))
                    dst = h[k]
                    if u.source == "z":
                        if ever("resid", LOCAL0, u):
                            dve.wait_ge(raised["resid", LOCAL0], so_far("resid", LOCAL0, u, pas, j))
                        dst = Y[0]
                    for t in range(TT):
                        last = nc.vector.tensor_scalar(dst[:, t, :], rows[:, t, :], moments[:, k, t, 0:1], rstd[:, k, t:t + 1],
                                                       ALU.subtract, ALU.mult)
                    last.then_inc(sig("normed", u), 1)
                elif u.kind == "qkv":
                    t, s = u.part, tile("dense", u)
                    dve.wait_ge(has_filled("dense", u), uses("dense", u, pas, j))
                    nc.vector.memset(QB[:, k, t, :, 24:26], 0.0)
                    qk = s[:, 0:2 * DIM]
                    if k == ATTN1:
                        dve.wait_ge(sig("v_ready", u), so_far("v_ready", k, u, pas, j) + 1)
                        cos = rope1_sb[:, t, 0, :].unsqueeze(1).broadcast_to([P, 2 * H16, HD8])
                        nc.vector.tensor_tensor(cosine1[:, t].rearrange("p (h d) -> p h d", d=HD8),
                                                qk.rearrange("p (h d) -> p h d", d=HD8), cos, ALU.mult).then_inc(sig("rot_cos", u), 1)
                        sn = sine1[:, t].rearrange("p (h d e) -> p h d e", d=HD8 // 2, e=2)
                        sw = qk.rearrange("p (h d e) -> p h d e", d=HD8 // 2, e=2)
                        tab = rope1_sb[:, t, 1, :].rearrange("p (d e) -> p d e", e=2)
                        for e in range(2):
                            last = nc.vector.tensor_tensor(sn[:, :, :, e], sw[:, :, :, 1 - e],
                                                           tab[:, :, e].unsqueeze(1).broadcast_to([P, 2 * H16, HD8 // 2]), ALU.mult)
                        last.then_inc(has_emptied("dense", u), 1)
                        qk = cosine1[:, t]
                    dve.wait_ge(sig("hi_ready", u), so_far("hi_ready", k, u, pas, j) + 1)
                    q, kk = (qk[:, m * DIM:(m + 1) * DIM].rearrange("p (h d) -> p h d", h=H16) for m in range(2))
                    nc.vector.tensor_tensor(QB[:, k, t, :, 16:24].bitcast(f32r), q, QB[:, k, t, :, 0:8], ALU.subtract)
                    nc.vector.tensor_tensor(KB[:, k, t, :, 8:16].bitcast(f32r), kk, KB[:, k, t, :, 0:8], ALU.subtract)\
                        .then_inc(has_emptied("dense", u) if k == ATTN0 else sig("lo_ready", u), 1)
                elif u.kind == "maxes":
                    dve.wait_ge(has_filled("score", u), uses("score", u, pas, j))
                    n = u.part
                    if k == ATTN0:
                        t, h0, nh = n // 4, 4 * (n % 4), 4
                    elif n < 2:
                        t, h0, nh = 0, 8 * n, 8
                    else:
                        t, h0, nh = 1, 4 * (n - 2), 4
                    nc.vector.reduce_max(negmax[:, k, t, h0:h0 + nh], tile("score", u)[:, :].rearrange("p (h k) -> p h k", h=nh),
                                         AX.X, negate=True).then_inc(has_emptied("score", u), 1)
                elif u.kind == "negmax":
                    for sem, count in newest(pas, j, *(taken("score", earlier(pas, u, "maxes", n)) for n in range(6 if k == ATTN1 else 8))):
                        dve.wait_ge(sem, count)
                    neg = negmax[:, k].rearrange("p t h -> p (t h)")
                    place = QB[:, k].rearrange("p t h c -> p (t h) c")
                    nc.vector.tensor_copy(place[:, :, 24].bitcast(f32r), neg).then_inc(sig("m_hi", u), 1)
                    dve.wait_ge(sig("m_hi", u), so_far("m_hi", k, u, pas, j) + 1)
                    nc.vector.tensor_tensor(place[:, :, 25].bitcast(f32r), neg, place[:, :, 24], ALU.subtract)\
                        .then_inc(sig("m_ready", u), 1)
                elif u.kind in ("mix", "mix2"):
                    dve.wait_ge(has_filled("dense", u), uses("dense", u, pas, j))
                    dst = oT[:, k, u.part, :] if u.kind == "mix" else o2T[:, l, u.part, :]
                    nc.vector.tensor_copy(dst, tile("dense", u)[:, 0:SEQ]).then_inc(has_emptied("dense", u), 1)
                elif u.kind == "attn_out":
                    t = u.part
                    dve.wait_ge(has_filled("dense", u), uses("dense", u, pas, j))
                    heads = tile("dense", u)[:, :].rearrange("p (h c) -> p h c", c=32)
                    nc.vector.reciprocal(recip[:, k, t, :], heads[:, :, HD8]).then_inc(sig("rec_done", u), 1)
                    dve.wait_ge(sig("rec_done", u), so_far("rec_done", k, u, pas, j) + 1)
                    nc.vector.tensor_tensor(att[k][:, t, :].rearrange("p (h d) -> p h d", h=H16), heads[:, :, 0:HD8],
                                            recip[:, k, t, :].unsqueeze(2).broadcast_to([P, H16, HD8]), ALU.mult)\
                        .then_inc(has_emptied("dense", u), 1)
                elif u.kind == "residual":
                    for sem, count in newest(pas, j, *(taken("dense", earlier(pas, u, "attn_out", t)) for t in range(TT))):
                        dve.wait_ge(sem, count)
                    nc.vector.tensor_tensor(X[k], xin[:], att[k], ALU.add).then_inc(sig("resid", u), 1)
                elif u.kind in ("project1", "project2", "down0", "down2"):
                    dst = old = X[k] if u.kind == "project1" else Y[l]
                    if u.kind in ("down0", "down2"):
                        dve.wait_ge(sig("plus_bias", u), so_far("plus_bias", k, u, pas, j) + 1)
                        old = biased[k]
                    if u.kind == "down0":
                        if ever("accepted", ATTN1, u):
                            dve.wait_ge(raised["accepted", ATTN1], so_far("accepted", ATTN1, u, pas, j))
                        dst = hand01[:]
                    if u.kind == "down2" and k == LOCAL0:
                        if ever("accepted", LOCAL1, u):
                            dve.wait_ge(raised["accepted", LOCAL1], so_far("accepted", LOCAL1, u, pas, j))
                        dst = hand23[:, 1]
                    dve.wait_ge(has_filled("dense", u), uses("dense", u, pas, j))
                    nc.vector.tensor_tensor(dst, tile("dense", u)[:, 0:SEQ].rearrange("p (t d) -> p t d", t=TT), old, ALU.add)\
                        .then_inc(has_emptied("dense", u), 1)
                    for sem, count in newest(pas, j, taken("dense", u, 0)):
                        dve.wait_ge(sem, count)
                    dve.sem_inc(sig("handed" if u.kind == "down0" else "resid", u), 1)
                elif u.kind == "qkv2" and u.part % 3 < 2:
                    t, m = u.part // 3, u.part % 3
                    dve.wait_ge(sig("sq_ready", u), so_far("sq_ready", k, u, pas, j) + 1)
                    nc.vector.reduce_sum(ss[:, l, t, m, :], two_in_P0[:, l, m, :].rearrange("p (h d) -> p h d", h=HEADS),
                                         AX.X).then_inc(sig("sums", u), 1)
                elif u.kind == "rope2":
                    t, m, n = u.part // 2, u.part % 2, u.part % 2
                    if u.part == 0:
                        dve.wait_ge(sig("sums", u), so_far("sums", k, u, pas, j))
                        flat = ss[:, l].rearrange("p t m h -> p (t m h)")
                        nc.vector.tensor_scalar(flat, flat, 1e-24, None, ALU.max).then_inc(sig("ss_ready", u), 1)
                    for sem, count in newest(pas, j, taken("dense", earlier(pas, u, "qkv2", 3 * t + m), 0)):
                        dve.wait_ge(sem, count)
                    if u.part >= 2:
                        dve.wait_ge(sig("rot_sum", u), so_far("rot_sum", k, u, pas, j) - 1)
                    raw = (q2, k2)[m][:, l, t, :].rearrange("p (h d) -> p h d", h=HEADS)
                    tab = rope2_sb[:, l, t, m, 1, :]
                    sn = two_in_P0[:, l, n, :].rearrange("p (h d) -> p h d", h=HEADS)
                    nc.vector.tensor_tensor(sn[:, :, 0:32], raw[:, :, 32:64],
                                            tab[:, 0:32].unsqueeze(1).broadcast_to([P, HEADS, 32]), ALU.mult)
                    nc.vector.tensor_tensor(sn[:, :, 32:64], raw[:, :, 0:32],
                                            tab[:, 32:64].unsqueeze(1).broadcast_to([P, HEADS, 32]), ALU.mult)\
                        .then_inc(sig("sin_part", u), 1)
                elif u.kind == "scale2":
                    t, m, n = u.part // 2, u.part % 2, u.part % 2
                    src = earlier(pas, u, "rope2", u.part)
                    dve.wait_ge(sig("rot_sum", src), so_far("rot_sum", k, src, pas, j) + 1)
                    dve.wait_ge(sig("rn_ready", u), so_far("rn_ready", k, u, pas, j))
                    nc.vector.tensor_tensor((q2, k2)[m][:, l, t, :].rearrange("p (h d) -> p h d", h=HEADS),
                                            cosine2[:, l, n, :].rearrange("p (h d) -> p h d", h=HEADS),
                                            rn[:, l, t, m, :].unsqueeze(2).broadcast_to([P, HEADS, HD]), ALU.mult)\
                        .then_inc(sig("rope_ready", u), 1)
                elif u.kind == "turn_k2":
                    dve.wait_ge(has_filled("dense", u), uses("dense", u, pas, j))
                    for e in range(2):
                        r = slice(64 * e, 64 * e + 64)
                        last = nc.vector.tensor_copy(kT2[r, l, 2 * u.part:2 * u.part + 2, e, :],
                                                     tile("dense", u)[r, :].rearrange("p (g q) -> p g q", g=2))
                    last.then_inc(has_emptied("dense", u), 1)
                elif u.kind == "scores2":
                    n = u.part
                    dve.wait_ge(has_filled("score", u), uses("score", u, pas, j))
                    if n == 0:
                        dst, src = negmax[:, k, 0, 0:8], tile("score", u)[:, :].rearrange("p (h k) -> p h k", h=8)
                    else:
                        dst = negmax[:, k, 1, 4 * (n - 1):4 * n]
                        src = tile("score", u)[:, :].rearrange("p (h k) -> p h k", h=4)[:, :, 0:SEQ - WINDOW]
                    nc.vector.reduce_max(dst, src, AX.X, negate=True).then_inc(sig("max_done", u), 1)
                elif u.kind == "norm2":
                    t = u.part
                    for sem, count in newest(pas, j, *(taken("score", earlier(pas, u, "scores2", n)) for n in ((0,), (1, 2))[t])):
                        dve.wait_ge(sem, count)
                    nc.vector.reciprocal(recip[:, k, t, 0:HEADS], expsum[:, l, t, :]).then_inc(sig("rec_done", u), 1)
                    dve.wait_ge(sig("rec_done", u), so_far("rec_done", k, u, pas, j) + 1)
                    part = P0[:, l] if t == 0 else P1[:, l, :, WINDOW:SEQ]
                    n = P if t == 0 else SEQ - WINDOW
                    nc.vector.tensor_tensor(part, part, recip[:, k, t, 0:HEADS].unsqueeze(2).broadcast_to([P, HEADS, n]),
                                            ALU.mult).then_inc(sig("p_ready", u), 1)
                elif u.kind == "up2":
                    for c, (at, n) in enumerate(HTILES):
                        dve.wait_ge(sig("gelu_done", u), so_far("gelu_done", k, u, pas, j) + c + 1)
                        nc.vector.scalar_tensor_tensor(up2T[0:n, l, c, :], tile("dense", u, c)[0:n, 0:SEQ], b1_2_sb[0:n, l, 0, c:c + 1],
                                                       gates[0:n, l, c, :], ALU.add, ALU.mult).then_inc(has_emptied("dense", u, c), 1)

            run(dve, unit)

        @block.tensor
        def _(pe):
            pe.wait_ge(loaded, ALL_LOADED)
            pe.wait_ge(setup_pool, PRESETS)
            pe.wait_ge(setup_act, 2)
            pe.wait_ge(setup_dve, RINGS["dense"])
            pe.wait_ge(staged, 4 * LAYERS)
            mm, turn = nc.tensor.matmul, nc.tensor.transpose

            def unit(u, pas, j):
                k, l = u.stream, u.stream - LOCAL0

                def of(kind, *parts, ring="dense", n=0):
                    return [taken(ring, earlier(pas, u, kind, part), n) for part in parts or (None,)]

                if u.kind in ("turn", "shift", "back"):
                    needs = [free("dense", u)]
                    if u.kind == "turn":
                        src = h[k]
                        if u.source == "att":
                            needs += of("attn_out", *range(TT))
                        else:
                            pe.wait_ge(sig("normed", u), so_far("normed", k, u, pas, j))
                    elif u.kind == "shift":
                        src = Y[l]
                        if u.part == 1:
                            pe.wait_ge(sig("resid", u), so_far("resid", k, u, pas, j))
                        elif k == LOCAL0:
                            pe.wait_ge(raised["normed", ATTN1], so_far("normed", ATTN1, u, pas, j))
                        else:
                            pe.wait_ge(sig("accepted", u), so_far("accepted", k, u, pas, j))
                    else:
                        needs += of("shift")
                        src = hS[:, l, 0:SEQ].rearrange("p (t q) -> p t q", t=TT)
                    for sem, count in newest(pas, j, *needs):
                        pe.wait_ge(sem, count)
                    for t in range(TT):
                        last = turn(tile("dense", u)[:, t * P:(t + 1) * P], src[:, t, :], ident)
                    last.then_inc(has_filled("dense", u), 1)
                elif u.kind == "qkv":
                    t = u.part
                    for sem, count in newest(pas, j, *of("turn"), free("dense", u)):
                        pe.wait_ge(sem, count)
                    mm(tile("dense", u)[:, 0:3 * DIM], hT[k][:, t * P:(t + 1) * P], wqkv_sb[:, k], start=True, stop=True)\
                        .then_inc(has_filled("dense", u), 1)
                elif u.kind in ("turn_q", "turn_k"):
                    src = QB if u.kind == "turn_q" else KB
                    needs = [free("dense", u)]
                    if k == ATTN0:
                        needs += of("qkv", *range(TT))
                    else:
                        pe.wait_ge(sig("lo_ready", u), so_far("lo_ready", k, u, pas, j))
                    if u.source == "with maxima":
                        pe.wait_ge(sig("m_ready", u), so_far("m_ready", k, u, pas, j))
                    for sem, count in newest(pas, j, *needs):
                        pe.wait_ge(sem, count)
                    for e in range(2):
                        g = 2 * u.part + e
                        for t in range(TT):
                            last = turn(tile("dense", u)[:, e * SEQ + t * P:e * SEQ + (t + 1) * P],
                                        src[:, k, t, 4 * g:4 * g + 4, :].rearrange("p h c -> p (h c)"), ident)
                    last.then_inc(has_filled("dense", u), 1)
                elif u.kind == "maxes":
                    for sem, count in newest(pas, j, *of("turn_q", 0, 1), *of("turn_k", 0, 1), free("score", u)):
                        pe.wait_ge(sem, count)
                    n = u.part
                    for e in range(2):
                        bank = tile("score", u)[:, e * 512:(e + 1) * 512]
                        if k == ATTN0:
                            t, g = n // 4, n % 4
                            last = mm(bank, qT[:, k, g, t * P:(t + 1) * P], kT[:, k, 4 * g + 2 * e:4 * g + 2 * e + 2, :],
                                      start=True, stop=True)
                        elif n < 2:
                            g = 2 * n + e
                            mm(bank, ident_r[:], causal.unsqueeze(1).broadcast_to([P, 4, P]), start=True, stop=False)
                            last = mm(bank, qT[:, k, g, 0:P], kT[:, k, 4 * g:4 * g + 4, 0:P], start=False, stop=True)
                        else:
                            g = n - 2
                            mm(bank, qT[:, k, g, P:SEQ], kT[:, k, 4 * g + 2 * e:4 * g + 2 * e + 2, :], start=True, stop=False,
                               skip_group_check=True)
                            last = mm(bank.rearrange("p (a k) -> p a k", a=2)[:, :, P:SEQ], ident_r[:],
                                      causal.unsqueeze(1).broadcast_to([P, 2, P]), start=False, stop=True, skip_group_check=True)
                    last.then_inc(has_filled("score", u), 1)
                elif u.kind == "scores":
                    g = u.part
                    for sem, count in newest(pas, j, *of("turn_q", 0, 1)):
                        pe.wait_ge(sem, count)
                    for t in range(TT):
                        for sem, count in newest(pas, j, free("score", u, t)):
                            pe.wait_ge(sem, count)
                        for n in range(4):
                            last = mm(tile("score", u, t)[:, n * SEQ:(n + 1) * SEQ], kT[:, k, 4 * g + n, t * P:(t + 1) * P],
                                      qT[:, k, g, :], start=True, stop=True)
                        last.then_inc(has_filled("score", u, t), 1)
                elif u.kind == "mix":
                    g = u.part
                    pe.wait_ge(sig("v_ready", u), so_far("v_ready", k, u, pas, j))
                    for sem, count in newest(pas, j, free("dense", u)):
                        pe.wait_ge(sem, count)
                    for t in range(TT):
                        if k == ATTN0:
                            for sem, count in newest(pas, j, *of("scores", g, ring="score", n=t)):
                                pe.wait_ge(sem, count)
                        else:
                            pe.wait_ge(sig("masked", u), so_far("masked", k, u, pas, j) + t - 1)
                        q0 = P if k == ATTN1 and t == 1 else 0
                        w = SEQ - q0
                        for n in range(4):
                            last = mm(tile("dense", u)[32 * n:32 * n + 16, q0:SEQ], V[:, k, t, 4 * g + n, :],
                                      probs[k][t][:, n * w:(n + 1) * w], start=t == 0, stop=t == 1)
                    last.then_inc(has_filled("dense", u), 1)
                elif u.kind == "attn_out":
                    t = u.part
                    for sem, count in newest(pas, j, *of("mix", *range(GROUPS)), free("dense", u)):
                        pe.wait_ge(sem, count)
                    for g in range(GROUPS):
                        last = turn(tile("dense", u)[:, g * P:(g + 1) * P], oT[:, k, g, t * P:(t + 1) * P], ident)
                    last.then_inc(has_filled("dense", u), 1)
                elif u.kind == "project1":
                    for sem, count in newest(pas, j, *of("turn"), free("dense", u)):
                        pe.wait_ge(sem, count)
                    for t in range(TT):
                        last = mm(tile("dense", u)[:, t * P:(t + 1) * P], hT[k][:, t * P:(t + 1) * P], wo1_sb[:], start=True, stop=True)
                    last.then_inc(has_filled("dense", u), 1)
                elif u.kind == "up0":
                    for sem, count in newest(pas, j, *of("turn"), free("dense", u)):
                        pe.wait_ge(sem, count)
                    for e in range(2):
                        c = 2 * u.part + e
                        last = mm(tile("dense", u)[:, e * SEQ:(e + 1) * SEQ], w1_0_sb[:, c * P:(c + 1) * P], hT[k],
                                  start=True, stop=True)
                    last.then_inc(has_filled("dense", u), 1)
                elif u.kind == "down0":
                    for sem, count in newest(pas, j, *of("up0", 0, 1), free("dense", u)):
                        pe.wait_ge(sem, count)
                    for t in range(TT):
                        for c in range(FF0 // P):
                            last = mm(tile("dense", u)[:, t * P:(t + 1) * P], up0T[:, c, t * P:(t + 1) * P], w2_0_sb[:, c, :],
                                      start=c == 0, stop=c == FF0 // P - 1)
                    last.then_inc(has_filled("dense", u), 1)
                elif u.kind == "qkv2":
                    t, m = u.part // 3, u.part % 3
                    for sem, count in newest(pas, j, *of("shift"), free("dense", u)):
                        pe.wait_ge(sem, count)
                    mm(tile("dense", u)[:], hS[:, l, t * P:(t + 1) * P], wqkv2_sb[:, l, m * INNER:(m + 1) * INNER],
                       start=True, stop=True).then_inc(has_filled("dense", u), 1)
                elif u.kind in ("turn_q2", "turn_k2"):
                    src = q2 if u.kind == "turn_q2" else k2
                    pe.wait_ge(sig("rope_ready", u), so_far("rope_ready", k, u, pas, j))
                    for sem, count in newest(pas, j, free("dense", u)):
                        pe.wait_ge(sem, count)
                    for e in range(2):
                        pr = 2 * u.part + e
                        for t in range(TT):
                            last = turn(tile("dense", u)[:, e * SEQ + t * P:e * SEQ + (t + 1) * P],
                                        src[:, l, t, pr * P:(pr + 1) * P], ident)
                    last.then_inc(has_filled("dense", u), 1)
                elif u.kind == "scores2":
                    for sem, count in newest(pas, j, *of("turn_q2", 0, 1), *of("turn_k2", 0, 1), free("score", u)):
                        pe.wait_ge(sem, count)
                    for e in range(2):
                        bank = tile("score", u)[:, e * 512:(e + 1) * 512]
                        if u.part == 0:
                            mm(bank, ident_r[:], band0.unsqueeze(1).broadcast_to([P, 4, P]), start=True, stop=False)
                            for pr in (2 * e, 2 * e + 1):
                                last = mm(bank[:, (pr - 2 * e) * SEQ:(pr - 2 * e + 1) * SEQ], qT2[:, l, pr, 0:P],
                                          kT2[:, l, pr, :, 0:P], start=False, stop=pr == 2 * e + 1)
                        else:
                            pr = 2 * (u.part - 1) + e
                            two = bank.rearrange("p (a k) -> p a k", a=2)[:, :, 0:SEQ - WINDOW]
                            mm(two, ident_r[:], band1.unsqueeze(1).broadcast_to([P, 2, SEQ - WINDOW]), start=True, stop=False)
                            last = mm(two, qT2[:, l, pr, P:SEQ], kT2[:, l, pr, :, WINDOW:SEQ], start=False, stop=True)
                    last.then_inc(has_filled("score", u), 1)
                elif u.kind == "turn_p":
                    pe.wait_ge(sig("p_ready", u), so_far("p_ready", k, u, pas, j))
                    for sem, count in newest(pas, j, free("score", u)):
                        pe.wait_ge(sem, count)
                    s = tile("score", u)
                    for e in range(2):
                        hd, at = 2 * u.part + e, 512 * e
                        turn(s[:, at:at + P], P0[:, l, hd, :], ident)
                        turn(s[:, at + P:at + P + WINDOW], P1[0:WINDOW, l, hd, 0:P], ident[0:WINDOW, 0:WINDOW])
                        last = turn(s[:, at + P + WINDOW:at + 2 * P + WINDOW], P1[:, l, hd, P:SEQ], ident)
                    last.then_inc(has_filled("score", u), 1)
                elif u.kind == "mix2":
                    n = u.part
                    for sem, count in newest(pas, j, *of("qkv2", 2, 5), *of("turn_p", n, ring="score"), free("dense", u)):
                        pe.wait_ge(sem, count)
                    for q0, w, t, c0 in ((0, P + WINDOW, 0, 0), (P, P, 1, P + WINDOW)):
                        for e in range(2):
                            hd = 2 * n + e
                            last = mm(tile("dense", u)[64 * e:64 * e + 64, q0:q0 + w], V2[:, l, t, hd * HD:(hd + 1) * HD],
                                      probs2[l][n % 2][:, e, c0:c0 + w], start=t == 0, stop=t == 1, skip_group_check=True)
                    last.then_inc(has_filled("dense", u), 1)
                elif u.kind == "project2":
                    for sem, count in newest(pas, j, *of("mix2", *range(PAIRS)), free("dense", u)):
                        pe.wait_ge(sem, count)
                    for t in range(TT):
                        for c in range(PAIRS):
                            last = mm(tile("dense", u)[:, t * P:(t + 1) * P], o2T[:, l, c, t * P:(t + 1) * P], wo2_sb[:, l, c, :],
                                      start=c == 0, stop=c == PAIRS - 1)
                    last.then_inc(has_filled("dense", u), 1)
                elif u.kind == "up2":
                    for c, (at, n) in enumerate(HTILES):
                        for sem, count in newest(pas, j, *(of("turn") if c == 0 else []), free("dense", u, c)):
                            pe.wait_ge(sem, count)
                        for half in range(2):
                            last = mm(tile("dense", u, c)[0:n, half * SEQ:(half + 1) * SEQ],
                                      w1_2_sb[:, l, half * HID + at:half * HID + at + n], hT[k], start=True, stop=True)
                        last.then_inc(has_filled("dense", u, c), 1)
                elif u.kind == "down2":
                    for sem, count in newest(pas, j, *(of("up2", n=c)[0] for c in range(3)), free("dense", u)):
                        pe.wait_ge(sem, count)
                    for t in range(TT):
                        for c, (at, n) in enumerate(HTILES):
                            last = mm(tile("dense", u)[:, t * P:(t + 1) * P], up2T[0:n, l, c, t * P:(t + 1) * P], w2_2_sb[0:n, l, c, :],
                                      start=c == 0, stop=c == 2)
                    last.then_inc(has_filled("dense", u), 1)

            run(pe, unit)


def tiles_on_columns(b):
    out = np.zeros((P, LAYERS, 2, len(HTILES)), b.dtype)
    for c, (at, n) in enumerate(HTILES):
        out[0:n, :, :, c] = b.reshape(LAYERS, 2, HID)[:, :, at:at + n].transpose(2, 0, 1)
    return out


def kernel(**inputs):
    import concourse.bacc as bacc
    from concourse.bass_utils import run_bass_kernel_spmd

    a = {k: np.asarray(v) for k, v in inputs.items()}
    arrays = {
        "x": a["L0_attn_x"],
        "wqkv0": np.concatenate([a["L0_attn_Wq"].T, a["L0_attn_Wk"].T, a["L0_attn_Wv"].T], axis=1),
        "w1_0": a["L0_ffn_w1"], "b1_0": a["L0_ffn_b1"].reshape(FF0 // P, P).T, "w2_0": a["L0_ffn_w2"], "b2_0": a["L0_ffn_b2"],
        "wqkv1": np.concatenate([a["L1_attn_wq"].T, a["L1_attn_wk"].T, a["L1_attn_wv"].T], axis=1),
        "wo1": a["L1_attn_wo"].T,
        "wqkv2": a["L1_ffn_wqkv"], "q_scale": a["L1_ffn_q_scale"], "k_scale": a["L1_ffn_k_scale"], "wo2": a["L1_ffn_wo"],
        "ln_g": a["L1_ffn_ln_g"].T, "ln_b": a["L1_ffn_ln_b"].T, "w1_2": a["L1_ffn_w1"], "b1_2": tiles_on_columns(a["L1_ffn_b1"]),
        "w2_2": a["L1_ffn_w2"], "b2_2": a["L1_ffn_b2"],
    }
    arrays.update(shape_constants())
    arrays = {k: np.ascontiguousarray(v) for k, v in arrays.items()}
    nc = bacc.Bacc("TRN2", target_bir_lowering=False, num_devices=1)
    args = [nc.dram_tensor(k, v.shape, mybir.dt.from_np(v.dtype), kind="ExternalInput").ap() for k, v in arrays.items()]
    args.append(nc.dram_tensor("out", (BATCH, SEQ, DIM), mybir.dt.float32, kind="ExternalOutput").ap())
    fused_block(nc, *args)
    r = run_bass_kernel_spmd(nc, [arrays], core_ids=[0])
    return r.results[0]["out"]
```

```python
import numpy as np
from contextlib import ExitStack

import concourse.bass as bass
from concourse import mybir

BATCH, SEQ, DIM = 32, 256, 128
STREAMS = 4
P = 128
TT = SEQ // P
H16, HD8 = 16, 8
GROUPS = H16 // 4
FF0 = 512
HEADS, HD, INNER = 8, 64, 512
PAIRS = HEADS // 2
WINDOW = 64
LAYERS = 2
HID = int(DIM * 4 * 2 / 3)
HTILES = [(0, 128), (128, 128), (256, HID - 256)]
EPS = 1e-5
NEG = -1e30
SCALE0 = 1.0 / float(np.sqrt(DIM))
SCALE1 = 1.0 / float(np.sqrt(HD8))


def shape_constants():
    f = np.float32
    tri = np.where(np.arange(P)[None, :] > np.arange(P)[:, None], f(NEG), f(0)).astype(f)
    i1 = P + np.arange(P)[:, None]
    j1 = WINDOW + np.arange(SEQ - WINDOW)[None, :]
    band = np.where((i1 < j1) | (i1 > j1 + WINDOW), f(NEG), f(0)).astype(f)
    masks = np.concatenate([tri, band], axis=1)
    t = np.arange(SEQ, dtype=f)
    freq1 = (f(1) / f(10000.0) ** (np.arange(0, HD8, 2, dtype=f) / f(HD8))).astype(f)
    ang1 = np.outer(t, freq1).astype(f)
    cos1 = np.repeat(np.cos(ang1), 2, axis=1)
    sin1 = np.stack([-np.sin(ang1), np.sin(ang1)], axis=-1).reshape(SEQ, HD8)
    rope1 = np.concatenate([cos1, sin1], axis=1).astype(f)
    half = np.arange(0, HD, 2, dtype=f)
    freq2 = (f(1) / f(10000.0) ** (half / f(HD))).astype(f)
    ang2 = (t[:, None] * freq2[None, :]).astype(f)
    base = (half + f(0.4 * HD)) / f(1.4 * HD)
    power = (t - SEQ // 2) / f(WINDOW // 2)
    scale = (base[None, :] ** power[:, None]).astype(f)
    cos2, sin2 = np.cos(ang2).astype(f), np.sin(ang2).astype(f)
    qk_scale = f(8.0)

    def table(c, s):
        return np.concatenate([c, c, -s, s], axis=1)

    rope2 = np.concatenate([table(cos2 * scale * qk_scale, sin2 * scale * qk_scale),
                            table(cos2 / scale, sin2 / scale)], axis=1).astype(f)
    return {"c_ident": np.eye(P, dtype=f), "c_masks": masks, "c_rope1": rope1, "c_rope2": rope2}


ATTN0, ATTN1, LOCAL0, LOCAL1 = range(STREAMS)
TAKES_UP = (0, 2, 3, 4)
BEGINS = (47, 48, 46, 30)
TURNS = {
    "tensor": (
        "11220233000320213133333110033031101123002322311112"
        "00223320022333111113330000111131131333332212011220"
        "02212201211300200031113000110000222222221100011102"
        "22203330223330322220023323300220111110000333233131"
        "013012200030"
    ),
    "scalar": (
        "11022200002231333133113003333101012001222111133323"
        "00223320220111113331111011000000131330333322002333"
        "00021131211001222222000003311111222322332000221111"
        "10222200333220322202223302233000111111000013331233"
        "003312200030"
    ),
    "vector": (
        "11022200002211003331133333311003331312003320220332"
        "22211112200331311133312223111111133322133322000022"
        "00003000002111000321100001232211131122320003220033"
        "30222112013233113322220220222111113332330000000122"
        "311031000030"
    ),
    "gpsimd": (
        "31130222232333131333300000003111111032020232003330"
        "01111000000003332001000111100000001111222113221330"
        "00133333332222222222222222211112202212222222222000"
        "00000000103111113333333333322331111133333111111311"
        "230122000030"
    ),
    "sync": (
        "11022200000033333333333220101311320011330013322210"
        "03332222111122111111111111333331000033333000111221"
        "21013222230022000000211100002311000202200223330222"
        "11133333311332222220022222222111113333300200000131"
        "131022000030"
    ),
}
RINGS = {"dense": 4, "score": 4}


class Unit:

    def __init__(self, kind, part=0, source=None, **counts):
        self.kind, self.part, self.source = kind, part, source
        self.uses = {r: counts.pop(r) for r in RINGS if r in counts}
        self.raises = counts
        self.at, self.buffers = {}, {}


def norm_units(source):
    return [Unit("stats", source=source, bn_done=2, moments=2, var_eps=1, rstd=1),
            Unit("apply", source=source, normed=1)]


def attention_units(rotary):
    units = [Unit("turn", source="h", dense=1)]
    extra = dict(rot_cos=1, rot_done=1, lo_ready=1) if rotary else {}
    units += [Unit("qkv", t, dense=1, v_ready=1, hi_ready=1, **extra) for t in range(TT)]
    units += [Unit("turn_q", u, dense=1) for u in range(2)]
    units += [Unit("turn_k", u, dense=1, k_in=4 * 16 * u) for u in range(2)]
    units += [Unit("maxes", u, score=1) for u in range(12 if rotary else 16)]
    units += [Unit("negmax", m_hi=1, m_ready=1)]
    units += [Unit("turn_q", u, source="with maxima", dense=1) for u in range(2)]
    for g in range(GROUPS):
        units += [Unit("scores", 4 * g + n, score=1, **(dict(masked=1) if rotary else {})) for n in range(2 * TT)]
        units += [Unit("mix", g, dense=1)]
    units += [Unit("attn_out", t, dense=1, rec_done=1) for t in range(TT)]
    return units


def local_units(last):
    units = [Unit("shift", dense=1)]
    units += [Unit("qkv2", n, dense=1, **(dict(sq_ready=1, sums=1) if n % 3 < 2 else {})) for n in range(6)]

    def rope(u):
        return Unit("rope2", u, cos_part=1, sin_part=1, rot_sum=1)

    def norms(t):
        return Unit("norms2", t, ss_ready=1, rn_ready=1)

    def scale(u):
        return Unit("scale2", u, rope_ready=1)

    units += [rope(0), norms(0), rope(1), scale(0), rope(2), norms(1), scale(1), rope(3), scale(2), scale(3)]
    units += [Unit("turn_q2", u, dense=1) for u in range(2)]
    units += [Unit("turn_k2", u, dense=1, k_in=2 * 16 * u) for u in range(2)]
    units += [Unit("scores2", u, score=1, max_done=1) for u in range(6)]
    units += [Unit("norm2", t, rec_done=1, p_ready=1) for t in range(TT)]

    def turn_p(u):
        return Unit("turn_p", u, score=1)

    def mix2(u):
        return Unit("mix2", u, dense=1)

    units += [turn_p(0), turn_p(1), turn_p(2), turn_p(3), mix2(0), turn_p(4), turn_p(5), mix2(1),
              turn_p(6), turn_p(7), mix2(2), mix2(3)]
    units += [Unit("project2", dense=1, resid=1)]
    units += [Unit("shift_rows", rows_in=2 * 16, rows_left=1)]
    units += norm_units("h")
    units += [Unit("turn", source="gained", dense=1)]
    units += [Unit("up2", c, dense=1, gelu_done=1) for c in range(len(HTILES))]
    units += [Unit("down2", dense=1, plus_bias=1, resid=1)]
    units += [Unit("finish", out_ready=1) if last else Unit("carry", carried=1)]
    return units


def stream_units(k):
    if k == ATTN0:
        units = norm_units("x") + attention_units(rotary=False)
        units += [Unit("residual", resid=1)] + norm_units("x")
        units += [Unit("turn", source="h", dense=1)] + [Unit("up0", u, dense=1) for u in range(2)]
        units += [Unit("down0", dense=1, plus_bias=1, handed=1)]
    elif k == ATTN1:
        units = [Unit("accept", accepted=1)] + norm_units("x") + attention_units(rotary=True)
        units += [Unit("turn", source="att", dense=1), Unit("project1", dense=1, resid=1)]
        units += norm_units("z") + [Unit("carry", carried=1)]
    else:
        units = ([Unit("accept", accepted=1)] if k == LOCAL1 else []) + local_units(last=k == LOCAL1)
    for n, u in enumerate(units):
        u.stream, u.number = k, n
        u.stage = TAKES_UP[k] + (1 if n >= BEGINS[k] > 0 else 0)
    return units


def merged_units(engine):
    queues = []
    for k in range(STREAMS):
        units = stream_units(k)
        queues.append(iter(units[BEGINS[k]:] + units[:BEGINS[k]]))
    return [next(queues[int(k)]) for k in TURNS[engine]]


class Pass:

    def __init__(self, first, times):
        self.first, self.times = first, times
        self.units = merged_units("tensor")
        position = {r: 0 for r in RINGS}
        for u in self.units:
            for r, n in u.uses.items():
                u.buffers[r] = [(position[r] + i) % RINGS[r] for i in range(n)]
                position[r] += n
        self.units = [u for u in self.units if 0 <= first - u.stage < BATCH]
        self.per, self.before = {}, None

    def ordered(self, engine):
        mine = {(u.stream, u.number): u for u in self.units}
        places = [(u.stream, u.number) for u in merged_units(engine)]
        return [mine[place] for place in places if place in mine]


def plan():
    last = max(u.stage for k in range(STREAMS) for u in stream_units(k))
    passes = [Pass(p, 1) for p in range(last + 1)]
    passes += [Pass(last + 1, BATCH - last - 2)]
    passes += [Pass(BATCH - 1 + p, 1) for p in range(last + 1)]
    count, before = {}, None
    for pas in passes:
        start = dict(count)
        pas.before, before = before, pas
        for u in pas.units:
            u.at = dict(count)
            for r, buffers in u.buffers.items():
                for i, b in enumerate(buffers):
                    count[r, b] = count.get((r, b), 0) + 1
                    buffers[i] = (b, count[r, b])
            for name, n in u.raises.items():
                count[name, u.stream] = count.get((name, u.stream), 0) + n
        pas.per = {c: n - start.get(c, 0) for c, n in count.items()}
        for c in count:
            count[c] += (pas.times - 1) * pas.per[c]
    return passes


def earlier(pas, u, kind, part=None):
    v = [v for v in stream_units(u.stream) if v.number < u.number and v.kind == kind and (part is None or v.part == part)][-1]
    ago = u.stage - v.stage
    assert ago in (0, 1)
    home = pas if ago == 0 or pas.times > 1 else pas.before
    found = [w for w in home.units if (w.stream, w.number) == (v.stream, v.number)][0]
    if ago == 0:
        return found
    rounds = -1 if home is pas else home.times - 1
    seen = Unit(kind, found.part)
    seen.stream, seen.number, seen.stage = found.stream, found.number, found.stage
    seen.at = {c: n + rounds * home.per.get(c, 0) for c, n in found.at.items()}
    seen.buffers = {r: [(b, n + rounds * home.per[r, b]) for b, n in found.buffers[r]] for r in found.buffers}
    return seen


def fused_block(nc, x, wqkv0, w1_0, b1_0, w2_0, b2_0, wqkv1, wo1, wqkv2, q_scale, k_scale, wo2,
                ln_g, ln_b, w1_2, b1_2, w2_2, b2_2, c_ident, c_masks, c_rope1, c_rope2, out):
    f32, f32r = mybir.dt.float32, mybir.dt.float32r
    ALU, ACT, AX = mybir.AluOpType, mybir.ActivationFunctionType, mybir.AxisListType

    x_rows = x.rearrange("b (t p) d -> b p t d", p=P)
    out_rows = out.rearrange("b (t p) d -> b p t d", p=P)

    with ExitStack() as ctx:
        def sb(name, shape, dt=f32):
            return ctx.enter_context(nc.sbuf_tensor(name, shape, dt))

        def pb(name, shape):
            return ctx.enter_context(nc.psum_tensor(name, shape, f32))

        def sem(name):
            return ctx.enter_context(nc.semaphore(name))

        ident_r = sb("ident_r", [P, P], f32r)
        ident = ident_r[:].bitcast(f32)
        masks = sb("masks", [P, P + SEQ - WINDOW], f32r)
        causal = masks[:, 0:P]
        band1 = masks[:, P:P + SEQ - WINDOW]
        band0 = masks[:, P + WINDOW:2 * P + WINDOW]
        wqkv_sb = sb("wqkv_sb", [P, 2, 3 * DIM])
        wo1_sb = sb("wo1_sb", [P, DIM])
        w1_0_sb = sb("w1_0_sb", [P, FF0])
        b1_0_sb = sb("b1_0_sb", [P, FF0 // P])
        w2_0_sb = sb("w2_0_sb", [P, FF0 // P, DIM])
        b2_0_sb = sb("b2_0_sb", [P, DIM])
        wqkv2_sb = sb("wqkv2_sb", [P, LAYERS, 3 * INNER])
        wo2_sb = sb("wo2_sb", [P, LAYERS, INNER // P, DIM])
        w1_2_sb = sb("w1_2_sb", [P, LAYERS, 2 * HID])
        b1_2_sb = sb("b1_2_sb", [P, LAYERS, 2, 3])
        w2_2_sb = sb("w2_2_sb", [P, LAYERS, 3, DIM])
        b2_2_sb = sb("b2_2_sb", [P, LAYERS, DIM])
        lng_sb = sb("lng_sb", [P, LAYERS])
        lnb_sb = sb("lnb_sb", [P, LAYERS])
        rope1_sb = sb("rope1_sb", [P, TT, 2, HD8])
        rope2_sb = sb("rope2_sb", [P, LAYERS, TT, 2, 2, HD])
        minus_half = sb("minus_half", [P, 2 * HEADS])
        eps_tile = sb("eps_tile", [P, TT])

        xin = sb("xin", [P, TT, DIM])
        xout = sb("xout", [P, TT, DIM])
        X1 = sb("X1", [P, TT, DIM])
        X2 = sb("X2", [P, TT, DIM])
        Y2 = sb("Y2", [P, TT, DIM])
        XY3 = sb("XY3", [P, 2, TT, DIM])
        hand01 = sb("hand01", [P, TT, DIM])
        hand23 = sb("hand23", [P, 2, TT, DIM])
        bn = sb("bn", [P, STREAMS, TT, 6])
        moments = sb("moments", [P, STREAMS, TT, 2])
        veps = sb("veps", [P, STREAMS, TT])
        rstd = sb("rstd", [P, STREAMS, TT])
        negmax = sb("negmax", [P, STREAMS, TT, H16])
        recip = sb("recip", [P, STREAMS, TT, H16])
        QB = sb("QB", [P, 2, TT, H16, 32])
        KB = sb("KB", [P, 2, TT, H16, 32])
        qT = sb("qT", [P, 2, GROUPS, SEQ], f32r)
        kT = sb("kT", [P, 2, H16, SEQ], f32r)
        V = sb("V", [P, 2, TT, H16, 16])
        rawC = sb("rawC", [P, 2, 1024])
        probs_in = sb("probs", [P, 3 * 1024 + 512])
        probs = [[probs_in[:, 0:1024], probs_in[:, 1024:2048]], [probs_in[:, 2048:3072], probs_in[:, 3072:3584]]]
        oT = rawC[:, :, :].rearrange("p a (g q) -> p a g q", g=GROUPS)
        up0T = rawC[:, ATTN0, :].rearrange("p (c q) -> p c q", c=FF0 // P)
        kS = rawC[:, :, :].rearrange("p a (u n) -> p a u n", u=2)
        cosine1 = rawC[:, ATTN1, 0:512].rearrange("p (t n) -> p t n", t=TT)
        sine1 = rawC[:, ATTN1, 512:1024].rearrange("p (t n) -> p t n", t=TT)
        hS = sb("hS", [P, 2, SEQ + 1])
        rawA = sb("rawA", [P, 2, 1024])
        rawB = sb("rawB", [P, 2, 1024])
        V2 = sb("V2", [P, 2, TT, INNER])
        rawQ = sb("rawQ", [P, 2, PAIRS * SEQ])
        qT2 = rawQ[:, :, :].rearrange("p l (c q) -> p l c q", c=PAIRS)
        kT2 = sb("kT2", [P, 2, PAIRS, 2, SEQ])
        rawP = sb("rawP", [P, 2, HEADS * P])
        P0 = rawP[:, :, :].rearrange("p l (h k) -> p l h k", h=HEADS)
        P1 = sb("P1", [P, 2, HEADS, SEQ])
        expsum = sb("expsum", [P, 2, TT, HEADS])
        ss = sb("ss", [P, 2, TT, 2, HEADS])
        rn = sb("rn", [P, 2, TT, 2, HEADS])
        q2 = rawA[:, :, 0:1024].rearrange("p l (t n) -> p l t n", t=TT)
        k2 = rawB[:, :, :].rearrange("p l (t n) -> p l t n", t=TT)
        probs2 = [[raw[:, l, 0:640].rearrange("p (e n) -> p e n", e=2) for raw in (rawA, rawQ)] for l in range(LAYERS)]
        o2T = rawB[:, :, :].rearrange("p l (c q) -> p l c q", c=PAIRS)
        up2T = rawA[:, :, 0:3 * SEQ].rearrange("p l (c q) -> p l c q", c=3)
        two_in_P0 = rawP[:, :, :].rearrange("p l (u n) -> p l u n", u=2)
        gates = rawP[:, :, :].rearrange("p l (c q) -> p l c q", c=4)
        cosine2 = rawQ[:, :, :].rearrange("p l (u n) -> p l u n", u=2)
        h = [probs[k][1][:, 0:TT * DIM].rearrange("p (t d) -> p t d", t=TT) for k in range(2)]\
            + [V2[:, l, 0, 0:TT * DIM].rearrange("p (t d) -> p t d", t=TT) for l in range(LAYERS)]
        hT = [probs[k][0][:, 0:SEQ] for k in range(2)] + [rawQ[:, l, 0:SEQ] for l in range(LAYERS)]
        X = [probs[ATTN0][0][:, 2 * SEQ:2 * SEQ + TT * DIM].rearrange("p (t d) -> p t d", t=TT), X1[:], X2[:], XY3[:, 0]]
        Y = [Y2[:], XY3[:, 1]]
        att = h
        biased = h
        ident_in = rawC[:, 0, 0:P]
        masks_in = rawA[:, 0, 0:P + SEQ - WINDOW]
        scales_in = rawB[:, 0, 0:2 * LAYERS * HD].rearrange("p (m l d) -> p m l d", m=2, l=LAYERS)
        rope2_in = rawB[:, 1, 0:TT * 4 * HD].rearrange("p (t m c d) -> p t m c d", t=TT, m=2, c=2)

        psum = {ring: [pb(f"{ring}{b}", [P, 512]) for b in range(n)] for ring, n in RINGS.items()}

        passes = plan()
        raised = {}
        for pas in passes:
            for u in pas.units:
                for name, n in u.raises.items():
                    if n and (name, u.stream) not in raised:
                        raised[name, u.stream] = sem(f"{name}_{u.stream}")
        full = {r: [sem(f"{r}{b}_full") for b in range(n)] for r, n in RINGS.items()}
        emptied = {r: [sem(f"{r}{b}_emptied") for b in range(n)] for r, n in RINGS.items()}
        loaded = sem("loaded")
        N_LOADS = [0]
        x_loaded, stored = sem("x_loaded"), sem("stored")
        setup_pool, setup_act, setup_dve = sem("setup_pool"), sem("setup_act"), sem("setup_dve")
        paced = sem("paced")
        staged = sem("staged")

        def sig(name, u):
            return raised[name, u.stream]

        def total(pas, j, c, count):
            return count + (j * pas.per.get(c, 0) if pas.times > 1 else 0)

        def so_far(name, k, u, pas, j):
            return total(pas, j, (name, k), u.at.get((name, k), 0))

        def ever(name, k, u):
            return u.at.get((name, k), 0) > 0

        def free(ring, u, n=0):
            b, count = u.buffers[ring][n]
            return (ring, b), count

        def taken(ring, u, n=0):
            b, count = u.buffers[ring][n]
            return (ring, b), count + 1

        def newest(pas, j, *counts):
            return [(emptied[c[0]][c[1]], total(pas, j, c, max(n for b, n in counts if b == c))) for c in dict(counts)]

        def uses(ring, u, pas, j, n=0):
            b, count = u.buffers[ring][n]
            return total(pas, j, (ring, b), count)

        def tile(ring, u, n=0):
            return psum[ring][u.buffers[ring][n][0]]

        def has_emptied(ring, u, n=0):
            return emptied[ring][u.buffers[ring][n][0]]

        def has_filled(ring, u, n=0):
            return full[ring][u.buffers[ring][n][0]]

        def run(eng, engine, unit):
            for pas in passes:
                if pas.times > 1:
                    with eng.Fori(0, pas.times) as j:
                        for u in pas.ordered(engine):
                            unit(u, pas, j)
                else:
                    for u in pas.ordered(engine):
                        unit(u, pas, 0)

        block = ctx.enter_context(nc.Block())

        @block.sync
        def _(sp):
            def load(dst, src):
                sp.dma_start(dst, src).then_inc(loaded, 16)
                N_LOADS[0] += 1

            sp.sem_inc(stored, 16)
            sp.dma_start(xin[:], x_rows[0]).then_inc(x_loaded, 16)
            load(ident_in, c_ident)
            load(masks_in, c_masks)
            load(wqkv_sb[:, 0], wqkv0)
            load(w1_0_sb[:], w1_0)
            load(b1_0_sb[:], b1_0)
            load(w2_0_sb[:], w2_0.rearrange("(c p) d -> p c d", p=P))
            load(b2_0_sb[:], b2_0.partition_broadcast(P))
            load(wqkv_sb[:, 1], wqkv1)
            load(wo1_sb[:], wo1)
            load(rope1_sb[:], c_rope1.rearrange("(t p) (c d) -> p t c d", p=P, c=2))
            load(rope2_in, c_rope2.rearrange("(t p) (m c d) -> p t m c d", p=P, m=2, c=2))
            load(wqkv2_sb[:], wqkv2.rearrange("l k n -> k l n"))
            load(lng_sb[:], ln_g)
            load(lnb_sb[:], ln_b)
            load(b1_2_sb[:], b1_2)
            load(w1_2_sb[:], w1_2.rearrange("l k n -> k l n"))
            for l in range(LAYERS):
                load(scales_in[:, 0, l, :], q_scale[l].partition_broadcast(P))
                load(scales_in[:, 1, l, :], k_scale[l].partition_broadcast(P))
                load(b2_2_sb[:, l, :], b2_2[l].partition_broadcast(P))
                load(wo2_sb[:, l], wo2[l].rearrange("(c p) d -> p c d", p=P))
                for c, (at, n) in enumerate(HTILES):
                    load(w2_2_sb[0:n, l, c, :], w2_2[l, at:at + n, :])

            def unit(u, pas, j):
                k, l = u.stream, u.stream - LOCAL0
                sequence = pas.first - u.stage + j
                if u.kind == "residual" and (pas.times > 1 or sequence + 1 < BATCH):
                    sp.wait_ge(sig("resid", u), so_far("resid", k, u, pas, j) + 1)
                    sp.sem_inc(paced, 1)
                    sp.dma_start(xin[:], x_rows[sequence + 1]).then_inc(x_loaded, 16)
                elif u.kind == "turn_k" and u.part == 1:
                    for sem, count in newest(pas, j, taken("dense", earlier(pas, u, "turn_k", 0)), taken("dense", u)):
                        sp.wait_ge(sem, count)
                        sp.sem_inc(paced, 1)
                    heads = kT[:, k].bitcast(f32).rearrange("p (g j) q -> p j g q", j=4)
                    for n in range(4):
                        q = slice(32 * n, 32 * n + 32)
                        sp.dma_start(heads[q, n], kS[q, k].rearrange("p u (g q) -> p (u g) q", g=2)).then_inc(sig("k_in", u), 16)
                elif u.kind == "turn_k2" and u.part == 1:
                    for sem, count in newest(pas, j, taken("dense", earlier(pas, u, "turn_k2", 0)), taken("dense", u)):
                        sp.wait_ge(sem, count)
                        sp.sem_inc(paced, 1)
                    for e in range(2):
                        half = slice(64 * e, 64 * e + 64)
                        sp.dma_start(kT2[half, l, :, e, :], two_in_P0[half, l].rearrange("p u (g q) -> p (u g) q", g=2))\
                            .then_inc(sig("k_in", u), 16)
                elif u.kind == "shift_rows":
                    sp.wait_ge(sig("resid", u), so_far("resid", k, u, pas, j))
                    sp.sem_inc(paced, 1)
                    sp.dma_start(h[k][1:P, :, 64:DIM], Y[l][0:P - 1, :, 64:DIM]).then_inc(sig("rows_in", u), 16)
                    sp.dma_start(h[k][0:1, 1, 64:DIM], Y[l][P - 1:P, 0, 64:DIM]).then_inc(sig("rows_in", u), 16)
                elif u.kind == "finish":
                    sp.wait_ge(sig("out_ready", u), so_far("out_ready", k, u, pas, j) + 1)
                    sp.sem_inc(paced, 1)
                    sp.dma_start(out_rows[sequence], xout[:]).then_inc(stored, 16)

            run(sp, "sync", unit)
            sp.wait_ge(stored, 16 * BATCH + 16)

        ALL_LOADED = 16 * N_LOADS[0]
        PRESETS, CLEARED = 9, RINGS["dense"] + 2

        @block.gpsimd
        def _(pool):
            nc.gpsimd.memset(minus_half[:], -0.5).then_inc(setup_pool, 1)
            nc.gpsimd.memset(eps_tile[:], EPS).then_inc(setup_pool, 1)
            nc.gpsimd.memset(V[:], 0.0).then_inc(setup_pool, 1)
            nc.gpsimd.memset(QB[:], 0.0).then_inc(setup_pool, 1)
            nc.gpsimd.memset(KB[:], 0.0).then_inc(setup_pool, 1)
            nc.gpsimd.memset(P1[:], 0.0).then_inc(setup_pool, 1)
            nc.gpsimd.memset(hS[:], 0.0).then_inc(setup_pool, 1)
            pool.wait_ge(setup_pool, PRESETS - 2)
            nc.gpsimd.memset(V[:, :, :, :, HD8:HD8 + 1], 1.0).then_inc(setup_pool, 1)
            nc.gpsimd.memset(KB[:, :, :, :, 24:26], 1.0).then_inc(setup_pool, 1)
            for r, n in RINGS.items():
                for b in range(n):
                    pool.sem_inc(emptied[r][b], 1)
            pool.wait_ge(loaded, ALL_LOADED)
            pool.wait_ge(setup_pool, PRESETS)

            def unit(u, pas, j):
                k, l = u.stream, u.stream - LOCAL0
                if u.kind == "stats":
                    pool.wait_ge(sig("moments", u), so_far("moments", k, u, pas, j) + 2)
                    nc.gpsimd.tensor_tensor(veps[:, k, :], moments[:, k, :, 1], eps_tile[:], ALU.add)\
                        .then_inc(sig("var_eps", u), 1)
                    pool.wait_ge(sig("var_eps", u), so_far("var_eps", k, u, pas, j) + 1)
                    nc.gpsimd.tensor_tensor(rstd[:, k, :], veps[:, k, :], minus_half[:, 0:TT], ALU.pow)\
                        .then_inc(sig("rstd", u), 1)
                elif u.kind == "qkv" and k == ATTN1:
                    t = u.part
                    for sem, count in newest(pas, j, taken("dense", u, 0)):
                        pool.wait_ge(sem, count)
                    nc.gpsimd.tensor_tensor(cosine1[:, t], cosine1[:, t], sine1[:, t], ALU.add)\
                        .then_inc(sig("rot_done", u), 1)
                elif u.kind == "scores" and k == ATTN1:
                    t, e = u.part % 4 // 2, u.part % 2
                    for sem, count in newest(pas, j, taken("score", u)):
                        pool.wait_ge(sem, count)
                    pool.sem_inc(paced, 1)
                    w = SEQ if t == 0 else P
                    part = probs[k][t][:, 2 * e * w:2 * (e + 1) * w].rearrange("p (j q) -> p j q", j=2)[:, :, 0:P]
                    nc.gpsimd.affine_select(out=part, in_=part, compare_op=ALU.is_ge, fill=0.0, base=0,
                                            pattern=[[0, 2], [1, P]], channel_multiplier=-1)\
                        .then_inc(sig("masked", u), 1)
                elif u.kind in ("down0", "down2"):
                    pool.wait_ge(sig("resid", u), so_far("resid", k, u, pas, j))
                    for sem, count in newest(pas, j, taken("dense", earlier(pas, u, "turn"), 0)):
                        pool.wait_ge(sem, count)
                    old, bias = (X[k], b2_0_sb[:]) if u.kind == "down0" else (Y[l], b2_2_sb[:, l])
                    nc.gpsimd.tensor_tensor(biased[k], old, bias.unsqueeze(1).broadcast_to([P, TT, DIM]), ALU.add)\
                        .then_inc(sig("plus_bias", u), 1)
                elif u.kind == "rope2":
                    t, m, n = u.part // 2, u.part % 2, u.part % 2
                    raw = (q2, k2)[m][:, l, t, :].rearrange("p (h d) -> p h d", h=HEADS)
                    tab = rope2_sb[:, l, t, m, 0, :].unsqueeze(1).broadcast_to([P, HEADS, HD])
                    cos = cosine2[:, l, n, :].rearrange("p (h d) -> p h d", h=HEADS)
                    for sem, count in newest(pas, j, taken("dense", earlier(pas, u, "qkv2", 3 * t + m), 0)):
                        pool.wait_ge(sem, count)
                    if u.part >= 2:
                        pool.wait_ge(sig("rope_ready", u), so_far("rope_ready", k, u, pas, j))
                    nc.gpsimd.tensor_tensor(cos, raw, tab, ALU.mult).then_inc(sig("cos_part", u), 1)
                    pool.wait_ge(sig("cos_part", u), so_far("cos_part", k, u, pas, j) + 1)
                    pool.wait_ge(sig("sin_part", u), so_far("sin_part", k, u, pas, j) + 1)
                    nc.gpsimd.tensor_tensor(cosine2[:, l, n, :], cosine2[:, l, n, :], two_in_P0[:, l, n, :], ALU.add)\
                        .then_inc(sig("rot_sum", u), 1)
                elif u.kind == "norms2":
                    t = u.part
                    pool.wait_ge(sig("ss_ready", u), so_far("ss_ready", k, u, pas, j) + 1)
                    nc.gpsimd.tensor_tensor(rn[:, l, t].rearrange("p m h -> p (m h)"), ss[:, l, t].rearrange("p m h -> p (m h)"),
                                            minus_half[:], ALU.pow).then_inc(sig("rn_ready", u), 1)
                elif u.kind == "finish":
                    pool.wait_ge(sig("resid", u), so_far("resid", k, u, pas, j))
                    pool.wait_ge(stored, total(pas, j, ("out_ready", k), 16 * (u.at.get(("out_ready", k), 0) + 1))
                                 if pas.times == 1 else j * 16 + 16 * (u.at.get(("out_ready", k), 0) + 1))
                    nc.gpsimd.tensor_tensor(xout[:], X[k], Y[l], ALU.add).then_inc(sig("out_ready", u), 1)

            run(pool, "gpsimd", unit)

        @block.scalar
        def _(act):
            act.wait_ge(loaded, ALL_LOADED)
            nc.scalar.activation(ident_r[:], ident_in, ACT.Copy).then_inc(setup_act, 1)
            nc.scalar.activation(masks[:], masks_in, ACT.Copy).then_inc(setup_act, 1)
            act.wait_ge(setup_pool, PRESETS)

            def unit(u, pas, j):
                k, l = u.stream, u.stream - LOCAL0
                if u.kind == "turn":
                    act.wait_ge(has_filled("dense", u), uses("dense", u, pas, j))
                    src = tile("dense", u)[:, 0:SEQ]
                    if u.source == "gained":
                        nc.scalar.activation(hT[k], src, ACT.Identity, bias=lnb_sb[:, l:l + 1], scale=lng_sb[:, l:l + 1])\
                            .then_inc(has_emptied("dense", u), 1)
                    else:
                        nc.scalar.activation(hT[k], src, ACT.Copy).then_inc(has_emptied("dense", u), 1)
                elif u.kind == "shift":
                    act.wait_ge(has_filled("dense", u), uses("dense", u, pas, j))
                    src = tile("dense", u)
                    nc.scalar.activation(hS[0:64, l, 0:SEQ], src[0:64, 0:SEQ], ACT.Copy)
                    nc.scalar.activation(hS[64:128, l, 1:SEQ + 1], src[64:128, 0:SEQ], ACT.Copy)\
                        .then_inc(has_emptied("dense", u), 1)
                elif u.kind == "qkv":
                    t = u.part
                    src = tile("dense", u)
                    act.wait_ge(has_filled("dense", u), uses("dense", u, pas, j))
                    nc.scalar.activation(V[:, k, t, :, 0:HD8], src[:, 2 * DIM:3 * DIM].rearrange("p (h d) -> p h d", h=H16),
                                         ACT.Copy).then_inc(sig("v_ready", u), 1)
                    qk = src[:, 0:2 * DIM]
                    if k == ATTN1:
                        act.wait_ge(sig("rot_done", u), so_far("rot_done", k, u, pas, j) + 1)
                        qk = cosine1[:, t]
                    q, kk = (qk[:, m * DIM:(m + 1) * DIM].rearrange("p (h d) -> p h d", h=H16).unsqueeze(2)
                             .broadcast_to([P, H16, 2, HD8]) for m in range(2))
                    nc.scalar.activation(QB[:, k, t, :, 0:16].bitcast(f32r).rearrange("p h (a d) -> p h a d", a=2), q, ACT.Copy)
                    last = nc.scalar.activation(KB[:, k, t, :, :].bitcast(f32r).rearrange("p h (a d) -> p h a d", a=2)[:, :, :, 0:HD8],
                                                kk, ACT.Copy)
                    last.then_inc(sig("hi_ready", u), 1)
                elif u.kind in ("turn_q", "turn_q2"):
                    act.wait_ge(has_filled("dense", u), uses("dense", u, pas, j))
                    dst = qT[:, k] if u.kind == "turn_q" else qT2[:, l]
                    nc.scalar.activation(dst[:, 2 * u.part:2 * u.part + 2, :].rearrange("p g q -> p (g q)"), tile("dense", u)[:],
                                         ACT.Copy).then_inc(has_emptied("dense", u), 1)
                elif u.kind in ("turn_k", "turn_k2"):
                    act.wait_ge(has_filled("dense", u), uses("dense", u, pas, j))
                    dst = kS[:, k, u.part].bitcast(f32r) if u.kind == "turn_k" else two_in_P0[:, l, u.part, :]
                    nc.scalar.activation(dst, tile("dense", u)[:], ACT.Copy).then_inc(has_emptied("dense", u), 1)
                elif u.kind == "scores":
                    t, e = u.part % 4 // 2, u.part % 2
                    act.wait_ge(has_filled("score", u), uses("score", u, pas, j))
                    src, w = tile("score", u)[:], 2 * SEQ
                    if k == ATTN1 and t == 1:
                        src, w = src.rearrange("p (j q) -> p j q", j=2)[:, :, P:SEQ], SEQ
                    dst = probs[k][t][:, e * w:(e + 1) * w]
                    if k == ATTN1 and t == 1:
                        dst = dst.rearrange("p (j q) -> p j q", j=2)
                    nc.scalar.activation(dst, src, ACT.Exp, scale=SCALE0 if k == ATTN0 else SCALE1)\
                        .then_inc(has_emptied("score", u), 1)
                elif u.kind == "up0":
                    act.wait_ge(has_filled("dense", u), uses("dense", u, pas, j))
                    for e in range(2):
                        c = 2 * u.part + e
                        last = nc.scalar.activation(up0T[:, c, :], tile("dense", u)[:, e * SEQ:(e + 1) * SEQ], ACT.Relu,
                                                    bias=b1_0_sb[:, c:c + 1])
                    last.then_inc(has_emptied("dense", u), 1)
                elif u.kind == "qkv2":
                    t, m = u.part // 3, u.part % 3
                    act.wait_ge(has_filled("dense", u), uses("dense", u, pas, j))
                    if m < 2:
                        if t == 1:
                            act.wait_ge(sig("sums", u), so_far("sums", k, u, pas, j) - 1)
                        nc.scalar.activation(two_in_P0[:, l, m, :], tile("dense", u)[:], ACT.Square).then_inc(sig("sq_ready", u), 1)
                    dst = (q2, k2, V2)[m]
                    nc.scalar.activation(dst[:, l, t, :], tile("dense", u)[:], ACT.Copy).then_inc(has_emptied("dense", u), 1)
                elif u.kind == "scores2":
                    n, e = u.part // 2, u.part % 2
                    t, nh = (0, 4) if n == 0 else (1, 2)
                    act.wait_ge(sig("max_done", u), so_far("max_done", k, u, pas, j) + 1)
                    bank = tile("score", u)
                    for i in range(nh):
                        if n == 0:
                            hd = 4 * e + i
                            dst, src = P0[:, l, hd, :], bank[:, i * P:(i + 1) * P]
                        else:
                            hd = 4 * (n - 1) + 2 * e + i
                            dst, src = P1[:, l, hd, WINDOW:SEQ], bank[:, i * SEQ:i * SEQ + SEQ - WINDOW]
                        last = nc.scalar.activation(dst, src, ACT.Exp, bias=negmax[:, k, t, hd:hd + 1],
                                                    accum_out=expsum[:, l, t, hd:hd + 1])
                    last.then_inc(has_emptied("score", u), 1)
                elif u.kind == "turn_p":
                    act.wait_ge(has_filled("score", u), uses("score", u, pas, j))
                    nc.scalar.activation(probs2[l][u.part // 2 % 2][:, u.part % 2, :], tile("score", u)[:, 0:320], ACT.Copy)\
                        .then_inc(has_emptied("score", u), 1)
                elif u.kind == "up2":
                    c, n = u.part, HTILES[u.part][1]
                    act.wait_ge(has_filled("dense", u), uses("dense", u, pas, j))
                    nc.scalar.activation(gates[0:n, l, c, :], tile("dense", u)[0:n, SEQ:2 * SEQ], ACT.Gelu,
                                         bias=b1_2_sb[0:n, l, 1, c:c + 1]).then_inc(sig("gelu_done", u), 1)
                elif u.kind == "carry":
                    if k == LOCAL0:
                        if ever("accepted", LOCAL1, u):
                            act.wait_ge(raised["accepted", LOCAL1], so_far("accepted", LOCAL1, u, pas, j))
                    else:
                        if ever("carried", LOCAL0, u):
                            act.wait_ge(raised["carried", LOCAL0], so_far("carried", LOCAL0, u, pas, j))
                        act.wait_ge(sig("resid", u), so_far("resid", k, u, pas, j))
                    nc.scalar.activation(X[LOCAL0] if k == ATTN1 else hand23[:, 0], X[k], ACT.Copy).then_inc(sig("carried", u), 1)
                elif u.kind == "accept":
                    if k == ATTN1:
                        act.wait_ge(raised["handed", ATTN0], so_far("handed", ATTN0, u, pas, j))
                        if ever("normed", k, u):
                            act.wait_ge(sig("normed", u), so_far("normed", k, u, pas, j))
                            act.wait_ge(sig("carried", u), so_far("carried", k, u, pas, j))
                        nc.scalar.activation(X1[:], hand01[:], ACT.Copy).then_inc(sig("accepted", u), 1)
                    else:
                        act.wait_ge(raised["resid", LOCAL0], so_far("resid", LOCAL0, u, pas, j))
                        act.wait_ge(raised["carried", LOCAL0], so_far("carried", LOCAL0, u, pas, j))
                        if ever("out_ready", k, u):
                            act.wait_ge(sig("out_ready", u), so_far("out_ready", k, u, pas, j))
                        nc.scalar.activation(XY3[:], hand23[:], ACT.Copy).then_inc(sig("accepted", u), 1)

            run(act, "scalar", unit)

        @block.vector
        def _(dve):
            nc.vector.memset(kT[:].bitcast(f32), 0.0).then_inc(setup_dve, 1)
            nc.vector.memset(kT2[:], 0.0).then_inc(setup_dve, 1)
            for t in psum["dense"]:
                nc.vector.memset(t[:], 0.0).then_inc(setup_dve, 1)
            dve.wait_ge(loaded, ALL_LOADED)
            dve.wait_ge(setup_pool, PRESETS)
            for l in range(LAYERS):
                for t in range(TT):
                    for m in range(2):
                        sc = scales_in[:, m, l, :]
                        nc.vector.tensor_tensor(rope2_sb[:, l, t, m, 0, :], rope2_in[:, t, m, 0, :], sc, ALU.mult)
                        nc.vector.tensor_tensor(rope2_sb[:, l, t, m, 1, 0:32], rope2_in[:, t, m, 1, 0:32], sc[:, 32:64], ALU.mult)
                        nc.vector.tensor_tensor(rope2_sb[:, l, t, m, 1, 32:64], rope2_in[:, t, m, 1, 32:64], sc[:, 0:32], ALU.mult)\
                            .then_inc(staged, 1)
            dve.wait_ge(staged, 4 * LAYERS)
            dve.wait_ge(setup_act, 2)

            def unit(u, pas, j):
                k, l = u.stream, u.stream - LOCAL0
                first = u.number < 3
                if u.kind in ("stats", "apply"):
                    rows = xin[:] if k == ATTN0 and first else h[k] if u.source == "h" else X[k]
                if u.kind == "stats":
                    if k == ATTN0 and first:
                        n = 16 * (pas.first + 1)
                        dve.wait_ge(x_loaded, n + j * 16 if pas.times > 1 else n)
                    elif k == ATTN1 and first:
                        dve.wait_ge(sig("accepted", u), so_far("accepted", k, u, pas, j))
                    elif u.source == "h":
                        dve.wait_ge(sig("rows_in", u), so_far("rows_in", k, u, pas, j))
                        dve.wait_ge(sig("rows_left", u), so_far("rows_left", k, u, pas, j))
                    else:
                        dve.wait_ge(sig("resid", u), so_far("resid", k, u, pas, j))
                    for t in range(TT):
                        nc.vector.bn_stats(bn[:, k, t, :], rows[:, t, :]).then_inc(sig("bn_done", u), 1)
                    for t in range(TT):
                        dve.wait_ge(sig("bn_done", u), so_far("bn_done", k, u, pas, j) + t + 1)
                        dve.sem_inc(paced, 1)
                        nc.vector.bn_aggr(moments[:, k, t, :], bn[:, k, t, :]).then_inc(sig("moments", u), 1)
                elif u.kind == "shift_rows":
                    dve.wait_ge(sig("resid", u), so_far("resid", k, u, pas, j))
                    nc.vector.tensor_copy(h[k][:, :, 0:64], Y[l][:, :, 0:64])
                    nc.vector.memset(h[k][0:1, 0, 64:DIM], 0.0).then_inc(sig("rows_left", u), 1)
                elif u.kind == "apply":
                    dve.wait_ge(sig("rstd", u), so_far("rstd", k, u, pas, j))
                    dst = h[k]
                    if u.source == "z":
                        if ever("resid", LOCAL0, u):
                            dve.wait_ge(raised["resid", LOCAL0], so_far("resid", LOCAL0, u, pas, j))
                        dst = Y[0]
                    for t in range(TT):
                        last = nc.vector.tensor_scalar(dst[:, t, :], rows[:, t, :], moments[:, k, t, 0:1], rstd[:, k, t:t + 1],
                                                       ALU.subtract, ALU.mult)
                    last.then_inc(sig("normed", u), 1)
                elif u.kind == "qkv":
                    t, s = u.part, tile("dense", u)
                    dve.wait_ge(has_filled("dense", u), uses("dense", u, pas, j))
                    nc.vector.memset(QB[:, k, t, :, 24:26], 0.0)
                    qk = s[:, 0:2 * DIM]
                    if k == ATTN1:
                        dve.wait_ge(sig("v_ready", u), so_far("v_ready", k, u, pas, j) + 1)
                        cos = rope1_sb[:, t, 0, :].unsqueeze(1).broadcast_to([P, 2 * H16, HD8])
                        nc.vector.tensor_tensor(cosine1[:, t].rearrange("p (h d) -> p h d", d=HD8),
                                                qk.rearrange("p (h d) -> p h d", d=HD8), cos, ALU.mult).then_inc(sig("rot_cos", u), 1)
                        sn = sine1[:, t].rearrange("p (h d e) -> p h d e", d=HD8 // 2, e=2)
                        sw = qk.rearrange("p (h d e) -> p h d e", d=HD8 // 2, e=2)
                        tab = rope1_sb[:, t, 1, :].rearrange("p (d e) -> p d e", e=2)
                        for e in range(2):
                            last = nc.vector.tensor_tensor(sn[:, :, :, e], sw[:, :, :, 1 - e],
                                                           tab[:, :, e].unsqueeze(1).broadcast_to([P, 2 * H16, HD8 // 2]), ALU.mult)
                        last.then_inc(has_emptied("dense", u), 1)
                        qk = cosine1[:, t]
                    dve.wait_ge(sig("hi_ready", u), so_far("hi_ready", k, u, pas, j) + 1)
                    q, kk = (qk[:, m * DIM:(m + 1) * DIM].rearrange("p (h d) -> p h d", h=H16) for m in range(2))
                    nc.vector.tensor_tensor(QB[:, k, t, :, 16:24].bitcast(f32r), q, QB[:, k, t, :, 0:8], ALU.subtract)
                    nc.vector.tensor_tensor(KB[:, k, t, :, 8:16].bitcast(f32r), kk, KB[:, k, t, :, 0:8], ALU.subtract)\
                        .then_inc(has_emptied("dense", u) if k == ATTN0 else sig("lo_ready", u), 1)
                elif u.kind == "maxes":
                    n, e = u.part // 2, u.part % 2
                    if k == ATTN0:
                        t, h0, nh = n // 4, 4 * (n % 4) + 2 * e, 2
                    elif n < 2:
                        t, h0, nh = 0, 8 * n + 4 * e, 4
                    else:
                        t, h0, nh = 1, 4 * (n - 2) + 2 * e, 2
                    dve.wait_ge(has_filled("score", u), uses("score", u, pas, j))
                    nc.vector.reduce_max(negmax[:, k, t, h0:h0 + nh], tile("score", u)[:, :].rearrange("p (h k) -> p h k", h=nh),
                                         AX.X, negate=True).then_inc(has_emptied("score", u), 1)
                elif u.kind == "negmax":
                    for sem, count in newest(pas, j, *(taken("score", earlier(pas, u, "maxes", n)) for n in range(12 if k == ATTN1 else 16))):
                        dve.wait_ge(sem, count)
                    neg = negmax[:, k].rearrange("p t h -> p (t h)")
                    place = QB[:, k].rearrange("p t h c -> p (t h) c")
                    nc.vector.tensor_copy(place[:, :, 24].bitcast(f32r), neg).then_inc(sig("m_hi", u), 1)
                    dve.wait_ge(sig("m_hi", u), so_far("m_hi", k, u, pas, j) + 1)
                    nc.vector.tensor_tensor(place[:, :, 25].bitcast(f32r), neg, place[:, :, 24], ALU.subtract)\
                        .then_inc(sig("m_ready", u), 1)
                elif u.kind in ("mix", "mix2"):
                    dve.wait_ge(has_filled("dense", u), uses("dense", u, pas, j))
                    dst = oT[:, k, u.part, :] if u.kind == "mix" else o2T[:, l, u.part, :]
                    nc.vector.tensor_copy(dst, tile("dense", u)[:, 0:SEQ]).then_inc(has_emptied("dense", u), 1)
                elif u.kind == "attn_out":
                    t = u.part
                    dve.wait_ge(has_filled("dense", u), uses("dense", u, pas, j))
                    heads = tile("dense", u)[:, :].rearrange("p (h c) -> p h c", c=32)
                    nc.vector.reciprocal(recip[:, k, t, :], heads[:, :, HD8]).then_inc(sig("rec_done", u), 1)
                    dve.wait_ge(sig("rec_done", u), so_far("rec_done", k, u, pas, j) + 1)
                    nc.vector.tensor_tensor(att[k][:, t, :].rearrange("p (h d) -> p h d", h=H16), heads[:, :, 0:HD8],
                                            recip[:, k, t, :].unsqueeze(2).broadcast_to([P, H16, HD8]), ALU.mult)\
                        .then_inc(has_emptied("dense", u), 1)
                elif u.kind == "residual":
                    for sem, count in newest(pas, j, *(taken("dense", earlier(pas, u, "attn_out", t)) for t in range(TT))):
                        dve.wait_ge(sem, count)
                    nc.vector.tensor_tensor(X[k], xin[:], att[k], ALU.add).then_inc(sig("resid", u), 1)
                elif u.kind in ("project1", "project2", "down0", "down2"):
                    dst = old = X[k] if u.kind == "project1" else Y[l]
                    if u.kind in ("down0", "down2"):
                        dve.wait_ge(sig("plus_bias", u), so_far("plus_bias", k, u, pas, j) + 1)
                        old = biased[k]
                    if u.kind == "down0":
                        if ever("accepted", ATTN1, u):
                            dve.wait_ge(raised["accepted", ATTN1], so_far("accepted", ATTN1, u, pas, j))
                        dst = hand01[:]
                    if u.kind == "down2" and k == LOCAL0:
                        if ever("accepted", LOCAL1, u):
                            dve.wait_ge(raised["accepted", LOCAL1], so_far("accepted", LOCAL1, u, pas, j))
                        dst = hand23[:, 1]
                    dve.wait_ge(has_filled("dense", u), uses("dense", u, pas, j))
                    nc.vector.tensor_tensor(dst, tile("dense", u)[:, 0:SEQ].rearrange("p (t d) -> p t d", t=TT), old, ALU.add)\
                        .then_inc(has_emptied("dense", u), 1)
                    for sem, count in newest(pas, j, taken("dense", u, 0)):
                        dve.wait_ge(sem, count)
                    dve.sem_inc(sig("handed" if u.kind == "down0" else "resid", u), 1)
                elif u.kind == "qkv2" and u.part % 3 < 2:
                    t, m = u.part // 3, u.part % 3
                    dve.wait_ge(sig("sq_ready", u), so_far("sq_ready", k, u, pas, j) + 1)
                    nc.vector.reduce_sum(ss[:, l, t, m, :], two_in_P0[:, l, m, :].rearrange("p (h d) -> p h d", h=HEADS),
                                         AX.X).then_inc(sig("sums", u), 1)
                elif u.kind == "rope2":
                    t, m, n = u.part // 2, u.part % 2, u.part % 2
                    for sem, count in newest(pas, j, taken("dense", earlier(pas, u, "qkv2", 3 * t + m), 0)):
                        dve.wait_ge(sem, count)
                    if u.part < 2:
                        dve.wait_ge(sig("sums", u), so_far("sums", k, u, pas, j))
                    else:
                        dve.wait_ge(sig("rot_sum", u), so_far("rot_sum", k, u, pas, j) - 1)
                    raw = (q2, k2)[m][:, l, t, :].rearrange("p (h d) -> p h d", h=HEADS)
                    tab = rope2_sb[:, l, t, m, 1, :]
                    sn = two_in_P0[:, l, n, :].rearrange("p (h d) -> p h d", h=HEADS)
                    nc.vector.tensor_tensor(sn[:, :, 0:32], raw[:, :, 32:64],
                                            tab[:, 0:32].unsqueeze(1).broadcast_to([P, HEADS, 32]), ALU.mult)
                    nc.vector.tensor_tensor(sn[:, :, 32:64], raw[:, :, 0:32],
                                            tab[:, 32:64].unsqueeze(1).broadcast_to([P, HEADS, 32]), ALU.mult)\
                        .then_inc(sig("sin_part", u), 1)
                elif u.kind == "norms2":
                    dve.wait_ge(sig("sums", u), so_far("sums", k, u, pas, j))
                    flat = ss[:, l, u.part].rearrange("p m h -> p (m h)")
                    nc.vector.tensor_scalar(flat, flat, 1e-24, None, ALU.max).then_inc(sig("ss_ready", u), 1)
                elif u.kind == "scale2":
                    t, m, n = u.part // 2, u.part % 2, u.part % 2
                    src = earlier(pas, u, "rope2", u.part)
                    dve.wait_ge(sig("rot_sum", src), so_far("rot_sum", k, src, pas, j) + 1)
                    dve.wait_ge(sig("rn_ready", u), so_far("rn_ready", k, u, pas, j))
                    nc.vector.tensor_tensor((q2, k2)[m][:, l, t, :].rearrange("p (h d) -> p h d", h=HEADS),
                                            cosine2[:, l, n, :].rearrange("p (h d) -> p h d", h=HEADS),
                                            rn[:, l, t, m, :].unsqueeze(2).broadcast_to([P, HEADS, HD]), ALU.mult)\
                        .then_inc(sig("rope_ready", u), 1)
                elif u.kind == "scores2":
                    n, e = u.part // 2, u.part % 2
                    src = tile("score", u)[:, :]
                    if n == 0:
                        dst, src = negmax[:, k, 0, 4 * e:4 * e + 4], src.rearrange("p (h k) -> p h k", h=4)
                    else:
                        h0 = 4 * (n - 1) + 2 * e
                        dst, src = negmax[:, k, 1, h0:h0 + 2], src.rearrange("p (h k) -> p h k", h=2)[:, :, 0:SEQ - WINDOW]
                    dve.wait_ge(has_filled("score", u), uses("score", u, pas, j))
                    nc.vector.reduce_max(dst, src, AX.X, negate=True).then_inc(sig("max_done", u), 1)
                elif u.kind == "norm2":
                    t = u.part
                    for sem, count in newest(pas, j, *(taken("score", earlier(pas, u, "scores2", n)) for n in ((0, 1), (2, 3, 4, 5))[t])):
                        dve.wait_ge(sem, count)
                    nc.vector.reciprocal(recip[:, k, t, 0:HEADS], expsum[:, l, t, :]).then_inc(sig("rec_done", u), 1)
                    dve.wait_ge(sig("rec_done", u), so_far("rec_done", k, u, pas, j) + 1)
                    part = P0[:, l] if t == 0 else P1[:, l, :, WINDOW:SEQ]
                    n = P if t == 0 else SEQ - WINDOW
                    nc.vector.tensor_tensor(part, part, recip[:, k, t, 0:HEADS].unsqueeze(2).broadcast_to([P, HEADS, n]),
                                            ALU.mult).then_inc(sig("p_ready", u), 1)
                elif u.kind == "up2":
                    c, n = u.part, HTILES[u.part][1]
                    dve.wait_ge(sig("gelu_done", u), so_far("gelu_done", k, u, pas, j) + 1)
                    nc.vector.scalar_tensor_tensor(up2T[0:n, l, c, :], tile("dense", u)[0:n, 0:SEQ], b1_2_sb[0:n, l, 0, c:c + 1],
                                                   gates[0:n, l, c, :], ALU.add, ALU.mult).then_inc(has_emptied("dense", u), 1)

            run(dve, "vector", unit)

        @block.tensor
        def _(pe):
            pe.wait_ge(loaded, ALL_LOADED)
            pe.wait_ge(setup_pool, PRESETS)
            pe.wait_ge(setup_act, 2)
            pe.wait_ge(setup_dve, CLEARED)
            pe.wait_ge(staged, 4 * LAYERS)
            mm, turn = nc.tensor.matmul, nc.tensor.transpose

            def unit(u, pas, j):
                k, l = u.stream, u.stream - LOCAL0

                def of(kind, *parts, ring="dense", n=0):
                    return [taken(ring, earlier(pas, u, kind, part), n) for part in parts or (None,)]

                if u.kind in ("turn", "shift"):
                    needs = [free("dense", u)]
                    if u.kind == "turn":
                        src = h[k]
                        if u.source == "att":
                            needs += of("attn_out", *range(TT))
                        else:
                            pe.wait_ge(sig("normed", u), so_far("normed", k, u, pas, j))
                    else:
                        src = Y[l]
                        if k == LOCAL0:
                            pe.wait_ge(raised["normed", ATTN1], so_far("normed", ATTN1, u, pas, j))
                        else:
                            pe.wait_ge(sig("accepted", u), so_far("accepted", k, u, pas, j))
                    for sem, count in newest(pas, j, *needs):
                        pe.wait_ge(sem, count)
                    for t in range(TT):
                        last = turn(tile("dense", u)[:, t * P:(t + 1) * P], src[:, t, :], ident)
                    last.then_inc(has_filled("dense", u), 1)
                elif u.kind == "qkv":
                    t = u.part
                    for sem, count in newest(pas, j, *of("turn"), free("dense", u)):
                        pe.wait_ge(sem, count)
                    mm(tile("dense", u)[:, 0:3 * DIM], hT[k][:, t * P:(t + 1) * P], wqkv_sb[:, k], start=True, stop=True)\
                        .then_inc(has_filled("dense", u), 1)
                elif u.kind in ("turn_q", "turn_k"):
                    src = QB if u.kind == "turn_q" else KB
                    needs = [free("dense", u)]
                    if k == ATTN0:
                        needs += of("qkv", *range(TT))
                    else:
                        pe.wait_ge(sig("lo_ready", u), so_far("lo_ready", k, u, pas, j))
                    if u.source == "with maxima":
                        pe.wait_ge(sig("m_ready", u), so_far("m_ready", k, u, pas, j))
                    for sem, count in newest(pas, j, *needs):
                        pe.wait_ge(sem, count)
                    for e in range(2):
                        g = 2 * u.part + e
                        for t in range(TT):
                            last = turn(tile("dense", u)[:, e * SEQ + t * P:e * SEQ + (t + 1) * P],
                                        src[:, k, t, 4 * g:4 * g + 4, :].rearrange("p h c -> p (h c)"), ident)
                    last.then_inc(has_filled("dense", u), 1)
                elif u.kind == "maxes":
                    needs = [free("score", u)]
                    if u.part == 0:
                        pe.wait_ge(sig("k_in", u), so_far("k_in", k, u, pas, j))
                        needs += of("turn_q", 0, 1)
                    n, e = u.part // 2, u.part % 2
                    for sem, count in newest(pas, j, *needs):
                        pe.wait_ge(sem, count)
                    bank = tile("score", u)[:]
                    if k == ATTN0:
                        t, g = n // 4, n % 4
                        last = mm(bank, qT[:, k, g, t * P:(t + 1) * P], kT[:, k, 4 * g + 2 * e:4 * g + 2 * e + 2, :],
                                  start=True, stop=True)
                    elif n < 2:
                        g = 2 * n + e
                        mm(bank, ident_r[:], causal.unsqueeze(1).broadcast_to([P, 4, P]), start=True, stop=False)
                        last = mm(bank, qT[:, k, g, 0:P], kT[:, k, 4 * g:4 * g + 4, 0:P], start=False, stop=True)
                    else:
                        g = n - 2
                        mm(bank, qT[:, k, g, P:SEQ], kT[:, k, 4 * g + 2 * e:4 * g + 2 * e + 2, :], start=True, stop=False,
                           skip_group_check=True)
                        last = mm(bank.rearrange("p (a k) -> p a k", a=2)[:, :, P:SEQ], ident_r[:],
                                  causal.unsqueeze(1).broadcast_to([P, 2, P]), start=False, stop=True, skip_group_check=True)
                    last.then_inc(has_filled("score", u), 1)
                elif u.kind == "scores":
                    g, t, e = u.part // 4, u.part % 4 // 2, u.part % 2
                    for sem, count in newest(pas, j, *(of("turn_q", 0, 1) if u.part == 0 else []), free("score", u)):
                        pe.wait_ge(sem, count)
                    for i in range(2):
                        last = mm(tile("score", u)[:, i * SEQ:(i + 1) * SEQ], kT[:, k, 4 * g + 2 * e + i, t * P:(t + 1) * P],
                                  qT[:, k, g, :], start=True, stop=True)
                    last.then_inc(has_filled("score", u), 1)
                elif u.kind == "mix":
                    g = u.part
                    if g == 0:
                        pe.wait_ge(sig("v_ready", u), so_far("v_ready", k, u, pas, j))
                    for sem, count in newest(pas, j, free("dense", u)):
                        pe.wait_ge(sem, count)
                    for t in range(TT):
                        if k == ATTN0:
                            for sem, count in newest(pas, j, *of("scores", 4 * g + 2 * t, 4 * g + 2 * t + 1, ring="score")):
                                pe.wait_ge(sem, count)
                        else:
                            pe.wait_ge(sig("masked", u), so_far("masked", k, u, pas, j) + 2 * t - 2)
                        q0 = P if k == ATTN1 and t == 1 else 0
                        w = SEQ - q0
                        for n in range(4):
                            last = mm(tile("dense", u)[32 * n:32 * n + 16, q0:SEQ], V[:, k, t, 4 * g + n, :],
                                      probs[k][t][:, n * w:(n + 1) * w], start=t == 0, stop=t == 1)
                    last.then_inc(has_filled("dense", u), 1)
                elif u.kind == "attn_out":
                    t = u.part
                    for sem, count in newest(pas, j, *of("mix", *range(GROUPS)), free("dense", u)):
                        pe.wait_ge(sem, count)
                    for g in range(GROUPS):
                        last = turn(tile("dense", u)[:, g * P:(g + 1) * P], oT[:, k, g, t * P:(t + 1) * P], ident)
                    last.then_inc(has_filled("dense", u), 1)
                elif u.kind == "project1":
                    for sem, count in newest(pas, j, *of("turn"), free("dense", u)):
                        pe.wait_ge(sem, count)
                    for t in range(TT):
                        last = mm(tile("dense", u)[:, t * P:(t + 1) * P], hT[k][:, t * P:(t + 1) * P], wo1_sb[:], start=True, stop=True)
                    last.then_inc(has_filled("dense", u), 1)
                elif u.kind == "up0":
                    for sem, count in newest(pas, j, *of("turn"), free("dense", u)):
                        pe.wait_ge(sem, count)
                    for e in range(2):
                        c = 2 * u.part + e
                        last = mm(tile("dense", u)[:, e * SEQ:(e + 1) * SEQ], w1_0_sb[:, c * P:(c + 1) * P], hT[k],
                                  start=True, stop=True)
                    last.then_inc(has_filled("dense", u), 1)
                elif u.kind == "down0":
                    for sem, count in newest(pas, j, *of("up0", 0, 1), free("dense", u)):
                        pe.wait_ge(sem, count)
                    for t in range(TT):
                        for c in range(FF0 // P):
                            last = mm(tile("dense", u)[:, t * P:(t + 1) * P], up0T[:, c, t * P:(t + 1) * P], w2_0_sb[:, c, :],
                                      start=c == 0, stop=c == FF0 // P - 1)
                    last.then_inc(has_filled("dense", u), 1)
                elif u.kind == "qkv2":
                    t, m = u.part // 3, u.part % 3
                    for sem, count in newest(pas, j, *of("shift"), free("dense", u)):
                        pe.wait_ge(sem, count)
                    mm(tile("dense", u)[:], hS[:, l, t * P:(t + 1) * P], wqkv2_sb[:, l, m * INNER:(m + 1) * INNER],
                       start=True, stop=True).then_inc(has_filled("dense", u), 1)
                elif u.kind in ("turn_q2", "turn_k2"):
                    src = q2 if u.kind == "turn_q2" else k2
                    pe.wait_ge(sig("rope_ready", u), so_far("rope_ready", k, u, pas, j))
                    for sem, count in newest(pas, j, free("dense", u)):
                        pe.wait_ge(sem, count)
                    for e in range(2):
                        pr = 2 * u.part + e
                        for t in range(TT):
                            last = turn(tile("dense", u)[:, e * SEQ + t * P:e * SEQ + (t + 1) * P],
                                        src[:, l, t, pr * P:(pr + 1) * P], ident)
                    last.then_inc(has_filled("dense", u), 1)
                elif u.kind == "scores2":
                    needs = [free("score", u)]
                    if u.part == 0:
                        pe.wait_ge(sig("k_in", u), so_far("k_in", k, u, pas, j))
                        needs += of("turn_q2", 0, 1)
                    n, e = u.part // 2, u.part % 2
                    for sem, count in newest(pas, j, *needs):
                        pe.wait_ge(sem, count)
                    bank = tile("score", u)[:]
                    if n == 0:
                        mm(bank, ident_r[:], band0.unsqueeze(1).broadcast_to([P, 4, P]), start=True, stop=False)
                        for pr in (2 * e, 2 * e + 1):
                            last = mm(bank[:, (pr - 2 * e) * SEQ:(pr - 2 * e + 1) * SEQ], qT2[:, l, pr, 0:P],
                                      kT2[:, l, pr, :, 0:P], start=False, stop=pr == 2 * e + 1)
                    else:
                        pr = 2 * (n - 1) + e
                        two = bank.rearrange("p (a k) -> p a k", a=2)[:, :, 0:SEQ - WINDOW]
                        mm(two, ident_r[:], band1.unsqueeze(1).broadcast_to([P, 2, SEQ - WINDOW]), start=True, stop=False)
                        last = mm(two, qT2[:, l, pr, P:SEQ], kT2[:, l, pr, :, WINDOW:SEQ], start=False, stop=True)
                    last.then_inc(has_filled("score", u), 1)
                elif u.kind == "turn_p":
                    if u.part == 0:
                        pe.wait_ge(sig("p_ready", u), so_far("p_ready", k, u, pas, j))
                    hd, bank = u.part, tile("score", u)
                    for sem, count in newest(pas, j, free("score", u)):
                        pe.wait_ge(sem, count)
                    turn(bank[:, 0:P], P0[:, l, hd, :], ident)
                    turn(bank[:, P:P + WINDOW], P1[0:WINDOW, l, hd, 0:P], ident[0:WINDOW, 0:WINDOW])
                    turn(bank[:, P + WINDOW:2 * P + WINDOW], P1[:, l, hd, P:SEQ], ident).then_inc(has_filled("score", u), 1)
                elif u.kind == "mix2":
                    n = u.part
                    for sem, count in newest(pas, j, *(of("qkv2", 2, 5) if n == 0 else []), *of("turn_p", 2 * n, 2 * n + 1, ring="score"), free("dense", u)):
                        pe.wait_ge(sem, count)
                    for q0, w, t, c0 in ((0, P + WINDOW, 0, 0), (P, P, 1, P + WINDOW)):
                        for e in range(2):
                            hd = 2 * n + e
                            last = mm(tile("dense", u)[64 * e:64 * e + 64, q0:q0 + w], V2[:, l, t, hd * HD:(hd + 1) * HD],
                                      probs2[l][n % 2][:, e, c0:c0 + w], start=t == 0, stop=t == 1, skip_group_check=True)
                    last.then_inc(has_filled("dense", u), 1)
                elif u.kind == "project2":
                    for sem, count in newest(pas, j, *of("mix2", *range(PAIRS)), free("dense", u)):
                        pe.wait_ge(sem, count)
                    for t in range(TT):
                        for c in range(PAIRS):
                            last = mm(tile("dense", u)[:, t * P:(t + 1) * P], o2T[:, l, c, t * P:(t + 1) * P], wo2_sb[:, l, c, :],
                                      start=c == 0, stop=c == PAIRS - 1)
                    last.then_inc(has_filled("dense", u), 1)
                elif u.kind == "up2":
                    c, (at, n) = u.part, HTILES[u.part]
                    for sem, count in newest(pas, j, *of("turn"), free("dense", u)):
                        pe.wait_ge(sem, count)
                    for half in range(2):
                        last = mm(tile("dense", u)[0:n, half * SEQ:(half + 1) * SEQ],
                                  w1_2_sb[:, l, half * HID + at:half * HID + at + n], hT[k], start=True, stop=True)
                    last.then_inc(has_filled("dense", u), 1)
                elif u.kind == "down2":
                    for sem, count in newest(pas, j, *of("up2", 0, 1, 2), free("dense", u)):
                        pe.wait_ge(sem, count)
                    for t in range(TT):
                        for c, (at, n) in enumerate(HTILES):
                            last = mm(tile("dense", u)[:, t * P:(t + 1) * P], up2T[0:n, l, c, t * P:(t + 1) * P], w2_2_sb[0:n, l, c, :],
                                      start=c == 0, stop=c == 2)
                    last.then_inc(has_filled("dense", u), 1)

            run(pe, "tensor", unit)


def tiles_on_columns(b):
    out = np.zeros((P, LAYERS, 2, len(HTILES)), b.dtype)
    for c, (at, n) in enumerate(HTILES):
        out[0:n, :, :, c] = b.reshape(LAYERS, 2, HID)[:, :, at:at + n].transpose(2, 0, 1)
    return out


def kernel(**inputs):
    import concourse.bacc as bacc
    from concourse.bass_utils import run_bass_kernel_spmd

    a = {k: np.asarray(v) for k, v in inputs.items()}
    arrays = {
        "x": a["L0_attn_x"],
        "wqkv0": np.concatenate([a["L0_attn_Wq"].T, a["L0_attn_Wk"].T, a["L0_attn_Wv"].T], axis=1),
        "w1_0": a["L0_ffn_w1"], "b1_0": a["L0_ffn_b1"].reshape(FF0 // P, P).T, "w2_0": a["L0_ffn_w2"], "b2_0": a["L0_ffn_b2"],
        "wqkv1": np.concatenate([a["L1_attn_wq"].T, a["L1_attn_wk"].T, a["L1_attn_wv"].T], axis=1),
        "wo1": a["L1_attn_wo"].T,
        "wqkv2": a["L1_ffn_wqkv"], "q_scale": a["L1_ffn_q_scale"], "k_scale": a["L1_ffn_k_scale"], "wo2": a["L1_ffn_wo"],
        "ln_g": a["L1_ffn_ln_g"].T, "ln_b": a["L1_ffn_ln_b"].T, "w1_2": a["L1_ffn_w1"], "b1_2": tiles_on_columns(a["L1_ffn_b1"]),
        "w2_2": a["L1_ffn_w2"], "b2_2": a["L1_ffn_b2"],
    }
    arrays.update(shape_constants())
    arrays = {k: np.ascontiguousarray(v) for k, v in arrays.items()}
    nc = bacc.Bacc("TRN2", target_bir_lowering=False, num_devices=1)
    args = [nc.dram_tensor(k, v.shape, mybir.dt.from_np(v.dtype), kind="ExternalInput").ap() for k, v in arrays.items()]
    args.append(nc.dram_tensor("out", (BATCH, SEQ, DIM), mybir.dt.float32, kind="ExternalOutput").ap())
    fused_block(nc, *args)
    r = run_bass_kernel_spmd(nc, [arrays], core_ids=[0])
    return r.results[0]["out"]
```
